# Optimizing a Trainium2 kernel written in Bass

```python
import numpy as np
import jax
import jax.numpy as jnp

def _softmax(x, axis=-1):
    return jax.nn.softmax(x, axis=axis)

def _gelu(x):
    return jax.nn.gelu(x, approximate=True)

def _silu(x):
    return jax.nn.silu(x)

def _sigmoid(x):
    return jax.nn.sigmoid(x)

def _layernorm(x, axis=-1, eps=1e-05):
    m = jnp.mean(x, axis=axis, keepdims=True)
    v = jnp.var(x, axis=axis, keepdims=True)
    return (x - m) / jnp.sqrt(v + eps)

def _scatter_add(tgt, idx, src, axis=0):
    return tgt.at[idx].add(src)

def _segment_sum(src, seg, n):
    return jax.ops.segment_sum(src, seg, n)
kernel_name = 'mk_xattn_seq_d2_seqx_r8_557a71'

def setup_inputs(seed: int=0):
    np.random.seed(seed)
    _w = jnp.asarray

    def _rec_inputs():
        import jax
        import jax.numpy as jnp
        _rk = jax.random.key(seed)
        x = -0.000719 + 1.001 * jax.random.normal(jax.random.fold_in(_rk, 1), (2, 512, 160), jnp.float32)
        _lenS = 512 - jax.random.randint(jax.random.fold_in(_rk, 7), (2,), 0, max(1, 512 // 4) + 1, jnp.int32)
        _lenS2 = 154 - jax.random.randint(jax.random.fold_in(_rk, 8), (2,), 0, max(1, 154 // 4) + 1, jnp.int32)
        _ctx_2048P = jax.random.normal(jax.random.fold_in(_rk, 11), (2, 16, 256), jnp.float32)
        _ctx_2048c = jax.random.dirichlet(jax.random.fold_in(_rk, 511), 0.3 * jnp.ones((16,), jnp.float32), (2, 154))
        _ctx_2048t = jnp.einsum('bsk,bkd->bsd', _ctx_2048c, _ctx_2048P)
        _ctx_2048t = _ctx_2048t * jax.lax.rsqrt(jnp.mean(jnp.square(_ctx_2048t)) + 1e-12) * 0.953939
        ctx_2048 = 0.00257118 + 0.99863 * (_ctx_2048t + 0.3 * jax.random.normal(jax.random.fold_in(_rk, 611), (2, 154, 256), jnp.float32))
        fside_S_0 = jax.random.uniform(jax.random.fold_in(_rk, 12), (512,), jnp.float32, 0.0, 0.999706)
        return (x, ctx_2048, fside_S_0)
    x, ctx_2048, fside_S_0 = _rec_inputs()

    def _L0_xattn_setup():
        import jax, jax.numpy as jnp
        import numpy as np
        HEADS = 20
        NUM_TOKENS = 4
        IP_SCALE = 1.0
        SEM_SCALE = 0.5
        RESCALE = 1.0
        EPS = 1e-12

        def _l2norm(x, axis=-1):
            n = jnp.sqrt(jnp.sum(x * x, axis=axis, keepdims=True))
            return x / jnp.maximum(n, EPS)
        key = jax.random.key(seed)
        ks = jax.random.split(key, 10)
        B, S, C = (2, 128, 160)
        T, E = (81, 256)
        inp = {'hidden_states': jax.random.normal(ks[0], (B, S, C), jnp.float32), 'encoder_hidden_states': jax.random.normal(ks[1], (B, T, E), jnp.float32), 'spatial_mask': jax.random.uniform(ks[2], (S,), jnp.float32), 'W_q': jax.random.normal(ks[3], (C, C), jnp.float32) * C ** (-0.5), 'W_k': jax.random.normal(ks[4], (E, C), jnp.float32) * E ** (-0.5), 'W_v': jax.random.normal(ks[5], (E, C), jnp.float32) * E ** (-0.5), 'W_k_ip': jax.random.normal(ks[6], (E, C), jnp.float32) * E ** (-0.5), 'W_v_ip': jax.random.normal(ks[7], (E, C), jnp.float32) * E ** (-0.5), 'W_out': jax.random.normal(ks[8], (C, C), jnp.float32) * C ** (-0.5), 'b_out': jnp.zeros((C,), jnp.float32)}
        return inp
    _L0_xattn_all = _L0_xattn_setup()
    _L0_xattn_in = {k: v for k, v in _L0_xattn_all.items() if k in ('W_q', 'W_k', 'W_v', 'W_k_ip', 'W_v_ip', 'W_out', 'b_out')}
    del _L0_xattn_all

    def _L1_xattn_setup():
        import jax, jax.numpy as jnp
        import numpy as np
        DIM = 160
        HEADS = 20
        DHEAD = 64
        CTX_DIM = 256
        INNER = HEADS * DHEAD
        FF_INNER = 4 * DIM
        SCALE = DHEAD ** (-0.5)
        EPS = 1e-05

        def _layer_norm(x, g, b):
            m = jnp.mean(x, axis=-1, keepdims=True)
            v = jnp.mean(jnp.square(x - m), axis=-1, keepdims=True)
            return (x - m) * jax.lax.rsqrt(v + EPS) * g + b

        def _attention(x, ctx, wq, wk, wv, wo, bo):
            B, N, _ = x.shape
            M = ctx.shape[1]
            q = (x @ wq).reshape(B, N, HEADS, DHEAD).transpose(0, 2, 1, 3)
            k = (ctx @ wk).reshape(B, M, HEADS, DHEAD).transpose(0, 2, 1, 3)
            v = (ctx @ wv).reshape(B, M, HEADS, DHEAD).transpose(0, 2, 1, 3)
            sim = jnp.einsum('bhid,bhjd->bhij', q, k) * SCALE
            attn = jax.nn.softmax(sim, axis=-1)
            out = jnp.einsum('bhij,bhjd->bhid', attn, v)
            out = out.transpose(0, 2, 1, 3).reshape(B, N, INNER)
            return out @ wo + bo

        def _geglu_ff(x, w1, b1, w2, b2):
            h = x @ w1 + b1
            a, gate = jnp.split(h, 2, axis=-1)
            return a * jax.nn.gelu(gate, approximate=False) @ w2 + b2
        key = jax.random.key(seed)
        ks = jax.random.split(key, 16)
        s = 0.02
        d = {'x': jax.random.normal(ks[0], (2, 256, DIM), jnp.float32), 'context': jax.random.normal(ks[1], (2, 77, CTX_DIM), jnp.float32), 'a1_wq': jax.random.normal(ks[2], (DIM, INNER), jnp.float32) * s, 'a1_wk': jax.random.normal(ks[3], (DIM, INNER), jnp.float32) * s, 'a1_wv': jax.random.normal(ks[4], (DIM, INNER), jnp.float32) * s, 'a1_wo': jax.random.normal(ks[5], (INNER, DIM), jnp.float32) * s, 'a1_bo': jnp.zeros((DIM,), jnp.float32), 'a2_wq': jax.random.normal(ks[6], (DIM, INNER), jnp.float32) * s, 'a2_wk': jax.random.normal(ks[7], (CTX_DIM, INNER), jnp.float32) * s, 'a2_wv': jax.random.normal(ks[8], (CTX_DIM, INNER), jnp.float32) * s, 'a2_wo': jax.random.normal(ks[9], (INNER, DIM), jnp.float32) * s, 'a2_bo': jnp.zeros((DIM,), jnp.float32), 'ff_w1': jax.random.normal(ks[10], (DIM, 2 * FF_INNER), jnp.float32) * s, 'ff_b1': jnp.zeros((2 * FF_INNER,), jnp.float32), 'ff_w2': jax.random.normal(ks[11], (FF_INNER, DIM), jnp.float32) * s, 'ff_b2': jnp.zeros((DIM,), jnp.float32), 'ln1_g': jnp.ones((DIM,), jnp.float32), 'ln1_b': jnp.zeros((DIM,), jnp.float32), 'ln2_g': jnp.ones((DIM,), jnp.float32), 'ln2_b': jnp.zeros((DIM,), jnp.float32), 'ln3_g': jnp.ones((DIM,), jnp.float32), 'ln3_b': jnp.zeros((DIM,), jnp.float32)}
        return d
    _L1_xattn_all = _L1_xattn_setup()
    _L1_xattn_in = {k: v for k, v in _L1_xattn_all.items() if k in ('a1_wq', 'a1_wk', 'a1_wv', 'a1_wo', 'a1_bo', 'a2_wq', 'a2_wk', 'a2_wv', 'a2_wo', 'a2_bo', 'ff_w1', 'ff_b1', 'ff_w2', 'ff_b2', 'ln1_g', 'ln1_b', 'ln2_g', 'ln2_b', 'ln3_g', 'ln3_b')}
    del _L1_xattn_all
    return {'x': x, 'ctx_2048': ctx_2048, 'fside_S_0': fside_S_0, 'L0_xattn_W_q': _L0_xattn_in['W_q'], 'L0_xattn_W_k': _L0_xattn_in['W_k'], 'L0_xattn_W_v': _L0_xattn_in['W_v'], 'L0_xattn_W_k_ip': _L0_xattn_in['W_k_ip'], 'L0_xattn_W_v_ip': _L0_xattn_in['W_v_ip'], 'L0_xattn_W_out': _L0_xattn_in['W_out'], 'L0_xattn_b_out': _L0_xattn_in['b_out'], 'L1_xattn_a1_wq': _L1_xattn_in['a1_wq'], 'L1_xattn_a1_wk': _L1_xattn_in['a1_wk'], 'L1_xattn_a1_wv': _L1_xattn_in['a1_wv'], 'L1_xattn_a1_wo': _L1_xattn_in['a1_wo'], 'L1_xattn_a1_bo': _L1_xattn_in['a1_bo'], 'L1_xattn_a2_wq': _L1_xattn_in['a2_wq'], 'L1_xattn_a2_wk': _L1_xattn_in['a2_wk'], 'L1_xattn_a2_wv': _L1_xattn_in['a2_wv'], 'L1_xattn_a2_wo': _L1_xattn_in['a2_wo'], 'L1_xattn_a2_bo': _L1_xattn_in['a2_bo'], 'L1_xattn_ff_w1': _L1_xattn_in['ff_w1'], 'L1_xattn_ff_b1': _L1_xattn_in['ff_b1'], 'L1_xattn_ff_w2': _L1_xattn_in['ff_w2'], 'L1_xattn_ff_b2': _L1_xattn_in['ff_b2'], 'L1_xattn_ln1_g': _L1_xattn_in['ln1_g'], 'L1_xattn_ln1_b': _L1_xattn_in['ln1_b'], 'L1_xattn_ln2_g': _L1_xattn_in['ln2_g'], 'L1_xattn_ln2_b': _L1_xattn_in['ln2_b'], 'L1_xattn_ln3_g': _L1_xattn_in['ln3_g'], 'L1_xattn_ln3_b': _L1_xattn_in['ln3_b']}

def reference(x, ctx_2048, fside_S_0, L0_xattn_W_q, L0_xattn_W_k, L0_xattn_W_v, L0_xattn_W_k_ip, L0_xattn_W_v_ip, L0_xattn_W_out, L0_xattn_b_out, L1_xattn_a1_wq, L1_xattn_a1_wk, L1_xattn_a1_wv, L1_xattn_a1_wo, L1_xattn_a1_bo, L1_xattn_a2_wq, L1_xattn_a2_wk, L1_xattn_a2_wv, L1_xattn_a2_wo, L1_xattn_a2_bo, L1_xattn_ff_w1, L1_xattn_ff_b1, L1_xattn_ff_w2, L1_xattn_ff_b2, L1_xattn_ln1_g, L1_xattn_ln1_b, L1_xattn_ln2_g, L1_xattn_ln2_b, L1_xattn_ln3_g, L1_xattn_ln3_b):
    import jax
    import jax.numpy as jnp

    def _L0_xattn_ref(hidden_states, encoder_hidden_states, spatial_mask, W_q, W_k, W_v, W_k_ip, W_v_ip, W_out, b_out):
        import jax, jax.numpy as jnp
        import numpy as np
        HEADS = 20
        NUM_TOKENS = 4
        IP_SCALE = 1.0
        SEM_SCALE = 0.5
        RESCALE = 1.0
        EPS = 1e-12

        def _l2norm(x, axis=-1):
            n = jnp.sqrt(jnp.sum(x * x, axis=axis, keepdims=True))
            return x / jnp.maximum(n, EPS)
        B, S, C = hidden_states.shape
        H = HEADS
        Dh = C // H
        attn_scale = Dh ** (-0.5)
        residual = hidden_states
        text_ehs = encoder_hidden_states[:, :-NUM_TOKENS]
        ip_ehs = encoder_hidden_states[:, -NUM_TOKENS:]

        def heads(x):
            return x.reshape(B, -1, H, Dh).transpose(0, 2, 1, 3)
        q = heads(hidden_states @ W_q)
        k_t = heads(text_ehs @ W_k)
        v_t = heads(text_ehs @ W_v)
        scores_t = jnp.einsum('bhsd,bhtd->bhst', q, k_t) * attn_scale
        probs_t = jax.nn.softmax(scores_t, axis=-1)
        text_out = jnp.einsum('bhst,bhtd->bhsd', probs_t, v_t)
        text_out = text_out.transpose(0, 2, 1, 3).reshape(B, S, C)
        k_ip = heads(ip_ehs @ W_k_ip)
        v_ip = heads(ip_ehs @ W_v_ip)
        attn_scores = jnp.einsum('bhsd,bhnd->bhsn', q, k_ip) * attn_scale
        qsem = jnp.einsum('bhst,bte->bhse', probs_t, text_ehs)
        qsem = _l2norm(qsem)
        ip_n = _l2norm(ip_ehs)
        sem = jnp.einsum('bhse,bne->bhsn', qsem, ip_n)
        sem = jax.lax.stop_gradient(sem)
        fused = attn_scores + SEM_SCALE * sem
        probs_ip = jax.nn.softmax(fused, axis=-1)
        probs_ip = probs_ip * spatial_mask[None, None, :, None]
        ip_out = jnp.einsum('bhsn,bhnd->bhsd', probs_ip, v_ip)
        ip_out = ip_out.transpose(0, 2, 1, 3).reshape(B, S, C)
        out = text_out + IP_SCALE * ip_out
        out = out @ W_out + b_out
        out = out + residual
        return out / RESCALE

    def _L1_xattn_ref(x, context, a1_wq, a1_wk, a1_wv, a1_wo, a1_bo, a2_wq, a2_wk, a2_wv, a2_wo, a2_bo, ff_w1, ff_b1, ff_w2, ff_b2, ln1_g, ln1_b, ln2_g, ln2_b, ln3_g, ln3_b):
        import jax, jax.numpy as jnp
        import numpy as np
        DIM = 160
        HEADS = 20
        DHEAD = 64
        CTX_DIM = 256
        INNER = HEADS * DHEAD
        FF_INNER = 4 * DIM
        SCALE = DHEAD ** (-0.5)
        EPS = 1e-05

        def _layer_norm(x, g, b):
            m = jnp.mean(x, axis=-1, keepdims=True)
            v = jnp.mean(jnp.square(x - m), axis=-1, keepdims=True)
            return (x - m) * jax.lax.rsqrt(v + EPS) * g + b

        def _attention(x, ctx, wq, wk, wv, wo, bo):
            B, N, _ = x.shape
            M = ctx.shape[1]
            q = (x @ wq).reshape(B, N, HEADS, DHEAD).transpose(0, 2, 1, 3)
            k = (ctx @ wk).reshape(B, M, HEADS, DHEAD).transpose(0, 2, 1, 3)
            v = (ctx @ wv).reshape(B, M, HEADS, DHEAD).transpose(0, 2, 1, 3)
            sim = jnp.einsum('bhid,bhjd->bhij', q, k) * SCALE
            attn = jax.nn.softmax(sim, axis=-1)
            out = jnp.einsum('bhij,bhjd->bhid', attn, v)
            out = out.transpose(0, 2, 1, 3).reshape(B, N, INNER)
            return out @ wo + bo

        def _geglu_ff(x, w1, b1, w2, b2):
            h = x @ w1 + b1
            a, gate = jnp.split(h, 2, axis=-1)
            return a * jax.nn.gelu(gate, approximate=False) @ w2 + b2
        n = _layer_norm(x, ln1_g, ln1_b)
        x = x + _attention(n, n, a1_wq, a1_wk, a1_wv, a1_wo, a1_bo)
        n = _layer_norm(x, ln2_g, ln2_b)
        x = x + _attention(n, context, a2_wq, a2_wk, a2_wv, a2_wo, a2_bo)
        x = _geglu_ff(_layer_norm(x, ln3_g, ln3_b), ff_w1, ff_b1, ff_w2, ff_b2) + x
        return x
    x = _L0_xattn_ref(x, ctx_2048, fside_S_0, L0_xattn_W_q, L0_xattn_W_k, L0_xattn_W_v, L0_xattn_W_k_ip, L0_xattn_W_v_ip, L0_xattn_W_out, L0_xattn_b_out)
    x = _L1_xattn_ref(x, ctx_2048, L1_xattn_a1_wq, L1_xattn_a1_wk, L1_xattn_a1_wv, L1_xattn_a1_wo, L1_xattn_a1_bo, L1_xattn_a2_wq, L1_xattn_a2_wk, L1_xattn_a2_wv, L1_xattn_a2_wo, L1_xattn_a2_bo, L1_xattn_ff_w1, L1_xattn_ff_b1, L1_xattn_ff_w2, L1_xattn_ff_b2, L1_xattn_ln1_g, L1_xattn_ln1_b, L1_xattn_ln2_g, L1_xattn_ln2_b, L1_xattn_ln3_g, L1_xattn_ln3_b)
    return x

_drawn_inputs = setup_inputs


def setup_inputs(seed=0):
    import zlib

    import numpy as np

    out = dict(_drawn_inputs(seed))
    spreads = {'L0_xattn_b_out': (0.0, 0.1),
     'L1_xattn_a1_bo': (0.0, 0.1),
     'L1_xattn_a2_bo': (0.0, 0.1),
     'L1_xattn_ff_b1': (0.0, 0.8),
     'L1_xattn_ff_b2': (0.0, 0.1),
     'L1_xattn_ln1_g': (1.0, 0.6),
     'L1_xattn_ln1_b': (0.0, 0.52),
     'L1_xattn_ln2_g': (1.0, 0.6),
     'L1_xattn_ln2_b': (0.0, 0.8),
     'L1_xattn_ln3_g': (1.0, 0.6),
     'L1_xattn_ln3_b': (0.0, 0.8)}
    factors = {'L1_xattn_a1_wq': 8.0,
     'L1_xattn_a1_wk': 8.0,
     'L1_xattn_a2_wq': 8.0,
     'L1_xattn_a2_wk': 8.0,
     'L1_xattn_ff_w1': 3.598,
     'L1_xattn_ff_w2': 3.531}
    for name, (base, spread) in spreads.items():
        noise = np.random.default_rng([zlib.crc32(name.encode()), seed]).standard_normal(out[name].shape)
        drawn = base * np.exp(spread * noise) if base else spread * noise
        out[name] = jnp.asarray(drawn.astype(out[name].dtype))
    for name, factor in factors.items():
        out[name] = (out[name] * factor).astype(out[name].dtype)
    return out
```

```python
import concourse.bass as bass
from concourse import mybir
from contextlib import ExitStack

B, S, C = 2, 512, 160
T, E = 154, 256
NIP = 4
TT = T - NIP
HEADS = 20
P = 128
QT = S // P
NT = B * QT
N = B * S
CT = C - P
KC = S // P
EC = E // P
D0 = C // HEADS
D1 = 64
PAIRS = HEADS // 2
G4 = HEADS // 4
FF = 4 * C
FCH = FF // P
TXTAIL = TT - P
TTAIL = T - P
PW = 160
RHS = TT + D0 + NIP
RHT = TXTAIL + D0 + NIP
ST = 2 + D0 + NIP + NIP
STEPS0 = B * G4
EPS_NORM = 1e-12
EPS_LN = 1e-5
TINY = 1e-30
SEM_SCALE = 0.5


def cross_attention_block_kernel(nc, A, out):
    F32, F32R = mybir.dt.float32, mybir.dt.float32r
    ALU = mybir.AluOpType
    ACT = mybir.ActivationFunctionType
    AX = mybir.AxisListType
    x, ctx_in = A["x"], A["ctx_2048"]

    with ExitStack() as stack:
        def sb(name, shape, dt=F32):
            return stack.enter_context(nc.sbuf_tensor(name, shape, dt))

        def sem(name):
            return stack.enter_context(nc.semaphore(name))

        bank01 = stack.enter_context(nc.psum_tensor("bank01", [P, 2, 512], F32))
        bank23 = stack.enter_context(nc.psum_tensor("bank23", [P, 2, 512], F32))
        bank45 = stack.enter_context(nc.psum_tensor("bank45", [P, 2, 512], F32))
        bank67 = stack.enter_context(nc.psum_tensor("bank67", [P, 2, 512], F32))
        bank = [t[:, k, :] for t in (bank01, bank23, bank45, bank67) for k in range(2)]

        ident = sb("ident", [P, P])
        X = sb("X", [P, NT, C])
        XN = sb("XN", [P, NT, C])
        nTm, nTt = sb("nTm", [P, N]), sb("nTt", [CT, N])
        var, root = sb("var", [P, NT]), sb("root", [P, NT])
        bn6, mv, rstd = sb("bn6", [P, NT, 6]), sb("mv", [P, NT, 2]), sb("rstd", [P, NT])
        gcol = sb("gcol", [P, 12])
        brow = sb("brow", [P, 4, C])
        b1col = sb("b1col", [P, 2 * FCH])
        smask = sb("smask", [P, QT])
        cm, ct = sb("cm", [P, B, E]), sb("ct", [TTAIL, B, E])
        cT = sb("cT", [P, EC, B, T])
        cT4 = sb("cT4", [P, EC, B, 4, 32])
        first = ExitStack()

        def sb0(name, shape, dt=F32):
            return first.enter_context(nc.sbuf_tensor(name, shape, dt))

        wq0, wq0t = sb0("wq0", [P, C]), sb0("wq0t", [CT, C])
        wkv0 = sb0("wkv0", [P, 4, EC, C])
        wo0, wo0t = sb0("wo0", [P, C]), sb0("wo0t", [CT, C])
        wqe, wqet = sb0("wqe", [P, HEADS, 32]), sb0("wqet", [CT, HEADS, 32])
        wke = sb0("wke", [P, 2, EC, HEADS, 32])
        ipn, ips, ipj = sb0("ipn", [B * NIP, E]), sb0("ips", [B * NIP, 4]), sb0("ipj", [B * NIP, E])
        ipR = sb0("ipR", [P, EC, B, HEADS, NIP])
        ipT = sb0("ipT", [P, EC, B * NIP])
        low_q, low_k = sb0("low_q", [P, 1]), sb0("low_k", [P, 1])
        sign_q, sign_k = sb0("sign_q", [P, 1]), sb0("sign_k", [P, 1])
        QT0 = sb0("QT0", [P, G4, N], F32R)
        KB0 = sb0("KB0", [P, G4, B, 4, T], F32R)
        hi0, tm0 = sb0("hi0", [P, 2, 512], F32R), sb0("tm0", [P, 2, 512])
        GV, GVt = sb0("GV", [P, B, HEADS, RHS]), sb0("GVt", [P, B, G4, 4, RHT])
        VB0 = sb0("VB0", [4 * HEADS, B, C])
        bmask = sb0("bmask", [4 * HEADS, C])
        qs0 = sb0("qs0", [P, B, G4, P], F32R)
        nmax0 = sb0("nmax0", [P, 3, 4])
        P0 = sb0("P0", [P, 3, 4, PW])
        P0t = sb0("P0t", [P, 2, 4, 32])
        PT0, PT0t = sb0("PT0", [P, 2, 4, P]), sb0("PT0t", [P, 2, P])
        den0 = sb0("den0", [P, B, HEADS])
        scl = sb0("scl", [P, 512])
        st0 = sb0("st0", [P, B, HEADS, ST])
        sta = sb0("sta", [P, NT, HEADS, ST])
        h1, h2, h3 = sb0("h1", [P, NT, HEADS]), sb0("h2", [P, NT, HEADS]), sb0("h3", [P, NT, HEADS])
        f1 = sb0("f1", [P, NT, HEADS, NIP])
        f2 = sb0("f2", [P, NT, HEADS, NIP])
        FT = sb0("FT", [4 * HEADS, N])
        TX = sb0("TX", [P, NT, HEADS, D0])
        OTm, OTt = sb0("OTm", [P, N]), sb0("OTt", [CT, N])
        first.close()

        raw = {n: sb("raw_" + n, [P, P]) for n in ("q", "k", "v")}
        rawt = {n: sb("rawt_" + n, [P, P]) for n in ("q", "k", "v")}
        raw["o"] = sb("raw_o", [P, C])
        w = {n: sb("w_" + n, [P, P]) for n in ("q", "k", "v")}
        wt = {n: sb("wt_" + n, [P, P]) for n in ("q", "k", "v")}
        w["o"] = sb("w_o", [P, C])
        qT = sb("qT", [P, B, S])
        kZ = sb("kZ", [P, B, 2, S])
        vZ = sb("vZ", [P, B, 2, KC, P])
        pr = sb("pr", [P, 2, QT, S])
        pT = sb("pT", [P, 4, S])
        nmax = sb("nmax", [P, 2, QT])
        den = sb("den", [P, B, QT, 2])
        rden = sb("rden", [P, B, QT, 2])
        rbs = sb("rbs", [P, S])
        oT = sb("oT", [P, B, S])
        kZ2 = sb("kZ2", [P, B, 2, T])
        vZ2 = sb("vZ2", [P, B, 2, P])
        vZ2t = sb("vZ2t", [P, B, 2, P])
        P2 = sb("P2", [P, 3, 4, PW])
        P2t = sb("P2t", [P, 2, 4, 32])
        rsp = sb("rsp", [P, QT, 2, D1])
        P2T, P2Tt = sb("P2T", [P, 2, 4, P]), sb("P2Tt", [P, 2, P])
        nmax2 = sb("nmax2", [P, 3, 4])
        raw1, raw1t, raw2 = sb("raw1", [P, 2, P]), sb("raw1t", [CT, 2, P]), sb("raw2", [P, C])
        w1, w1t, w2 = sb("w1", [P, 2, P]), sb("w1t", [CT, 2, P]), sb("w2", [P, C])
        gel = sb("gel", [P, N])
        hid = sb("hid", [P, N])
        b1s = sb("b1s", [P, 2])
        block = stack.enter_context(nc.Block())

        loaded_x, loaded_ctx = sem("loaded_x"), sem("loaded_ctx")
        loaded_w0, loaded_small = sem("loaded_w0"), sem("loaded_small")
        masks_ready = sem("masks_ready")
        spread_ready = sem("spread_ready")
        ip_ready = sem("ip_ready")
        stored = sem("stored")
        ps_ready = sem("ps_ready")
        by_act, by_dve = sem("by_act"), sem("by_dve")
        hi_ready = sem("hi_ready")
        dve_step = sem("dve_step")
        pool_step = sem("pool_step")
        pool_held = sem("pool_held")
        s_ipn = sem("s_ipn")
        square_ready, root_ready = sem("square_ready"), sem("root_ready")

        USES = [("cT0", "act"), ("cT1", "act"), ("ipT", "dve"),
                ("x_m0", "act"), ("x_m1", "act"), ("x_t0", "dve"), ("x_t1", "dve")]
        USES += [(f"K0_{g}", "dve") for g in range(G4)]
        USES += [(f"Q0_{g}_{h}", "dve") for g in range(G4) for h in range(B)]
        USES += [("GV_0", "act"), ("GV_1", "act"), ("GVt_0", "dve"), ("GVt_1", "dve"),
                 ("VB_0", "dve"), ("VB_1", "dve")]
        USES += [("F_0", "act"), ("F_1", "act"), ("O_m0", "act"), ("O_m1", "act"), ("O_t0", "act"),
                 ("O_t1", "act")] + [(f"out_{k}", "dve") for k in range(4)]
        for k in (1, 2, 3):
            USES += [(f"n{k}_{p}", "act") for p in ("m0", "m1", "t0", "t1")]
        index = {name: k for k, (name, _) in enumerate(USES)}
        count = {name: sum(e == eng for _, e in USES[:k + 1]) for k, (name, eng) in enumerate(USES)}

        def make(pe, name):
            k = index[name]
            if k >= 8:
                taken(pe, USES[k - 8][0])
            return bank[k % 8]

        def taken(eng, name):
            eng.wait_ge(by_act if USES[index[name]][1] == "act" else by_dve, count[name])

        def made(eng, name):
            eng.wait_ge(ps_ready, index[name] + 1)
            return bank[index[name] % 8]

        q0_ready, s0_ready, m0_ready = sem("q0_ready"), sem("s0_ready"), sem("m0_ready")
        p0_ready, t0_ready, pt0_ready = sem("p0_ready"), sem("t0_ready"), sem("pt0_ready")
        u0_ready, u0_taken, st0_saved = sem("u0_ready"), sem("u0_taken"), sem("st0_saved")
        p0t_ready = sem("p0t_ready")
        f_ready, fe_ready, fn_ready = sem("f_ready"), sem("fe_ready"), sem("fn_ready")
        xn_ready, bias_added = sem("xn_ready"), sem("bias_added")
        names = ("raw", "rawo", "w", "wo", "s", "m", "p", "t", "ptd", "pta", "pv", "rden", "o", "pt", "rsp", "misc0",
                 "misc1", "taken0", "taken1")
        at = [{n: sem(f"{n}_{kind}") for n in names} for kind in ("self", "cross")]
        zeroed = sem("zeroed")
        ff_raw, ff_w, ff_g, ff_a, ff_gel, ff_hid = (sem(f"ff_{n}") for n in ("raw", "w", "g", "a", "gel", "hid"))
        ff_out, ff_added = sem("ff_out"), sem("ff_added")
        x_final = sem("x_final")

        from_one = [q0_ready, s0_ready, m0_ready, p0_ready, t0_ready, pt0_ready, u0_ready, u0_taken, st0_saved,
                    p0t_ready, ff_raw, ff_w, ff_g, ff_a, ff_gel, ff_hid, ff_out, ff_added]
        from_one += [s_ for q in at for s_ in q.values()]

        def reach(eng, sem_, n):
            eng.wait_ge(sem_, n + 1)

        W_IN = [("L0_xattn_W_k", 0), ("L0_xattn_W_k_ip", 1), ("L0_xattn_W_v", 2), ("L0_xattn_W_v_ip", 3)]
        ATT = [("a1", P, CT), ("a2", P, P)]

        @block.sync
        def _(sp):
            for s_ in from_one:
                sp.sem_inc(s_, 1)
            for b in range(B):
                sp.dma_start(cm[:, b, :], ctx_in[b, 0:P, :]).then_inc(loaded_ctx, 16)
                sp.dma_start(ct[:, b, :], ctx_in[b, P:T, :]).then_inc(loaded_ctx, 16)
                sp.dma_start(ipn[b * NIP:(b + 1) * NIP, :], ctx_in[b, TT:T, :]).then_inc(loaded_ctx, 16)
            sp.dma_start(X[:, :, :], x.rearrange("b (t p) c -> p (b t) c", p=P)).then_inc(loaded_x, 16)
            for name, k in W_IN:
                sp.dma_start(wkv0[:, k, :, :], A[name].rearrange("(c p) n -> p c n", p=P)).then_inc(loaded_w0, 16)
            sp.dma_start(wq0[:, :], A["L0_xattn_W_q"][0:P, :]).then_inc(loaded_w0, 16)
            sp.dma_start(wq0t[:, :], A["L0_xattn_W_q"][P:C, :]).then_inc(loaded_w0, 16)
            sp.dma_start(wo0[:, :], A["L0_xattn_W_out"][0:P, :]).then_inc(loaded_w0, 16)
            sp.dma_start(wo0t[:, :], A["L0_xattn_W_out"][P:C, :]).then_inc(loaded_w0, 16)
            for k in range(3):
                for j, v in enumerate(("g", "b")):
                    col = A[f"L1_xattn_ln{k + 1}_{v}"].rearrange("(c a) -> c a", a=1)
                    sp.dma_start(gcol[:, 4 * k + j:4 * k + j + 1], col[0:P, :]).then_inc(loaded_small, 16)
                    sp.dma_start(gcol[0:CT, 4 * k + 2 + j:4 * k + 3 + j], col[P:C, :]).then_inc(loaded_small, 16)
            for k, v in enumerate(("L0_xattn_b_out", "L1_xattn_a1_bo", "L1_xattn_a2_bo", "L1_xattn_ff_b2")):
                sp.dma_start(brow[:, k, :], A[v].rearrange("(a c) -> a c", a=1).broadcast_to([P, C]))\
                    .then_inc(loaded_small, 16)
            sp.dma_start(b1col[:, :], A["L1_xattn_ff_b1"].rearrange("(c p) -> p c", p=P),
                         allow_slow_non_contiguous=True).then_inc(loaded_small, 16)
            sp.dma_start(smask[:, :], A["fside_S_0"].rearrange("(t p) -> p t", p=P),
                         allow_slow_non_contiguous=True).then_inc(loaded_small, 16)
            taken(sp, "out_3")
            for a, (pre, _, second) in enumerate(ATT):
                q = at[a]
                if a:
                    reach(sp, at[a - 1]["w"], 6 * PAIRS)
                    reach(sp, at[a - 1]["wo"], PAIRS)
                with sp.Fori(0, PAIRS) as i:
                    reach(sp, q["w"], 6 * i)
                    for n in ("q", "k", "v"):
                        src = A[f"L1_xattn_{pre}_w{n}"]
                        rows = src.shape[0] - P
                        sp.dma_start(raw[n][:, :], src[0:P, bass.ds(i * P, P)]).then_inc(q["raw"], 16)
                        sp.dma_start(rawt[n][0:rows, :], src[P:P + rows, bass.ds(i * P, P)]).then_inc(q["raw"], 16)
                    reach(sp, q["wo"], i)
                    sp.dma_start(raw["o"][:, :], A[f"L1_xattn_{pre}_wo"][bass.ds(i * P, P), :])\
                        .then_inc(q["rawo"], 16)
            ff1 = A["L1_xattn_ff_w1"].rearrange("k (s n) -> k s n", s=2)
            with sp.Fori(0, FCH) as c:
                reach(sp, ff_w, 5 * c)
                sp.dma_start(raw1[:, :, :], ff1[0:P, :, bass.ds(c * P, P)]).then_inc(ff_raw, 16)
                sp.dma_start(raw1t[:, :, :], ff1[P:C, :, bass.ds(c * P, P)]).then_inc(ff_raw, 16)
                sp.dma_start(raw2[:, :], A["L1_xattn_ff_w2"][bass.ds(c * P, P), :]).then_inc(ff_raw, 16)
            sp.wait_ge(x_final, 1)
            sp.dma_start(out.rearrange("b (t p) c -> p (b t) c", p=P), X[:, :, :]).then_inc(stored, 16)
            sp.wait_ge(stored, 16)

        @block.gpsimd
        def _(pool):
            steps = 0

            def hold(sem_, value):
                reach(pool, sem_, value)
                pool.sem_inc(pool_held, 1)

            def link(ins):
                nonlocal steps
                steps += 1
                ins.then_inc(pool_step, 1)
                pool.wait_ge(pool_step, steps)

            pool.memset(ident[:, :], 0.0).then_inc(pool_step, 1)
            pool.memset(bmask[:, :], 1.0).then_inc(pool_step, 1)
            pool.memset(KB0[:, :, :, :, :].bitcast(F32), 0.0).then_inc(pool_step, 1)
            pool.memset(GVt[:, :, :, :, :], 0.0).then_inc(pool_step, 1)
            pool.memset(P0[:, :, :, TT:PW], 0.0).then_inc(pool_step, 1)
            pool.memset(cT4[:, :, :, :, :], 0.0).then_inc(pool_step, 1)
            pool.memset(wqe[:, :, :], 0.0).then_inc(pool_step, 1)
            pool.memset(wqet[:, :, :], 0.0).then_inc(pool_step, 1)
            pool.memset(wke[:, :, :, :, :], 0.0).then_inc(pool_step, 1)
            steps += 9
            pool.wait_ge(pool_step, steps)
            link(pool.affine_select(out=ident[:, :], in_=ident[:, :], compare_op=ALU.not_equal, fill=1.0,
                                    base=0, pattern=[[-1, P]], channel_multiplier=1))
            bm = bmask[:, :].rearrange("p (h d) -> p h d", d=D0)
            link(pool.affine_select(out=bm, in_=bm, compare_op=ALU.is_ge, fill=0.0, base=0,
                                    pattern=[[-NIP, HEADS], [0, D0]], channel_multiplier=1))
            pool.affine_select(out=bm, in_=bm, compare_op=ALU.is_ge, fill=0.0, base=NIP - 1,
                               pattern=[[NIP, HEADS], [0, D0]], channel_multiplier=-1).then_inc(masks_ready, 1)
            pool.wait_ge(loaded_w0, 16 * 8)
            for dst, src in [(wqe[:, :, 0:24], wq0[:, :]), (wqet[:, :, 0:24], wq0t[:, :])] + [
                    (wke[:, k, c, :, 0:24], wkv0[:, k, c, :]) for k in range(2) for c in range(EC)]:
                rows = src.shape[0]
                pool.tensor_copy(dst.rearrange("p h (r d) -> p h r d", r=3),
                                 src.rearrange("p (h r d) -> p h r d", r=1, d=D0)
                                 .broadcast_to([rows, HEADS, 3, D0])).then_inc(spread_ready, 1)
            taken(pool, "cT1")
            for c in range(EC):
                pool.tensor_copy(ipR[:, c, :, :, :], cT[:, c, :, TT:T].rearrange("p b (h n) -> p b h n", h=1)
                                 .broadcast_to([P, B, HEADS, NIP])).then_inc(ip_ready, 1)
            for c in range(EC):
                for b in range(B):
                    pool.tensor_copy(cT4[:, c, b, :, 0:TTAIL],
                                     cT[:, c, b, P:T].rearrange("p (j n) -> p j n", j=1)
                                     .broadcast_to([P, 4, TTAIL])).then_inc(ip_ready, 1)
            taken(pool, f"Q0_{G4 - 1}_{B - 1}")
            with pool.Fori(0, QT) as i:
                hold(s0_ready, i * STEPS0)
                for b in range(B):
                    pool.tensor_copy(qs0[:, b, :, :], QT0[:, :, bass.ds(i * P + b * S, P)]).then_inc(q0_ready, 1)
                for n in range(STEPS0):
                    hold(p0_ready, i * STEPS0 + n + 1)
                    hold(t0_ready, i * STEPS0 + max(n - 1, 0))
                    pool.tensor_copy(P0t[:, n % 2, :, :], P0[:, n % 3, :, P:PW]).then_inc(p0t_ready, 1)
                for b in range(B):
                    hold(u0_taken, i * STEPS0 + (b + 1) * G4)
                    pool.tensor_copy(sta[:, bass.ds(i + b * QT, 1), :, 0:1],
                                     st0[:, b:b + 1, :, 0:1]).then_inc(st0_saved, 1)
                    pool.tensor_copy(sta[:, bass.ds(i + b * QT, 1), :, 1:2],
                                     den0[:, b:b + 1, :].rearrange("p b (h o) -> p b h o", o=1))\
                        .then_inc(st0_saved, 1)
                    pool.tensor_copy(sta[:, bass.ds(i + b * QT, 1), :, 2:ST],
                                     st0[:, b:b + 1, :, 2:ST]).then_inc(st0_saved, 1)
            pool.wait_ge(loaded_small, 16 * 18)
            taken(pool, "x_t1")
            pool.tensor_tensor(X[:, :, :], X[:, :, :], brow[:, 0:1, :].broadcast_to([P, NT, C]), ALU.add)\
                .then_inc(bias_added, 1)
            taken(pool, "out_3")
            for t in (kZ[:, :, :, :], vZ[:, :, :, :, :], kZ2[:, :, :, :], vZ2[:, :, :, :], vZ2t[:, :, :, :],
                      P2[:, :, :, T:PW]):
                pool.memset(t, 0.0).then_inc(zeroed, 1)
            for a, (pre, _, second) in enumerate(ATT):
                q = at[a]
                pool.wait_ge(xn_ready, a + 1)
                pool.tensor_tensor(X[:, :, :], X[:, :, :], brow[:, a + 1:a + 2, :].broadcast_to([P, NT, C]),
                                   ALU.add).then_inc(bias_added, 1)
                per = 6 if a == 0 else 5
                with pool.Fori(0, PAIRS) as i:
                    hold(q["raw"], i * 96 + 96)
                    for n in ("q", "k", "v"):
                        rows = A[f"L1_xattn_{pre}_w{n}"].shape[0] - P
                        pool.tensor_copy(wt[n][0:rows, :], rawt[n][0:rows, :]).then_inc(q["w"], 1)
                        pool.tensor_copy(w[n][:, :], raw[n][:, :]).then_inc(q["w"], 1)
                    for b in range(B):
                        if a == 1:
                            for n in (2 * b, 2 * b + 1):
                                hold(q["p"], i * 8 + 2 * n + 2)
                                hold(q["t"], i * 4 + max(n - 1, 0))
                                pool.tensor_copy(P2t[:, n % 2, :, :], P2[:, n % 2, :, P:PW]).then_inc(q["pt"], 1)
                        hold(q["rden"], i * B + b + 1)
                        m = (6 if a == 0 else 4) if b == 1 else 0
                        if b == 1:
                            hold(q[f"misc{m % 2}"], i * per + m // 2 + 1)
                        pool.tensor_copy(rsp[:, :, :, :], rden[:, b, :, :].rearrange("p t (h o) -> p t h o", o=1)
                                         .broadcast_to([P, QT, 2, D1])).then_inc(q["rsp"], 1)
                    m = 9 if a == 0 else 7
                    hold(q[f"misc{m % 2}"], i * per + m // 2 + 1)
            pool.wait_ge(xn_ready, 3)
            pool.tensor_tensor(X[:, :, :], X[:, :, :], brow[:, 3:4, :].broadcast_to([P, NT, C]), ALU.add)\
                .then_inc(bias_added, 1)
            with pool.Fori(0, FCH) as c:
                hold(ff_raw, c * 48 + 48)
                hold(ff_out, c * 4)
                pool.tensor_copy(w1[:, :, :], raw1[:, :, :]).then_inc(ff_w, 1)
                pool.tensor_copy(w1t[:, :, :], raw1t[:, :, :]).then_inc(ff_w, 1)
                pool.tensor_copy(w2[:, :], raw2[:, :]).then_inc(ff_w, 1)
                for s in range(2):
                    pool.tensor_copy(b1s[:, s:s + 1], b1col[:, bass.ds(c + s * FCH, 1)]).then_inc(ff_w, 1)

        @block.scalar
        def _(act):
            def copy(out_, in_, **kw):
                return act.activation(out_, in_, ACT.Copy, **kw)

            act.wait_ge(square_ready, 1)
            act.activation(ips[:, 3:4], ips[:, 1:2], ACT.Sqrt).then_inc(root_ready, 1)
            for c in range(EC):
                copy(cT[:, c, :, :], made(act, f"cT{c}")[:, 0:B * T].rearrange("p (b t) -> p b t", b=B))\
                    .then_inc(by_act, 1)
            for h in range(B):
                copy(nTm[:, h * S:(h + 1) * S], made(act, f"x_m{h}")).then_inc(by_act, 1)
            for n, (name, _) in enumerate([u for u in USES if u[0][:3] in ("K0_", "Q0_")]):
                if n >= 2:
                    taken(act, [u[0] for u in USES if u[0][:3] in ("K0_", "Q0_")][n - 2])
                cols = B * T if name[0] == "K" else 512
                copy(hi0[:, n % 2, 0:cols], made(act, name)[:, 0:cols],
                     scale=1.0 if name[0] == "K" else D0 ** -0.5).then_inc(hi_ready, 1)
            for b in range(B):
                ps = made(act, f"GV_{b}")
                copy(GV[:, b, :, 0:P], ps[:, 0:P].rearrange("p (h t) -> p h t", h=1).broadcast_to([P, HEADS, P]))
                copy(GV[:, b, :, P:TT], ps[:, P:TT].rearrange("p (h t) -> p h t", h=1)
                     .broadcast_to([P, HEADS, TXTAIL]), scale=2.0)
                copy(GV[:, b, :, TT:TT + D0], ps[:, TT:TT + C].rearrange("p (h d) -> p h d", d=D0))
                copy(GV[:, b, :, TT + D0:RHS], ps[:, TT + C:TT + C + NIP].rearrange("p (h n) -> p h n", h=1)
                     .broadcast_to([P, HEADS, NIP])).then_inc(by_act, 1)

            def exps0(i, n):
                b, g = n // G4, n % G4
                reach(act, m0_ready, i * STEPS0 + n + 1)
                reach(act, u0_taken, i * STEPS0 + max(n - 2, 0))
                if n % G4 == 0:
                    reach(act, st0_saved, i * 6)
                for j in range(4):
                    ins = act.activation(P0[:, n % 3, j, 0:TT], (bank01, bank23)[n % 2][:, j // 2, j % 2 * T:j % 2 * T + TT],
                                         ACT.Exp, bias=nmax0[:, n % 3, j:j + 1],
                                         accum_out=den0[:, b, 4 * g + j:4 * g + j + 1])
                ins.then_inc(p0_ready, 1)

            def evac0(i, n):
                reach(act, t0_ready, i * STEPS0 + n + 1)
                reach(act, u0_ready, i * STEPS0 + max(n - 1, 0))
                copy(PT0[:, n % 2, :, :], bank45[:, 0, :].rearrange("p (j s) -> p j s", j=4))
                copy(PT0t[:, n % 2, :], bank45[:, 1, 0:P]).then_inc(pt0_ready, 1)

            with act.Fori(0, QT) as i:
                for n in range(STEPS0 + 1):
                    if n < STEPS0:
                        exps0(i, n)
                    if n >= 1:
                        evac0(i, n - 1)
            act.wait_ge(square_ready, 2)
            act.activation(h1[:, :, :], h3[:, :, :], ACT.Sqrt).then_inc(root_ready, 1)
            act.wait_ge(f_ready, 1)
            act.activation(f2[:, :, :, :], f1[:, :, :, :], ACT.Exp).then_inc(fe_ready, 1)
            for h in range(B):
                copy(FT[:, h * S:(h + 1) * S], made(act, f"F_{h}")[0:4 * HEADS, :]).then_inc(by_act, 1)
            for h in range(B):
                copy(OTm[:, h * S:(h + 1) * S], made(act, f"O_m{h}")).then_inc(by_act, 1)
            for h in range(B):
                copy(OTt[:, h * S:(h + 1) * S], made(act, f"O_t{h}")[0:CT, :]).then_inc(by_act, 1)

            def norm_out(k):
                act.wait_ge(square_ready, k + 2)
                act.activation(root[:, :], var[:, :], ACT.Sqrt).then_inc(root_ready, 1)
                if k == 1:
                    act.wait_ge(loaded_small, 16 * 18)
                o = 4 * (k - 1)
                for h in range(B):
                    act.activation(nTm[:, h * S:(h + 1) * S], made(act, f"n{k}_m{h}"), ACT.Identity,
                                   scale=gcol[:, o:o + 1], bias=gcol[:, o + 1:o + 2]).then_inc(by_act, 1)
                for h in range(B):
                    act.activation(nTt[:, h * S:(h + 1) * S], made(act, f"n{k}_t{h}")[0:CT, :], ACT.Identity,
                                   scale=gcol[0:CT, o + 2:o + 3], bias=gcol[0:CT, o + 3:o + 4]).then_inc(by_act, 1)

            def query(q, i, per, m, b, scores):
                reach(act, q[f"misc{m % 2}"], i * per + m // 2 + 1)
                reach(act, q["s"], i * scores)
                copy(qT[:, b, :], bank[6 + m % 2], scale=D1 ** -0.5).then_inc(q[f"taken{m % 2}"], 1)

            def out_weights(q, i, per, last):
                reach(act, q["rawo"], i * 16 + 16)
                reach(act, q[f"misc{last % 2}"], i * per)
                copy(w["o"][:, :], raw["o"][:, :]).then_inc(q["wo"], 1)

            def spread_sums(q, i, per, m, b):
                reach(act, q[f"misc{m % 2}"], i * per + m // 2 + 1)
                reach(act, q["o"], i * B + b)
                copy(rbs[:, :], bank[6 + m % 2]).then_inc(q[f"taken{m % 2}"], 1)

            norm_out(1)
            q = at[0]

            def exps1(i, u):
                b, h = u // 2, u % 2
                reach(act, q["t"], i * 16 + max(4 * (u - 1), 0))
                if u == 0:
                    reach(act, q["rden"], i * B)
                for j in range(QT):
                    n = 4 * u + j
                    reach(act, q["m"], i * 16 + n + 1)
                    act.activation(pr[:, u % 2, j, :], bank[n % 3], ACT.Exp, bias=nmax[:, u % 2, j:j + 1],
                                   accum_out=den[:, b, j, h:h + 1]).then_inc(q["p"], 1)

            def evac1(i, u):
                n = 4 * u + 3
                reach(act, q["t"], i * 16 + n + 1)
                reach(act, q["pv"], i * 16 + max(n - 3, 0))
                copy(pT[:, 3, :], bank[3 + n % 2]).then_inc(q["pta"], 1)

            with act.Fori(0, PAIRS) as i:
                query(q, i, 6, 1, 0, 16)
                exps1(i, 0)
                query(q, i, 6, 4, 1, 16)
                out_weights(q, i, 6, 11)
                for u in range(4):
                    if u < 3:
                        exps1(i, u + 1)
                    evac1(i, u)
                    if u % 2:
                        spread_sums(q, i, 6, 6 if u == 1 else 9, u // 2)

            norm_out(2)
            r = at[1]

            def exps2(i, n):
                b, half = n // 2, n % 2
                reach(act, r["t"], i * 4 + max(n - 1, 0))
                if n == 0:
                    reach(act, r["rden"], i * B)
                for k in range(2):
                    reach(act, r["m"], i * 8 + 2 * n + k + 1)
                    for h in range(2):
                        ins = act.activation(P2[:, n % 2, 2 * k + h, 0:T], bank[(2 * n + k) % 3][:, h * T:(h + 1) * T],
                                             ACT.Exp, bias=nmax2[:, n % 2, 2 * k + h:2 * k + h + 1],
                                             accum_out=den[:, b, 2 * half + k, h:h + 1])
                    ins.then_inc(r["p"], 1)

            with act.Fori(0, PAIRS) as i:
                query(r, i, 5, 2, 0, 8)
                exps2(i, 0)
                query(r, i, 5, 3, 1, 8)
                exps2(i, 1)
                out_weights(r, i, 5, 9)
                exps2(i, 2)
                exps2(i, 3)
                spread_sums(r, i, 5, 4, 0)
                spread_sums(r, i, 5, 7, 1)

            norm_out(3)
            with act.Fori(0, FCH) as c:
                for h in range(B):
                    reach(act, ff_g, c * B + h + 1)
                    reach(act, ff_hid, c * B)
                    act.activation(gel[:, h * S:(h + 1) * S], bank[2 + h], ACT.Gelu, bias=b1s[:, 1:2])\
                        .then_inc(ff_gel, 1)

        @block.vector
        def _(dve):
            steps = 0

            def link(ins):
                nonlocal steps
                steps += 1
                ins.then_inc(dve_step, 1)
                dve.wait_ge(dve_step, steps)

            dve.wait_ge(loaded_ctx, 96)
            link(dve.tensor_tensor_reduce(out=ipj[:, :], in0=ipn[:, :], in1=ipn[:, :], scale=1.0, scalar=0.0,
                                          op0=ALU.mult, op1=ALU.add, accum_out=ips[:, 0:1]))
            dve.tensor_scalar(ips[:, 1:2], ips[:, 0:1], TINY, None, ALU.max).then_inc(square_ready, 1)
            dve.wait_ge(root_ready, 1)
            link(dve.tensor_scalar(ips[:, 1:2], ips[:, 3:4], EPS_NORM, None, ALU.max))
            link(dve.reciprocal(ips[:, 2:3], ips[:, 1:2]))
            dve.tensor_scalar(ipj[:, :], ipn[:, :], ips[:, 2:3], None, ALU.mult).then_inc(s_ipn, 1)
            dve.wait_ge(masks_ready, 1)
            heads = ident[:, :].rearrange("p (j r) -> p j r", j=4)
            link(dve.tensor_reduce(low_q[:, :], heads[:, :, 16:24], AX.XY, ALU.add))
            link(dve.tensor_reduce(low_k[:, :], heads[:, :, 8:16], AX.XY, ALU.add))
            link(dve.tensor_scalar(sign_q[:, :], low_q[:, :], -2.0, 1.0, ALU.mult, ALU.add))
            link(dve.tensor_scalar(sign_k[:, :], low_k[:, :], -2.0, 1.0, ALU.mult, ALU.add))
            dve.tensor_copy(ipT[:, :, :], made(dve, "ipT")[:, 0:EC * B * NIP].rearrange("p (c n) -> p c n", c=EC))\
                .then_inc(by_dve, 1)
            for h in range(B):
                dve.tensor_copy(nTt[:, h * S:(h + 1) * S], made(dve, f"x_t{h}")[0:CT, :]).then_inc(by_dve, 1)
            for n, (name, _) in enumerate([u for u in USES if u[0][:3] in ("K0_", "Q0_")]):
                ps = made(dve, name)
                dve.wait_ge(hi_ready, n + 1)
                g = int(name.split("_")[1])
                if name[0] == "K":
                    link(dve.tensor_scalar(tm0[:, n % 2, 0:B * T], hi0[:, n % 2, 0:B * T].bitcast(F32),
                                           sign_k[:, 0:1], None, ALU.mult))
                    for j in range(4):
                        r = slice(32 * j, 32 * j + 32)
                        ins = dve.scalar_tensor_tensor(
                            out=KB0[r, g, :, j, :], in0=ps[r, 0:B * T].rearrange("p (b t) -> p b t", b=B),
                            scalar=low_k[r, 0:1], in1=tm0[r, n % 2, 0:B * T].rearrange("p (b t) -> p b t", b=B),
                            op0=ALU.mult, op1=ALU.add)
                    ins.then_inc(by_dve, 1)
                else:
                    h = int(name.split("_")[2])
                    link(dve.tensor_scalar(tm0[:, n % 2, :], hi0[:, n % 2, :].bitcast(F32), sign_q[:, 0:1], None,
                                           ALU.mult))
                    link(dve.tensor_scalar(scl[:, :], ps, D0 ** -0.5, low_q[:, 0:1], ALU.mult, ALU.mult))
                    dve.tensor_tensor(QT0[:, g, h * S:(h + 1) * S], scl[:, :], tm0[:, n % 2, :], ALU.add)\
                        .then_inc(by_dve, 1)
            for b in range(B):
                ps = made(dve, f"GVt_{b}")
                for j in range(4):
                    r = slice(32 * j, 32 * j + 32)
                    dve.tensor_copy(GVt[r, b, :, j, 0:TXTAIL], ps[r, 0:TXTAIL].rearrange("p (g t) -> p g t", g=1)
                                    .broadcast_to([32, G4, TXTAIL]))
                    dve.tensor_copy(GVt[r, b, :, j, TXTAIL:TXTAIL + D0],
                                    ps[r, TXTAIL:TXTAIL + C].rearrange("p (g j d) -> p g j d", j=4, d=D0)[:, :, j, :])
                    ins = dve.tensor_copy(GVt[r, b, :, j, TXTAIL + D0:RHT],
                                          ps[r, TXTAIL + C:TXTAIL + C + NIP].rearrange("p (g n) -> p g n", g=1)
                                          .broadcast_to([32, G4, NIP]))
                ins.then_inc(by_dve, 1)
            for b in range(B):
                dve.tensor_tensor(VB0[:, b, :], made(dve, f"VB_{b}")[0:4 * HEADS, 0:C], bmask[:, :], ALU.mult)\
                    .then_inc(by_dve, 1)

            def max0(i, n):
                b, g = n // G4, n % G4
                sc = (bank01, bank23)[n % 2][:, :, 0:2 * T].rearrange("p k (j t) -> p k j t", j=2)
                reach(dve, s0_ready, i * STEPS0 + n + 1)
                if g == 0:
                    reach(dve, st0_saved, i * 6)
                dve.tensor_reduce(nmax0[:, n % 3, :].rearrange("p (k j) -> p k j", k=2), sc[:, :, :, 0:TT], AX.X,
                                  ALU.max, negate=True)
                dve.tensor_copy(st0[:, b, 4 * g:4 * g + 4, 2 + D0 + NIP:ST].rearrange("p (k j) n -> p k j n", k=2),
                                sc[:, :, :, TT:T]).then_inc(m0_ready, 1)

            def norms0(i, n):
                b, g = n // G4, n % G4
                reach(dve, u0_ready, i * STEPS0 + n + 1)
                for j in range(4):
                    u = bank67[:, j // 2, j % 2 * RHS:j % 2 * RHS + RHS]
                    dve.tensor_tensor_reduce(out=P0[:, n % 3, j, 0:TT], in0=u[:, 0:TT], in1=P0[:, n % 3, j, 0:TT], scale=1.0,
                                             scalar=0.0, op0=ALU.mult, op1=ALU.add,
                                             accum_out=st0[:, b, 4 * g + j, 0:1])
                dve.tensor_copy(st0[:, b, 4 * g:4 * g + 4, 2:2 + D0 + NIP].rearrange("p (k j) n -> p k j n", k=2),
                                bank67[:, :, 0:2 * RHS].rearrange("p k (j t) -> p k j t", j=2)[:, :, :, TT:RHS])\
                    .then_inc(u0_taken, 1)

            with dve.Fori(0, QT) as i:
                for n in range(STEPS0 + 2):
                    if n < STEPS0:
                        max0(i, n)
                    if n >= 2:
                        norms0(i, n - 2)
            reach(dve, st0_saved, 6 * QT)
            sq, sums = sta[:, :, :, 0], sta[:, :, :, 1]
            text, dots, simg = sta[:, :, :, 2:2 + D0], sta[:, :, :, 2 + D0:2 + D0 + NIP], sta[:, :, :, 2 + D0 + NIP:ST]

            def wide(t, n):
                return t[:, :, :].rearrange("p t (h o) -> p t h o", o=1).broadcast_to([P, NT, HEADS, n])

            dve.tensor_scalar(h3[:, :, :], sq, TINY, None, ALU.max).then_inc(square_ready, 1)
            dve.wait_ge(root_ready, 2)
            link(dve.scalar_tensor_tensor(out=h2[:, :, :], in0=sums, scalar=EPS_NORM, in1=h1[:, :, :],
                                          op0=ALU.mult, op1=ALU.max))
            link(dve.reciprocal(h1[:, :, :], h2[:, :, :]))
            link(dve.tensor_tensor(f1[:, :, :, :], dots, wide(h1, NIP), ALU.mult))
            link(dve.scalar_tensor_tensor(out=f2[:, :, :, :], in0=f1[:, :, :, :], scalar=SEM_SCALE, in1=simg,
                                          op0=ALU.mult, op1=ALU.add))
            link(dve.tensor_reduce(h2[:, :, :], f2[:, :, :, :], AX.X, ALU.max))
            dve.tensor_tensor(f1[:, :, :, :], f2[:, :, :, :], wide(h2, NIP), ALU.subtract).then_inc(f_ready, 1)
            link(dve.reciprocal(h3[:, :, :], sums))
            dve.tensor_tensor(TX[:, :, :, :], text, wide(h3, D0), ALU.mult).then_inc(dve_step, 1)
            steps += 1
            dve.wait_ge(fe_ready, 1)
            link(dve.tensor_reduce(h1[:, :, :], f2[:, :, :, :], AX.X, ALU.add))
            link(dve.reciprocal(h2[:, :, :], h1[:, :, :]))
            dve.wait_ge(loaded_small, 16 * 18)
            for b in range(B):
                ins = dve.tensor_tensor(h3[:, b * QT:(b + 1) * QT, :], h2[:, b * QT:(b + 1) * QT, :],
                                        smask[:, :].rearrange("p (t o) -> p t o", o=1).broadcast_to([P, QT, HEADS]),
                                        ALU.mult)
            link(ins)
            dve.tensor_tensor(f1[:, :, :, :], f2[:, :, :, :], wide(h3, NIP), ALU.mult).then_inc(fn_ready, 1)
            dve.wait_ge(bias_added, 1)
            for k in range(4):
                dve.tensor_tensor(X[:, 2 * k:2 * k + 2, :], X[:, 2 * k:2 * k + 2, :],
                                  made(dve, f"out_{k}")[:, 0:2 * C].rearrange("p (t c) -> p t c", t=2), ALU.add)\
                    .then_inc(by_dve, 1)
            dve.wait_ge(by_dve, sum(e == "dve" for _, e in USES))

            norms = 0

            def norm():
                nonlocal steps, norms
                for t in range(NT):
                    dve.bn_stats(bn6[:, t, :], X[:, t, :]).then_inc(dve_step, 1)
                for t in range(NT):
                    dve.wait_ge(dve_step, steps + t + 1)
                    dve.bn_aggr(mv[:, t, :], bn6[:, t, :]).then_inc(dve_step, 1)
                steps += 2 * NT
                dve.wait_ge(dve_step, steps)
                dve.tensor_scalar(var[:, :], mv[:, :, 1], EPS_LN, None, ALU.add).then_inc(square_ready, 1)
                norms += 1
                dve.wait_ge(root_ready, 2 + norms)
                link(dve.reciprocal(rstd[:, :], root[:, :]))
                for t in range(NT):
                    ins = dve.tensor_scalar(XN[:, t, :], X[:, t, :], mv[:, t, 0:1], rstd[:, t:t + 1],
                                            ALU.subtract, ALU.mult)
                ins.then_inc(xn_ready, 1)

            def add_out(q, i, per, m, k):
                reach(dve, q[f"misc{m % 2}"], i * per + m // 2 + 1)
                dve.tensor_tensor(X[:, 2 * k:2 * k + 2, :], X[:, 2 * k:2 * k + 2, :],
                                  bank[6 + m % 2][:, 0:2 * C].rearrange("p (t c) -> p t c", t=2), ALU.add)\
                    .then_inc(q[f"taken{m % 2}"], 1)

            def inverse_sums(q, i, ready, b):
                reach(dve, q["p"], ready)
                dve.reciprocal(rden[:, b, :, :], den[:, b, :, :]).then_inc(q["rden"], 1)

            def scale_out(q, i, per, m, b, pv):
                reach(dve, q[f"taken{m % 2}"], i * per + m // 2 + 1)
                reach(dve, q["pv"], pv)
                dve.tensor_tensor(oT[:, b, :], bank[5], rbs[:, :], ALU.mult).then_inc(q["o"], 1)

            norm()
            dve.wait_ge(bias_added, 2)
            dve.wait_ge(zeroed, 6)
            q = at[0]

            def keys(i, b):
                m = 0 if b == 0 else 3
                reach(dve, q[f"misc{m % 2}"], i * 6 + m // 2 + 1)
                reach(dve, q["s"], i * 16)
                dve.tensor_copy(kZ[0:64, b, 0, :], bank[6 + m % 2][0:64, :])
                dve.tensor_copy(kZ[64:P, b, 1, :], bank[6 + m % 2][64:P, :]).then_inc(q[f"taken{m % 2}"], 1)

            def values(i, b):
                m = 2 if b == 0 else 5
                reach(dve, q[f"misc{m % 2}"], i * 6 + m // 2 + 1)
                reach(dve, q["pv"], i * 16)
                ps = bank[6 + m % 2].rearrange("p (k d) -> p k d", k=KC)
                dve.tensor_copy(vZ[:, b, 0, :, 0:64], ps[:, :, 0:64])
                dve.tensor_copy(vZ[:, b, 1, :, 64:P], ps[:, :, 64:P]).then_inc(q[f"taken{m % 2}"], 1)

            def max1(i, n):
                reach(dve, q["s"], i * 16 + n + 1)
                dve.tensor_reduce(nmax[:, n // 4 % 2, n % 4:n % 4 + 1], bank[n % 3], AX.X, ALU.max, negate=True)\
                    .then_inc(q["m"], 1)

            def evac1(i, n):
                reach(dve, q["t"], i * 16 + n + 1)
                reach(dve, q["pv"], i * 16 + max(n - 3, 0))
                dve.tensor_copy(pT[:, n % 4, :], bank[3 + n % 2]).then_inc(q["ptd"], 1)

            with dve.Fori(0, PAIRS) as i:
                keys(i, 0)
                for n in range(3):
                    max1(i, n)
                values(i, 0)
                max1(i, 3)
                keys(i, 1)
                values(i, 1)
                for u in range(4):
                    for j in range(4):
                        if u < 3:
                            max1(i, 4 * u + 4 + j)
                        if j < 3:
                            evac1(i, 4 * u + j)
                    if u % 2:
                        inverse_sums(q, i, i * 16 + 8 * (u // 2 + 1), u // 2)
                        scale_out(q, i, 6, 6 if u == 1 else 9, u // 2, i * 16 + 8 * (u // 2 + 1))
                    if u == 2:
                        add_out(q, i, 6, 7, 0)
                        add_out(q, i, 6, 8, 1)
                add_out(q, i, 6, 10, 2)
                add_out(q, i, 6, 11, 3)
            reach(dve, q["taken1"], 6 * PAIRS)

            norm()
            dve.wait_ge(bias_added, 3)
            r = at[1]

            def max2(i, n):
                for k in range(2):
                    reach(dve, r["s"], i * 8 + 2 * n + k + 1)
                    dve.tensor_reduce(nmax2[:, n % 2, 2 * k:2 * k + 2],
                                      bank[(2 * n + k) % 3][:, 0:2 * T].rearrange("p (h t) -> p h t", h=2),
                                      AX.X, ALU.max, negate=True).then_inc(r["m"], 1)

            def evac2(i, n):
                reach(dve, r["t"], i * 4 + n + 1)
                reach(dve, r["pv"], i * 4 + max(n - 1, 0))
                dve.tensor_copy(P2T[:, n % 2, :, :], bank[3].rearrange("p (j s) -> p j s", j=4))
                dve.tensor_copy(P2Tt[:, n % 2, :], bank[4][:, 0:P]).then_inc(r["ptd"], 1)

            with dve.Fori(0, PAIRS) as i:
                reach(dve, r["misc0"], i * 5 + 1)
                reach(dve, r["s"], i * 8)
                ps = bank[6][:, 0:B * T].rearrange("p (b t) -> p b t", b=B)
                dve.tensor_copy(kZ2[0:64, :, 0, :], ps[0:64])
                dve.tensor_copy(kZ2[64:P, :, 1, :], ps[64:P]).then_inc(r["taken0"], 1)
                reach(dve, r["misc1"], i * 5 + 1)
                reach(dve, r["pv"], i * 4)
                ps = bank[7].rearrange("p (s b d) -> p s b d", s=2, b=B)
                for h in range(2):
                    dve.tensor_copy(vZ2[:, :, h, 64 * h:64 * h + 64], ps[:, 0, :, 64 * h:64 * h + 64])
                for k in range(2):
                    for h in range(2):
                        rows = slice(64 * k + 32 * h, 64 * k + 32 * h + 32)
                        ins = dve.tensor_copy(vZ2t[rows, :, k, 64 * h:64 * h + 64], ps[rows, 1, :, 64 * h:64 * h + 64])
                ins.then_inc(r["taken1"], 1)
                max2(i, 0)
                max2(i, 1)
                max2(i, 2)
                evac2(i, 0)
                max2(i, 3)
                inverse_sums(r, i, i * 8 + 4, 0)
                evac2(i, 1)
                evac2(i, 2)
                scale_out(r, i, 5, 4, 0, i * 4 + 2)
                inverse_sums(r, i, i * 8 + 8, 1)
                evac2(i, 3)
                add_out(r, i, 5, 5, 0)
                add_out(r, i, 5, 6, 1)
                scale_out(r, i, 5, 7, 1, i * 4 + 4)
                add_out(r, i, 5, 8, 2)
                add_out(r, i, 5, 9, 3)
            reach(dve, r["taken1"], 5 * PAIRS)

            norm()
            dve.wait_ge(bias_added, 4)
            with dve.Fori(0, FCH) as c:
                for h in range(B):
                    reach(dve, ff_a, c * B + h + 1)
                    reach(dve, ff_gel, c * B + h + 1)
                    dve.scalar_tensor_tensor(out=hid[:, h * S:(h + 1) * S], in0=bank[h], scalar=b1s[:, 0:1],
                                             in1=gel[:, h * S:(h + 1) * S], op0=ALU.add, op1=ALU.mult)\
                        .then_inc(ff_hid, 1)
                for k in range(4):
                    reach(dve, ff_out, c * 4 + k + 1)
                    dve.tensor_tensor(X[:, 2 * k:2 * k + 2, :], X[:, 2 * k:2 * k + 2, :],
                                      bank[4 + k][:, 0:2 * C].rearrange("p (t c) -> p t c", t=2), ALU.add)\
                        .then_inc(ff_added, 1)
            reach(dve, ff_added, 4 * FCH)
            dve.sem_inc(x_final, 1)

        @block.tensor
        def _(pe):
            def done(ins):
                ins.then_inc(ps_ready, 1)

            pe.wait_ge(masks_ready, 1)
            pe.wait_ge(loaded_ctx, 96)
            for c in range(EC):
                ps = make(pe, f"cT{c}")
                for b in range(B):
                    pe.transpose(ps[:, b * T:b * T + P], cm[:, b, c * P:(c + 1) * P], ident[:, :])
                    ins = pe.transpose(ps[:, b * T + P:(b + 1) * T], ct[:, b, c * P:(c + 1) * P],
                                       ident[0:TTAIL, 0:TTAIL])
                done(ins)
            pe.wait_ge(s_ipn, 1)
            ps = make(pe, "ipT")
            for c in range(EC):
                ins = pe.transpose(ps[:, c * 8:(c + 1) * 8], ipj[:, c * P:(c + 1) * P], ident[0:8, 0:8])
            done(ins)

            def turn(src, kind):
                for part, cols in (("m", slice(0, P)), ("t", slice(P, C))):
                    for h in range(B):
                        ps = make(pe, f"{kind}_{part}{h}")
                        for t in range(QT):
                            ins = pe.transpose(ps[0:cols.stop - cols.start, t * P:(t + 1) * P],
                                               src[:, h * QT + t, cols], ident[:, :])
                        done(ins)

            pe.wait_ge(loaded_x, 16)
            turn(X, "x")
            pe.wait_ge(spread_ready, 6)
            taken(pe, "cT1")
            for g in range(G4):
                ps = make(pe, f"K0_{g}")[:, 0:B * T].rearrange("p (b t) -> p b t", b=B)
                for k, cols in ((0, slice(0, TT)), (1, slice(TT, T))):
                    for c in range(EC):
                        ins = pe.matmul(ps[:, :, cols], wke[:, k, c, 4 * g:4 * g + 4, :], cT[:, c, :, cols],
                                        start=(c == 0), stop=(c == EC - 1))
                done(ins)
            taken(pe, "x_m1")
            taken(pe, "x_t1")
            for g in range(G4):
                for h in range(B):
                    ps = make(pe, f"Q0_{g}_{h}")
                    pe.matmul(ps, wqe[:, 4 * g:4 * g + 4, :], nTm[:, h * S:(h + 1) * S], start=True, stop=False)
                    done(pe.matmul(ps, wqet[:, 4 * g:4 * g + 4, :], nTt[:, h * S:(h + 1) * S], start=False, stop=True))
            pe.wait_ge(ip_ready, EC + EC * B)
            taken(pe, "ipT")
            for tail in range(2):
                for b in range(B):
                    ps = make(pe, f"GVt_{b}" if tail else f"GV_{b}")
                    at_ = 0
                    lo = P if tail else 0
                    for width, rhs in ((TT - lo, lambda c: cT[:, c, b, lo:TT]), (C, lambda c: wkv0[:, 2, c, :]),
                                       (NIP, lambda c: ipT[:, c, b * NIP:(b + 1) * NIP])):
                        for c in range(EC):
                            lhs = cT4[:, c, b, :, :] if tail else cT[:, c, b, 0:P]
                            ins = pe.matmul(ps[:, at_:at_ + width], lhs, rhs(c), start=(c == 0), stop=(c == EC - 1))
                        at_ += width
                    done(ins)
            for b in range(B):
                ps = make(pe, f"VB_{b}")
                for c in range(EC):
                    ins = pe.matmul(ps[0:4 * HEADS, 0:C], ipR[:, c, b, :, :], wkv0[:, 3, c, :],
                                    start=(c == 0), stop=(c == EC - 1))
                done(ins)
            taken(pe, "GVt_1")
            taken(pe, "VB_1")
            taken(pe, "GV_1")

            def scores0(i, n):
                b, g = n // G4, n % G4
                if g == 0:
                    reach(pe, q0_ready, i * B + b + 1)
                reach(pe, p0_ready, i * STEPS0 + max(n - 1, 0))
                sc = (bank01, bank23)[n % 2]
                for k in range(2):
                    ins = pe.matmul(sc[:, k, 0:2 * T], qs0[:, b, g, :], KB0[:, g, b, 2 * k:2 * k + 2, :],
                                    start=True, stop=True)
                ins.then_inc(s0_ready, 1)

            def turn0(i, n):
                reach(pe, p0_ready, i * STEPS0 + n + 1)
                reach(pe, pt0_ready, i * STEPS0 + n)
                for j in range(4):
                    pe.transpose(bank45[:, 0, j * P:(j + 1) * P], P0[:, n % 3, j, 0:P], ident[:, :])
                reach(pe, p0t_ready, i * STEPS0 + n + 1)
                pe.transpose(bank45[:, 1, 0:P], P0t[:, n % 2, :, :], ident[:, :]).then_inc(t0_ready, 1)

            def mix0(i, n):
                b, g = n // G4, n % G4
                reach(pe, pt0_ready, i * STEPS0 + n + 1)
                reach(pe, u0_taken, i * STEPS0 + n)
                for k in range(2):
                    for j in range(2):
                        pe.matmul(bank67[:, k, j * RHS:(j + 1) * RHS], PT0[:, n % 2, 2 * k + j, :],
                                  GV[:, b, 4 * g + 2 * k + j, :], start=(j == 0), stop=False, skip_group_check=True)
                    ins = pe.matmul(bank67[:, k, 0:2 * RHS].rearrange("p (j t) -> p j t", j=2)[:, :, P:RHS],
                                    PT0t[:, n % 2, :], GVt[:, b, g, 2 * k:2 * k + 2, :], start=False, stop=True,
                                    skip_group_check=True)
                ins.then_inc(u0_ready, 1)

            with pe.Fori(0, QT) as i:
                for n in range(STEPS0 + 2):
                    if n < STEPS0:
                        scores0(i, n)
                    if 1 <= n <= STEPS0:
                        turn0(i, n - 1)
                    if n >= 2:
                        mix0(i, n - 2)
            pe.wait_ge(fn_ready, 1)
            for h in range(B):
                ps = make(pe, f"F_{h}")
                for t in range(QT):
                    ins = pe.transpose(ps[0:4 * HEADS, t * P:(t + 1) * P],
                                       f1[:, h * QT + t, :, :].rearrange("p h n -> p (h n)"), ident[:, :])
                done(ins)
            for part, lo, hi in (("m", 0, P), ("t", P, C)):
                for b in range(B):
                    ps = make(pe, f"O_{part}{b}")[0:hi - lo, :]
                    taken(pe, f"F_{b}")
                    pe.matmul(ps, VB0[:, b, lo:hi], FT[:, b * S:(b + 1) * S], start=True, stop=False,
                              skip_group_check=True)
                    for t in range(QT):
                        tx = TX[:, b * QT + t, :, :].rearrange("p h d -> p (h d)")
                        ins = pe.matmul(ps[:, t * P:(t + 1) * P], tx[:, lo:hi], ident[:, :], start=False,
                                        stop=True, skip_group_check=True)
                    done(ins)
            for k in range(4):
                ps = make(pe, f"out_{k}")
                taken(pe, "O_t1")
                for j in range(2):
                    t = 2 * k + j
                    pe.matmul(ps[:, j * C:(j + 1) * C], OTm[:, t * P:(t + 1) * P], wo0[:, :], start=True, stop=False)
                    ins = pe.matmul(ps[:, j * C:(j + 1) * C], OTt[:, t * P:(t + 1) * P], wo0t[:, :], start=False,
                                    stop=True)
                done(ins)

            def misc(q, i, per, m):
                reach(pe, q[f"taken{m % 2}"], i * per + m // 2)
                return bank[6 + m % 2]

            def made_misc(q, m, ins):
                ins.then_inc(q[f"misc{m % 2}"], 1)

            def query(q, i, per, m, b, kind):
                ps = misc(q, i, per, m)
                pe.matmul(ps, w[kind][:, :], nTm[:, b * S:(b + 1) * S], start=True, stop=False)
                made_misc(q, m, pe.matmul(ps, wt[kind][0:CT, :], nTt[:, b * S:(b + 1) * S], start=False, stop=True))

            def spread_sums(q, i, per, m, b):
                ps = misc(q, i, per, m)
                reach(pe, q["rsp"], i * B + b + 1)
                for t in range(QT):
                    ins = pe.transpose(ps[:, t * P:(t + 1) * P], rsp[:, t, :, :], ident[:, :])
                made_misc(q, m, ins)

            def project(q, i, per, m, k):
                b = k // 2
                ps = misc(q, i, per, m)
                reach(pe, q["o"], i * B + b + 1)
                reach(pe, q["wo"], i + 1)
                for j in range(2):
                    t = 2 * (k % 2) + j
                    ins = pe.matmul(ps[:, j * C:(j + 1) * C], oT[:, b, t * P:(t + 1) * P], w["o"][:, :],
                                    start=True, stop=True)
                made_misc(q, m, ins)

            pe.wait_ge(xn_ready, 1)
            turn(XN, "n1")
            taken(pe, "n1_t1")
            q = at[0]

            def values(i, m, b):
                ps = misc(q, i, 6, m)
                for k in range(KC):
                    t = b * KC + k
                    pe.matmul(ps[:, k * P:(k + 1) * P], nTm[:, t * P:(t + 1) * P], w["v"][:, :], start=(k == 0),
                              stop=False, skip_group_check=True)
                    ins = pe.matmul(ps[:, k * P:(k + 1) * P], nTt[:, t * P:(t + 1) * P], wt["v"][0:CT, :],
                                    start=False, stop=True, skip_group_check=True)
                made_misc(q, m, ins)

            def scores1(i, n):
                u, j = n // 4, n % 4
                b, h = u // 2, u % 2
                if j == 0 and h == 0:
                    k, m = (0, 1) if b == 0 else (3, 4)
                    for x_ in (k, m):
                        reach(pe, q[f"taken{x_ % 2}"], i * 6 + x_ // 2 + 1)
                reach(pe, q["p"], i * 16 + max(n - 2, 0))
                pe.matmul(bank[n % 3], qT[:, b, j * P:(j + 1) * P], kZ[:, b, h, :], start=True, stop=True)\
                    .then_inc(q["s"], 1)

            def copied(i, n):
                if n % 4 == 3:
                    reach(pe, q["pta"], i * 4 + n // 4 + 1)
                else:
                    reach(pe, q["ptd"], i * 12 + n // 4 * 3 + n % 4 + 1)

            def turn1(i, n):
                u, j = n // 4, n % 4
                if j == 0:
                    reach(pe, q["p"], i * 16 + 4 * (u + 1))
                if n >= 2:
                    copied(i, n - 2)
                for t in range(QT):
                    ins = pe.transpose(bank[3 + n % 2][:, t * P:(t + 1) * P], pr[:, u % 2, t, j * P:(j + 1) * P],
                                       ident[:, :])
                ins.then_inc(q["t"], 1)

            def mix1(i, n):
                u, j = n // 4, n % 4
                b, h = u // 2, u % 2
                if h == 0 and j == 0:
                    reach(pe, q["o"], i * B + b)
                    m = 2 if b == 0 else 5
                    reach(pe, q[f"taken{m % 2}"], i * 6 + m // 2 + 1)
                copied(i, n)
                pe.matmul(bank[5], vZ[:, b, h, j, :], pT[:, n % 4, :], start=(h == 0 and j == 0),
                          stop=(h == 1 and j == 3)).then_inc(q["pv"], 1)

            with pe.Fori(0, PAIRS) as i:
                reach(pe, q["w"], 6 * i + 6)
                query(q, i, 6, 0, 0, "k")
                query(q, i, 6, 1, 0, "q")
                for n in range(3):
                    scores1(i, n)
                values(i, 2, 0)
                scores1(i, 3)
                query(q, i, 6, 3, 1, "k")
                query(q, i, 6, 4, 1, "q")
                values(i, 5, 1)
                for u in range(4):
                    for j in range(4):
                        if u < 3:
                            scores1(i, 4 * u + 4 + j)
                        turn1(i, 4 * u + j)
                        if j:
                            mix1(i, 4 * u + j - 1)
                    mix1(i, 4 * u + 3)
                    if u % 2:
                        spread_sums(q, i, 6, 6 if u == 1 else 9, u // 2)
                    if u == 2:
                        project(q, i, 6, 7, 0)
                        project(q, i, 6, 8, 1)
                project(q, i, 6, 10, 2)
                project(q, i, 6, 11, 3)

            pe.wait_ge(xn_ready, 2)
            turn(XN, "n2")
            taken(pe, "n2_t1")
            r = at[1]

            def scores2(i, n):
                b, half = n // 2, n % 2
                if half == 0:
                    m = 2 + b
                    reach(pe, r[f"taken{m % 2}"], i * 5 + m // 2 + 1)
                for k in range(2):
                    reach(pe, r["p"], i * 8 + max(2 * n + k - 2, 0))
                    t = 2 * half + k
                    pe.matmul(bank[(2 * n + k) % 3][:, 0:2 * T], qT[:, b, t * P:(t + 1) * P], kZ2[:, b, :, :],
                              start=True, stop=True).then_inc(r["s"], 1)

            def turn2(i, n):
                reach(pe, r["p"], i * 8 + 2 * n + 2)
                reach(pe, r["ptd"], i * 4 + n)
                for h in range(2):
                    for k in range(2):
                        c = 2 * h + k
                        pe.transpose(bank[3][:, c * P:(c + 1) * P], P2[:, n % 2, 2 * k + h, 0:P], ident[:, :])
                reach(pe, r["pt"], i * 4 + n + 1)
                pe.transpose(bank[4][:, 0:P], P2t[:, n % 2, :, :], ident[:, :]).then_inc(r["t"], 1)

            def mix2(i, n):
                b, half = n // 2, n % 2
                if half == 0:
                    reach(pe, r["o"], i * B + b)
                reach(pe, r["ptd"], i * 4 + n + 1)
                for h in range(2):
                    pe.matmul(bank[5][:, half * 256:half * 256 + 256], vZ2[:, b, h, :],
                              P2T[:, n % 2, 2 * h:2 * h + 2, :], start=(h == 0), stop=False, skip_group_check=True)
                for k in range(2):
                    o = half * 256 + k * P
                    ins = pe.matmul(bank[5][:, o:o + P], vZ2t[:, b, k, :], P2Tt[:, n % 2, :], start=False, stop=True,
                                    skip_group_check=True)
                ins.then_inc(r["pv"], 1)

            with pe.Fori(0, PAIRS) as i:
                reach(pe, r["w"], 6 * i + 6)
                ps = misc(r, i, 5, 0)
                for c, wk in enumerate((w["k"], wt["k"])):
                    ins = pe.matmul(ps[:, 0:B * T], wk[:, :], cT[:, c, :, :], start=(c == 0), stop=(c == 1))
                made_misc(r, 0, ins)
                ps = misc(r, i, 5, 1)
                for k in range(4):
                    b = k % 2
                    for c, wv in enumerate((w["v"], wt["v"])):
                        lhs = cT[:, c, b, 0:P] if k < 2 else cT4[:, c, b, :, :]
                        ins = pe.matmul(ps[:, k * P:(k + 1) * P], lhs, wv[:, :], start=(k == 0 and c == 0),
                                        stop=(c == 1), skip_group_check=True)
                made_misc(r, 1, ins)
                query(r, i, 5, 2, 0, "q")
                reach(pe, r["taken0"], i * 5 + 1)
                scores2(i, 0)
                query(r, i, 5, 3, 1, "q")
                reach(pe, r["taken1"], i * 5 + 1)
                scores2(i, 1)
                turn2(i, 0)
                scores2(i, 2)
                turn2(i, 1)
                mix2(i, 0)
                scores2(i, 3)
                turn2(i, 2)
                mix2(i, 1)
                spread_sums(r, i, 5, 4, 0)
                turn2(i, 3)
                mix2(i, 2)
                project(r, i, 5, 5, 0)
                project(r, i, 5, 6, 1)
                mix2(i, 3)
                spread_sums(r, i, 5, 7, 1)
                project(r, i, 5, 8, 2)
                project(r, i, 5, 9, 3)

            pe.wait_ge(xn_ready, 3)
            turn(XN, "n3")
            taken(pe, "n3_t1")
            with pe.Fori(0, FCH) as c:
                reach(pe, ff_w, 5 * c + 5)
                for s, made_sem, free in ((1, ff_g, ff_gel), (0, ff_a, ff_hid)):
                    for h in range(B):
                        reach(pe, free, c * B)
                        pe.matmul(bank[2 * s + h], w1[:, s, :], nTm[:, h * S:(h + 1) * S], start=True, stop=False)
                        pe.matmul(bank[2 * s + h], w1t[:, s, :], nTt[:, h * S:(h + 1) * S], start=False, stop=True)\
                            .then_inc(made_sem, 1)
                for k in range(4):
                    reach(pe, ff_hid, c * B + k // 2 + 1)
                    reach(pe, ff_added, c * 4)
                    for j in range(2):
                        t = 2 * k + j
                        ins = pe.matmul(bank[4 + k][:, j * C:(j + 1) * C], hid[:, t * P:(t + 1) * P], w2[:, :],
                                        start=True, stop=True)
                    ins.then_inc(ff_out, 1)


def kernel(**inputs):
    import numpy as _np
    import concourse.bacc as _bacc
    from concourse import mybir as _mybir
    from concourse.bass_utils import run_bass_kernel_spmd as _run

    nc = _bacc.Bacc("TRN2", target_bir_lowering=False, num_devices=1)
    arrays, aps = {}, {}
    for name in inputs:
        a = _np.ascontiguousarray(inputs[name])
        arrays[f"in_{name}"] = a
        aps[name] = nc.dram_tensor(f"in_{name}", a.shape, _mybir.dt.from_np(a.dtype), kind="ExternalInput").ap()
    result = nc.dram_tensor("result", (B, S, C), _mybir.dt.float32, kind="ExternalOutput").ap()
    cross_attention_block_kernel(nc, aps, result)
    r = _run(nc, [arrays], core_ids=[0])
    return r.results[0]["result"]
```

```python
import concourse.bass as bass
from concourse import mybir
from contextlib import ExitStack

B, S, C = 2, 512, 160
T, E = 154, 256
NIP = 4
TT = T - NIP
HEADS = 20
P = 128
QT = S // P
NT = B * QT
N = B * S
CT = C - P
KC = S // P
EC = E // P
D0 = C // HEADS
D1 = 64
PAIRS = HEADS // 2
G4 = HEADS // 4
FF = 4 * C
FCH = FF // P
TXTAIL = TT - P
TTAIL = T - P
PW = 160
RHS = TT + D0 + NIP
RHT = TXTAIL + D0 + NIP
ST = 2 + D0 + NIP + NIP
STEPS0 = B * G4
EPS_NORM = 1e-12
EPS_LN = 1e-5
TINY = 1e-30
SEM_SCALE = 0.5


def cross_attention_block_kernel(nc, A, out):
    F32, F32R = mybir.dt.float32, mybir.dt.float32r
    ALU = mybir.AluOpType
    ACT = mybir.ActivationFunctionType
    AX = mybir.AxisListType
    x, ctx_in = A["x"], A["ctx_2048"]

    with ExitStack() as stack:
        def sb(name, shape, dt=F32):
            return stack.enter_context(nc.sbuf_tensor(name, shape, dt))

        def sem(name):
            return stack.enter_context(nc.semaphore(name))

        bank01 = stack.enter_context(nc.psum_tensor("bank01", [P, 2, 512], F32))
        bank23 = stack.enter_context(nc.psum_tensor("bank23", [P, 2, 512], F32))
        bank45 = stack.enter_context(nc.psum_tensor("bank45", [P, 2, 512], F32))
        bank67 = stack.enter_context(nc.psum_tensor("bank67", [P, 2, 512], F32))
        bank = [t[:, k, :] for t in (bank01, bank23, bank45, bank67) for k in range(2)]

        ident = sb("ident", [P, P])
        X = sb("X", [P, NT, C])
        nTm, nTt = sb("nTm", [P, N]), sb("nTt", [3 * CT, N])
        var, root = sb("var", [P, NT]), sb("root", [P, NT])
        bn6, mv, rstd = sb("bn6", [P, NT, 6]), sb("mv", [P, NT, 2]), sb("rstd", [P, NT])
        gcol = sb("gcol", [P, 12])
        brow = sb("brow", [P, 4, C])
        b1col = sb("b1col", [P, 2 * FCH])
        smask = sb("smask", [P, QT])
        cm, ct = sb("cm", [P, B, E]), sb("ct", [TTAIL, B, E])
        cT = sb("cT", [P, EC, B, T])
        cT4 = sb("cT4", [P, EC, B, 4, 32])
        first = ExitStack()

        def sb0(name, shape, dt=F32):
            return first.enter_context(nc.sbuf_tensor(name, shape, dt))

        wq0, wq0t = sb0("wq0", [P, C]), sb0("wq0t", [CT, C])
        wkv0 = sb0("wkv0", [P, 4, EC, C])
        wo0, wo0t = sb0("wo0", [P, C]), sb0("wo0t", [CT, C])
        wqe, wqet = sb0("wqe", [P, HEADS, 32]), sb0("wqet", [CT, HEADS, 32])
        wke = sb0("wke", [P, 2, EC, HEADS, 32])
        ipn, ips, ipj = sb0("ipn", [B * NIP, E]), sb0("ips", [B * NIP, 4]), sb0("ipj", [B * NIP, E])
        ipR = sb0("ipR", [P, EC, B, HEADS, NIP])
        ipT = sb0("ipT", [P, EC, B * NIP])
        low_q, low_k = sb0("low_q", [P, 1]), sb0("low_k", [P, 1])
        sign_q, sign_k = sb0("sign_q", [P, 1]), sb0("sign_k", [P, 1])
        QT0 = sb0("QT0", [P, G4, N], F32R)
        KB0 = sb0("KB0", [P, G4, B, 4, T], F32R)
        hi0, tm0 = sb0("hi0", [P, 2, 512], F32R), sb0("tm0", [P, 2, 512])
        GV, GVt = sb0("GV", [P, B, HEADS, RHS]), sb0("GVt", [P, B, G4, 4, RHT])
        VB0 = sb0("VB0", [4 * HEADS, B, C])
        bmask = sb0("bmask", [4 * HEADS, C])
        qs0 = sb0("qs0", [P, B, G4, P], F32R)
        nmax0 = sb0("nmax0", [P, 5, 4])
        P0 = sb0("P0", [P, 5, 4, PW])
        P0t = sb0("P0t", [P, 2, 4, 32])
        PT0, PT0t = sb0("PT0", [P, 2, 4, P]), sb0("PT0t", [P, 2, P])
        den0 = sb0("den0", [P, B, HEADS])
        scl = sb0("scl", [P, 512])
        st0 = sb0("st0", [P, B, HEADS, ST])
        sta = sb0("sta", [P, NT, HEADS, ST])
        h1, h2, h3 = sb0("h1", [P, NT, HEADS]), sb0("h2", [P, NT, HEADS]), sb0("h3", [P, NT, HEADS])
        f1 = sb0("f1", [P, NT, HEADS, NIP])
        f2 = sb0("f2", [P, NT, HEADS, NIP])
        FT = sb0("FT", [4 * HEADS, N])
        TX = sb0("TX", [P, NT, HEADS, D0])
        OTm, OTt = sb0("OTm", [P, N]), sb0("OTt", [CT, N])
        first.close()

        XN, XN3 = sb("XN", [P, NT, C]), sb("XN3", [P, NT, 3, CT])
        nTh, nTl, nT3 = sb("nTh", [P, N], F32R), sb("nTl", [P, N], F32R), sb("nT3", [3 * CT, N], F32R)
        raw = {n: sb("raw_" + n, [P, P]) for n in ("q", "k", "v")}
        rawt = {n: sb("rawt_" + n, [P, P]) for n in ("q", "k", "v")}
        raw["o"] = sb("raw_o", [P, C])
        wh = {n: sb("wh_" + n, [P, P], F32R) for n in ("q", "k", "v")}
        wl = {n: sb("wl_" + n, [P, P], F32R) for n in ("q", "k", "v")}
        w3 = {n: sb("w3_" + n, [3 * CT, P], F32R) for n in ("q", "k", "v")}
        wo = sb("w_o", [P, C])
        nmax = sb("nmax", [P, 2, QT])
        den = sb("den", [P, B, QT, 2])
        rden = sb("rden", [P, B, QT, 2])
        rsp = sb("rsp", [P, QT, 2, D1])
        rbs = sb("rbs", [P, S])
        oT = sb("oT", [P, B, S])
        cwk, cwv = sb("cwk", [P, EC, P]), sb("cwv", [P, EC, P])
        q2H, q2L = sb("q2H", [P, B, S], F32R), sb("q2L", [P, B, S], F32R)
        k2H, k2L = sb("k2H", [P, B, 2, T], F32R), sb("k2L", [P, B, 2, T], F32R)
        vZ2, vZ2t = sb("vZ2", [P, B, 2, P]), sb("vZ2t", [P, B, 2, P])
        P2, P2t = sb("P2", [P, 2, 4, PW]), sb("P2t", [P, 2, 4, 32])
        P2T, P2Tt = sb("P2T", [P, 2, 4, P]), sb("P2Tt", [P, 2, P])
        nmax2 = sb("nmax2", [P, 2, 4])
        attn = ExitStack()

        def sba(name, shape, dt=F32R):
            return attn.enter_context(nc.sbuf_tensor(name, shape, dt))

        qS = sba("qS", [P, B, 2, S])
        kS = sba("kS", [P, B, 2, S])
        kL = sba("kL", [P, B, 2, S])
        vH = sba("vH", [P, B, 2, KC, P])
        vL = sba("vL", [P, B, 2, KC, P])
        pr = sba("pr", [P, 2, QT, S], F32)
        pH, pL = sba("pH", [P, 4, S]), sba("pL", [P, 4, S])
        attn.close()
        f1raw, f1rawt = sb("f1raw", [P, 2 * FF]), sb("f1rawt", [3 * CT, 2 * FF])
        f1h, f1l = sb("f1h", [P, 2 * FF], F32R), sb("f1l", [P, 2 * FF], F32R)
        f13 = sb("f13", [3 * CT, 2 * FF], F32R)
        f2w = sb("f2w", [P, FCH, C])
        gel, hid = sb("gel", [P, 2, N]), sb("hid", [P, 2, N])
        block = stack.enter_context(nc.Block())

        loaded_x, loaded_ctx = sem("loaded_x"), sem("loaded_ctx")
        loaded_w0, loaded_small = sem("loaded_w0"), sem("loaded_small")
        masks_ready = sem("masks_ready")
        spread_ready = sem("spread_ready")
        ip_ready = sem("ip_ready")
        stored = sem("stored")
        ps_ready = sem("ps_ready")
        by_act, by_dve = sem("by_act"), sem("by_dve")
        hi_ready = sem("hi_ready")
        dve_step = sem("dve_step")
        pool_step = sem("pool_step")
        pool_held = sem("pool_held")
        s_ipn = sem("s_ipn")
        square_ready, root_ready = sem("square_ready"), sem("root_ready")

        USES = [("cT0", "act"), ("cT1", "act"), ("ipT", "dve"),
                ("x_m0", "act"), ("x_m1", "act"), ("x_t0", "dve"), ("x_t1", "dve")]
        USES += [(f"K0_{g}", "dve") for g in range(G4)]
        USES += [(f"Q0_{g}_{h}", "dve") for g in range(G4) for h in range(B)]
        USES += [("GV_0", "act"), ("GV_1", "act"), ("GVt_0", "dve"), ("GVt_1", "dve"),
                 ("VB_0", "dve"), ("VB_1", "dve")]
        USES += [("F_0", "act"), ("F_1", "act"), ("O_m0", "act"), ("O_m1", "act"), ("O_t0", "act"),
                 ("O_t1", "act")] + [(f"out_{k}", "dve") for k in range(4)]
        for k in (1, 2, 3):
            USES += [(f"n{k}_{p}", "act") for p in ("m0", "t0", "m1", "t1")]
        index = {name: k for k, (name, _) in enumerate(USES)}
        count = {name: sum(e == eng for _, e in USES[:k + 1]) for k, (name, eng) in enumerate(USES)}

        def make(pe, name):
            k = index[name]
            if k >= 8:
                taken(pe, USES[k - 8][0])
            return bank[k % 8]

        def taken(eng, name):
            eng.wait_ge(by_act if USES[index[name]][1] == "act" else by_dve, count[name])

        def made(eng, name):
            eng.wait_ge(ps_ready, index[name] + 1)
            return bank[index[name] % 8]

        q0_ready, s0_ready, m0_ready = sem("q0_ready"), sem("s0_ready"), sem("m0_ready")
        p0_ready, p0t_ready, t0_ready, pt0_ready = sem("p0_ready"), sem("p0t_ready"), sem("t0_ready"), sem("pt0_ready")
        u0_ready, u0_taken, st0_saved = sem("u0_ready"), sem("u0_taken"), sem("st0_saved")
        f_ready, fe_ready, fn_ready = sem("f_ready"), sem("fe_ready"), sem("fn_ready")
        xn_ready, xn3_ready, bias_added = sem("xn_ready"), sem("xn3_ready"), sem("bias_added")
        nl_ready = sem("nl_ready")
        names = ("raw", "rawo", "w", "wv", "wo", "s", "m", "p", "pt", "t", "ph", "pd", "pv", "rden", "rsp", "o",
                 "kh", "kc", "qh", "vh", "misc6", "misc7", "taken6", "taken7")
        at = [{n: sem(f"{n}_{kind}") for n in names} for kind in ("self", "cross")]
        zeroed = sem("zeroed")
        ff_raw, ff_w, ff_g, ff_a, ff_gel, ff_hid = (sem(f"ff_{n}") for n in ("raw", "w", "g", "a", "gel", "hid"))
        ff_out, x_final = sem("ff_out"), sem("x_final")

        def reach(eng, sem_, n):
            if isinstance(n, int) and n <= 0:
                return
            eng.wait_ge(sem_, n)

        def sweep(eng, total, body):
            body(0)
            with eng.Fori(1, total - 1) as i:
                body(i)
            body(total - 1)

        def inside(i, k, per, total):
            return not isinstance(i, int) or 0 <= i * per + k < total

        UNITS = B * PAIRS
        MISC = [[("k", 1, 6), ("q", 1, 7), ("v", 1, 6), ("sums", -1, 7), ("outa", -1, 6), ("outb", -1, 7)],
                [("v", 1, 6), ("outa", -1, 7), ("outb", -1, 6), ("k", 2, 7), ("q", 2, 6), ("sums", 0, 7)]]

        def shared(a, i, v, kind):
            b6 = {n: bk for n, _, bk in MISC[a]}[kind]

            def exact(u):
                n = 0
                for w_ in range(-2, u + 1):
                    for name, rel, bk in MISC[a]:
                        if 0 <= w_ + rel < UNITS and bk == b6:
                            n += 1
                        if w_ == u and name == kind:
                            break
                return n
            if isinstance(i, int):
                return b6, exact(B * i + v)
            return b6, i * 6 + (exact(B * 2 + v) - 12)

        def use(pe, a, i, v, kind):
            bk, n = shared(a, i, v, kind)
            reach(pe, at[a][f"taken{bk}"], n - 1)
            return bank[bk]

        def finish(a, kind, ins):
            ins.then_inc(at[a][f"misc{ {n: bk for n, _, bk in MISC[a]}[kind] }"], 1)

        def arrived(eng, a, i, v, kind):
            bk, n = shared(a, i, v, kind)
            reach(eng, at[a][f"misc{bk}"], n)
            return bank[bk]

        def take(a, kind, ins):
            ins.then_inc(at[a][f"taken{ {n: bk for n, _, bk in MISC[a]}[kind] }"], 1)

        def gone(eng, a, i, v, kind):
            bk, n = shared(a, i, v, kind)
            reach(eng, at[a][f"taken{bk}"], n)

        W_IN = [("L0_xattn_W_k", 0), ("L0_xattn_W_k_ip", 1), ("L0_xattn_W_v", 2), ("L0_xattn_W_v_ip", 3)]
        SMALL = 3 * 2 * 4 + 4 + 2

        @block.sync
        def _(sp):
            for b in range(B):
                sp.dma_start(cm[:, b, :], ctx_in[b, 0:P, :]).then_inc(loaded_ctx, 16)
                sp.dma_start(ct[:, b, :], ctx_in[b, P:T, :]).then_inc(loaded_ctx, 16)
                sp.dma_start(ipn[b * NIP:(b + 1) * NIP, :], ctx_in[b, TT:T, :]).then_inc(loaded_ctx, 16)
            sp.dma_start(X[:, :, :], x.rearrange("b (t p) c -> p (b t) c", p=P)).then_inc(loaded_x, 16)
            for name, k in W_IN:
                sp.dma_start(wkv0[:, k, :, :], A[name].rearrange("(c p) n -> p c n", p=P)).then_inc(loaded_w0, 16)
            sp.dma_start(wq0[:, :], A["L0_xattn_W_q"][0:P, :]).then_inc(loaded_w0, 16)
            sp.dma_start(wq0t[:, :], A["L0_xattn_W_q"][P:C, :]).then_inc(loaded_w0, 16)
            sp.dma_start(wo0[:, :], A["L0_xattn_W_out"][0:P, :]).then_inc(loaded_w0, 16)
            sp.dma_start(wo0t[:, :], A["L0_xattn_W_out"][P:C, :]).then_inc(loaded_w0, 16)
            for k in range(3):
                for j, v in enumerate(("g", "b")):
                    col = A[f"L1_xattn_ln{k + 1}_{v}"].rearrange("(c a) -> c a", a=1)
                    sp.dma_start(gcol[:, 4 * k + j:4 * k + j + 1], col[0:P, :]).then_inc(loaded_small, 16)
                    for rep in range(3):
                        sp.dma_start(gcol[rep * CT:(rep + 1) * CT, 4 * k + 2 + j:4 * k + 3 + j], col[P:C, :])\
                            .then_inc(loaded_small, 16)
            for k, v in enumerate(("L0_xattn_b_out", "L1_xattn_a1_bo", "L1_xattn_a2_bo", "L1_xattn_ff_b2")):
                sp.dma_start(brow[:, k, :], A[v].rearrange("(a c) -> a c", a=1).broadcast_to([P, C]))\
                    .then_inc(loaded_small, 16)
            sp.dma_start(b1col[:, :], A["L1_xattn_ff_b1"].rearrange("(c p) -> p c", p=P),
                         allow_slow_non_contiguous=True).then_inc(loaded_small, 16)
            sp.dma_start(smask[:, :], A["fside_S_0"].rearrange("(t p) -> p t", p=P),
                         allow_slow_non_contiguous=True).then_inc(loaded_small, 16)
            taken(sp, "out_3")

            def load_pair(i, a):
                q, pre = at[a], ("a1", "a2")[a]
                if a == 0:
                    reach(sp, q["w"], i * 12)
                else:
                    reach(sp, q["wv"], i * 2)
                for n in ("q", "k", "v"):
                    src = A[f"L1_xattn_{pre}_w{n}"]
                    sp.dma_start(raw[n][:, :], src[0:P, bass.ds(i * P, P)]).then_inc(q["raw"], 16)
                    if src.shape[0] == E:
                        sp.dma_start(rawt[n][:, :], src[P:E, bass.ds(i * P, P)]).then_inc(q["raw"], 16)
                    else:
                        for k in range(3):
                            sp.dma_start(rawt[n][k * CT:(k + 1) * CT, :], src[P:C, bass.ds(i * P, P)])\
                                .then_inc(q["raw"], 16)
                reach(sp, q["wo"], i)
                sp.dma_start(raw["o"][:, :], A[f"L1_xattn_{pre}_wo"][bass.ds(i * P, P), :])\
                    .then_inc(q["rawo"], 16)

            sweep(sp, PAIRS, lambda i: load_pair(i, 0))
            sp.wait_ge(at[0]["w"], 12 * PAIRS)
            sp.wait_ge(at[0]["wo"], PAIRS)
            load_pair(0, 1)
            sp.wait_ge(xn_ready, 2)
            ff1 = A["L1_xattn_ff_w1"]
            sp.dma_start(f1raw[:, :], ff1[0:P, :]).then_inc(ff_raw, 16)
            for k in range(3):
                sp.dma_start(f1rawt[k * CT:(k + 1) * CT, :], ff1[P:C, :]).then_inc(ff_raw, 16)
            sp.dma_start(f2w[:, :, :], A["L1_xattn_ff_w2"].rearrange("(c p) n -> p c n", p=P)).then_inc(ff_raw, 16)
            with sp.Fori(1, PAIRS) as i:
                load_pair(i, 1)
            rows = out.rearrange("b (t p) c -> p (b t) c", p=P)
            for k, t in enumerate(range(0, NT, 3)):
                n = min(3, NT - t)
                sp.wait_ge(x_final, k + 1)
                sp.dma_start(rows[:, t:t + n, :], X[:, t:t + n, :]).then_inc(stored, 16)
            sp.wait_ge(stored, 16 * 3)

        @block.gpsimd
        def _(pool):
            steps = 0

            def hold(sem_, value):
                if isinstance(value, int) and value <= 0:
                    return
                pool.wait_ge(sem_, value)
                pool.sem_inc(pool_held, 1)

            def link(ins):
                nonlocal steps
                steps += 1
                ins.then_inc(pool_step, 1)
                pool.wait_ge(pool_step, steps)

            pool.memset(ident[:, :], 0.0).then_inc(pool_step, 1)
            pool.memset(bmask[:, :], 1.0).then_inc(pool_step, 1)
            pool.memset(KB0[:, :, :, :, :].bitcast(F32), 0.0).then_inc(pool_step, 1)
            pool.memset(GVt[:, :, :, :, :], 0.0).then_inc(pool_step, 1)
            pool.memset(P0[:, :, :, TT:PW], 0.0).then_inc(pool_step, 1)
            pool.memset(cT4[:, :, :, :, :], 0.0).then_inc(pool_step, 1)
            pool.memset(wqe[:, :, :], 0.0).then_inc(pool_step, 1)
            pool.memset(wqet[:, :, :], 0.0).then_inc(pool_step, 1)
            pool.memset(wke[:, :, :, :, :], 0.0).then_inc(pool_step, 1)
            steps += 9
            pool.wait_ge(pool_step, steps)
            link(pool.affine_select(out=ident[:, :], in_=ident[:, :], compare_op=ALU.not_equal, fill=1.0,
                                    base=0, pattern=[[-1, P]], channel_multiplier=1))
            bm = bmask[:, :].rearrange("p (h d) -> p h d", d=D0)
            link(pool.affine_select(out=bm, in_=bm, compare_op=ALU.is_ge, fill=0.0, base=0,
                                    pattern=[[-NIP, HEADS], [0, D0]], channel_multiplier=1))
            pool.affine_select(out=bm, in_=bm, compare_op=ALU.is_ge, fill=0.0, base=NIP - 1,
                               pattern=[[NIP, HEADS], [0, D0]], channel_multiplier=-1).then_inc(masks_ready, 1)
            pool.wait_ge(loaded_w0, 16 * 8)
            for dst, src in [(wqe[:, :, 0:24], wq0[:, :]), (wqet[:, :, 0:24], wq0t[:, :])] + [
                    (wke[:, k, c, :, 0:24], wkv0[:, k, c, :]) for k in range(2) for c in range(EC)]:
                rows = src.shape[0]
                pool.tensor_copy(dst.rearrange("p h (r d) -> p h r d", r=3),
                                 src.rearrange("p (h r d) -> p h r d", r=1, d=D0)
                                 .broadcast_to([rows, HEADS, 3, D0])).then_inc(spread_ready, 1)
            taken(pool, "cT1")
            for c in range(EC):
                pool.tensor_copy(ipR[:, c, :, :, :], cT[:, c, :, TT:T].rearrange("p b (h n) -> p b h n", h=1)
                                 .broadcast_to([P, B, HEADS, NIP])).then_inc(ip_ready, 1)
            for c in range(EC):
                for b in range(B):
                    pool.tensor_copy(cT4[:, c, b, :, 0:TTAIL],
                                     cT[:, c, b, P:T].rearrange("p (j n) -> p j n", j=1)
                                     .broadcast_to([P, 4, TTAIL])).then_inc(ip_ready, 1)
            def queries0(i, n):
                if inside(i, 0, 1, QT):
                    if not isinstance(i, int) or i > 0:
                        hold(s0_ready, (i - 1) * STEPS0 + n + 1)
                    b, g = n // G4, n % G4
                    pool.tensor_copy(qs0[:, b, g, :], QT0[:, g, bass.ds(i * P + b * S, P)]).then_inc(q0_ready, 1)

            def tails0(i, k):
                if inside(i, k, STEPS0, QT * STEPS0):
                    hold(p0_ready, i * STEPS0 + k + 1)
                    hold(t0_ready, i * STEPS0 + k - 1)
                    pool.tensor_copy(P0t[:, k % 2, :, :], P0[:, k % STEPS0 % 5, :, P:PW]).then_inc(p0t_ready, 1)

            def save0(i, b):
                if inside(i, 0, 1, QT):
                    hold(u0_taken, i * 2 * STEPS0 + 2 * (b + 1) * G4)
                    t = bass.ds(i + b * QT, 1)
                    pool.tensor_copy(sta[:, t, :, 0:1], st0[:, b:b + 1, :, 0:1]).then_inc(st0_saved, 1)
                    pool.tensor_copy(sta[:, t, :, 1:2], den0[:, b:b + 1, :].rearrange("p b (h o) -> p b h o", o=1))\
                        .then_inc(st0_saved, 1)
                    pool.tensor_copy(sta[:, t, :, 2:ST], st0[:, b:b + 1, :, 2:ST]).then_inc(st0_saved, 1)

            def first_block(i):
                for k in range(STEPS0):
                    tails0(i, k + 2)
                    if k == 0:
                        save0(i - 1, 1)
                    if k == 5:
                        save0(i, 0)
                    queries0(i + 1, k)

            taken(pool, f"Q0_{G4 - 1}_{B - 1}")
            for n in range(STEPS0):
                queries0(0, n)
            tails0(0, 0)
            tails0(0, 1)
            sweep(pool, QT, first_block)
            save0(QT - 1, 1)
            pool.wait_ge(loaded_small, 16 * SMALL)
            taken(pool, "x_t1")
            pool.tensor_tensor(X[:, :, :], X[:, :, :], brow[:, 0:1, :].broadcast_to([P, NT, C]), ALU.add)\
                .then_inc(bias_added, 1)
            taken(pool, "out_3")
            for t in (kL[:, :, :, :].bitcast(F32), vH[:, :, :, :, :].bitcast(F32), vL[:, :, :, :, :].bitcast(F32),
                      k2H[:, :, :, :].bitcast(F32), k2L[:, :, :, :].bitcast(F32), vZ2[:, :, :, :],
                      vZ2t[:, :, :, :], P2[:, :, :, T:PW]):
                pool.memset(t, 0.0).then_inc(zeroed, 1)

            def after_norm(k):
                pool.wait_ge(xn_ready, k + 1)
                pool.tensor_copy(XN3[:, :, :, :], XN[:, :, P:C].rearrange("p t (o c) -> p t o c", o=1)
                                 .broadcast_to([P, NT, 3, CT])).then_inc(xn3_ready, 1)
                pool.tensor_tensor(X[:, :, :], X[:, :, :], brow[:, k + 1:k + 2, :].broadcast_to([P, NT, C]),
                                   ALU.add).then_inc(bias_added, 1)

            def split_weights(names, q, before):
                for n in names:
                    pool.tensor_copy(wh[n][:, :], raw[n][:, :]).then_inc(q["w"], 1)
                    pool.tensor_copy(w3[n][:, :], rawt[n][0:3 * CT, :]).then_inc(q["w"], 1)
                hold(q["w"], before + 2 * len(names))
                for n in names:
                    pool.tensor_tensor(wl[n][:, :], raw[n][:, :], wh[n][:, :].bitcast(F32), ALU.subtract)\
                        .then_inc(q["w"], 1)
                    r = slice(0, CT)
                    pool.tensor_tensor(w3[n][r, :], rawt[n][r, :], w3[n][r, :].bitcast(F32), ALU.subtract)\
                        .then_inc(q["w"], 1)

            def spread(a, i, b):
                q = at[a]
                if not inside(i, 0, 1, PAIRS):
                    return
                hold(q["rden"], i * B + b + 1)
                if not (isinstance(i, int) and i * B + b == 0):
                    bk, n = shared(a, i, b + (0 if a == 0 else -1), "sums")
                    hold(q[f"misc{bk}"], n)
                pool.tensor_copy(rsp[:, :, :, :], rden[:, b, :, :].rearrange("p t (h o) -> p t h o", o=1)
                                 .broadcast_to([P, QT, 2, D1])).then_inc(q["rsp"], 1)

            q = at[0]
            after_norm(0)

            def weights1(i):
                if inside(i, 0, 1, PAIRS):
                    hold(q["raw"], i * 192 + 192)
                    if not isinstance(i, int) or i > 0:
                        bk, n = shared(0, i - 1, 0, "v")
                        hold(q[f"misc{bk}"], n)
                    split_weights(("q", "k", "v"), q, i * 12)

            def copy_keys(i, v):
                if not inside(i, v, B, UNITS):
                    return
                hold(q["rsp"], i * B + v - 1)
                hold(q["w"], 12 if v == 0 else 0)
                i, b = (i + 1, 0) if v == 2 else (i, v)
                hold(q["kh"], i * B + b + 1)
                pool.tensor_copy(kS[64:P, b, 0, :], kS[0:64, b, 0, :]).then_inc(q["kc"], 1)
                hold(q["kc"], i * 4 + 2 * b + 1)
                pool.tensor_copy(kS[0:64, b, 1, :], kS[64:P, b, 1, :]).then_inc(q["kc"], 1)
                hold(q["kc"], i * 4 + 2 * b + 2)

            def self_attention(i):
                copy_keys(i, 1)
                weights1(i + 1)
                spread(0, i, 0)
                copy_keys(i, 2)
                spread(0, i, 1)

            weights1(0)
            copy_keys(0, 0)
            sweep(pool, PAIRS, self_attention)

            after_norm(1)
            r = at[1]

            def weights2(i):
                if inside(i, 0, 1, PAIRS):
                    hold(r["raw"], i * 128 + 128)
                    if not isinstance(i, int) or i > 0:
                        for kind in ("k", "q"):
                            bk, n = shared(1, i - 1, -1, kind)
                            hold(r[f"misc{bk}"], n)
                    for c, src in enumerate((raw, rawt)):
                        pool.tensor_copy(cwk[:, c, :], src["k"][:, :]).then_inc(r["w"], 1)
                    split_weights(("q",), r, i * 6 + 2)

            def value_weights2(i):
                if inside(i, 0, 1, PAIRS):
                    hold(r["raw"], i * 128 + 128)
                    if not isinstance(i, int) or i > 0:
                        bk, n = shared(1, i - 1, 0, "v")
                        hold(r[f"misc{bk}"], n)
                    for c, src in enumerate((raw, rawt)):
                        pool.tensor_copy(cwv[:, c, :], src["v"][:, :]).then_inc(r["wv"], 1)

            def tails2(i, k):
                if inside(i, k, 4, 4 * PAIRS):
                    hold(r["p"], i * 8 + 2 * k + 2)
                    hold(r["t"], i * 4 + k - 1)
                    pool.tensor_copy(P2t[:, k % 2, :, :], P2[:, k % 2, :, P:PW]).then_inc(r["pt"], 1)

            def ff_weights(i, n):
                if not isinstance(i, int) or i < PAIRS - 1:
                    return
                pool.wait_ge(ff_raw, 16 * 5)
                if n == 0:
                    pool.tensor_copy(f13[:, :], f1rawt[:, :]).then_inc(ff_w, 1)
                elif n == 1:
                    pool.tensor_copy(f1h[:, :], f1raw[:, :]).then_inc(ff_w, 1)
                elif n == 2:
                    pool.wait_ge(ff_w, 2)
                    low = slice(0, CT)
                    pool.tensor_tensor(f13[low, :], f1rawt[low, :], f13[low, :].bitcast(F32), ALU.subtract)\
                        .then_inc(ff_w, 1)
                else:
                    pool.tensor_tensor(f1l[:, :], f1raw[:, :], f1h[:, :].bitcast(F32), ALU.subtract)\
                        .then_inc(ff_w, 1)

            def cross_attention(i):
                weights2(i + 1)
                spread(1, i, 0)
                tails2(i, 2)
                ff_weights(i, 0)
                value_weights2(i + 1)
                tails2(i, 3)
                ff_weights(i, 1)
                spread(1, i, 1)
                ff_weights(i, 2)
                ff_weights(i, 3)
                tails2(i, 4)
                tails2(i, 5)

            weights2(0)
            value_weights2(0)
            tails2(0, 0)
            tails2(0, 1)
            sweep(pool, PAIRS, cross_attention)
            after_norm(2)

        @block.scalar
        def _(act):
            def copy(out_, in_, **kw):
                return act.activation(out_, in_, ACT.Copy, **kw)

            act.wait_ge(square_ready, 1)
            act.activation(ips[:, 3:4], ips[:, 1:2], ACT.Sqrt).then_inc(root_ready, 1)
            for c in range(EC):
                copy(cT[:, c, :, :], made(act, f"cT{c}")[:, 0:B * T].rearrange("p (b t) -> p b t", b=B))\
                    .then_inc(by_act, 1)
            for h in range(B):
                copy(nTm[:, h * S:(h + 1) * S], made(act, f"x_m{h}")).then_inc(by_act, 1)
            for n, (name, _) in enumerate([u for u in USES if u[0][:3] in ("K0_", "Q0_")]):
                if n >= 2:
                    taken(act, [u[0] for u in USES if u[0][:3] in ("K0_", "Q0_")][n - 2])
                cols = B * T if name[0] == "K" else 512
                copy(hi0[:, n % 2, 0:cols], made(act, name)[:, 0:cols],
                     scale=1.0 if name[0] == "K" else D0 ** -0.5).then_inc(hi_ready, 1)
            for b in range(B):
                ps = made(act, f"GV_{b}")
                copy(GV[:, b, :, 0:P], ps[:, 0:P].rearrange("p (h t) -> p h t", h=1).broadcast_to([P, HEADS, P]))
                copy(GV[:, b, :, P:TT], ps[:, P:TT].rearrange("p (h t) -> p h t", h=1)
                     .broadcast_to([P, HEADS, TXTAIL]), scale=2.0)
                copy(GV[:, b, :, TT:TT + D0], ps[:, TT:TT + C].rearrange("p (h d) -> p h d", d=D0))
                copy(GV[:, b, :, TT + D0:RHS], ps[:, TT + C:TT + C + NIP].rearrange("p (h n) -> p h n", h=1)
                     .broadcast_to([P, HEADS, NIP])).then_inc(by_act, 1)

            def exps0(i, k):
                if not inside(i, k, STEPS0, QT * STEPS0):
                    return
                v, g = k // G4, k % G4
                reach(act, m0_ready, i * STEPS0 + k + 1)
                reach(act, u0_taken, i * 2 * STEPS0 + 2 * k - 8)
                if g == 0:
                    reach(act, st0_saved, i * 6 + 3 * v - 3)
                for j in range(4):
                    ins = act.activation(P0[:, k % 5, j, 0:TT],
                                         (bank01, bank23)[k % 2][:, j // 2, j % 2 * T:j % 2 * T + TT],
                                         ACT.Exp, bias=nmax0[:, k % 5, j:j + 1],
                                         accum_out=den0[:, v % B, 4 * g + j:4 * g + j + 1])
                ins.then_inc(p0_ready, 1)

            def evac0(i, k):
                if not inside(i, k, STEPS0, QT * STEPS0):
                    return
                reach(act, t0_ready, i * STEPS0 + k + 1)
                reach(act, u0_ready, i * 2 * STEPS0 + 2 * k - 2)
                copy(PT0[:, k % 2, :, :], bank45[:, 0, :].rearrange("p (j s) -> p j s", j=4))
                copy(PT0t[:, k % 2, :], bank45[:, 1, 0:P]).then_inc(pt0_ready, 1)

            def first_block(i):
                for k in range(STEPS0):
                    exps0(i, k + 2)
                    evac0(i, k + 1)

            exps0(0, 0)
            exps0(0, 1)
            evac0(0, 0)
            sweep(act, QT, first_block)
            act.wait_ge(square_ready, 2)
            act.activation(h1[:, :, :], h3[:, :, :], ACT.Sqrt).then_inc(root_ready, 1)
            act.wait_ge(f_ready, 1)
            act.activation(f2[:, :, :, :], f1[:, :, :, :], ACT.Exp).then_inc(fe_ready, 1)
            for h in range(B):
                copy(FT[:, h * S:(h + 1) * S], made(act, f"F_{h}")[0:4 * HEADS, :]).then_inc(by_act, 1)
            for h in range(B):
                copy(OTm[:, h * S:(h + 1) * S], made(act, f"O_m{h}")).then_inc(by_act, 1)
            for h in range(B):
                copy(OTt[:, h * S:(h + 1) * S], made(act, f"O_t{h}")[0:CT, :]).then_inc(by_act, 1)

            def norm_out(n):
                act.wait_ge(square_ready, n + 2)
                act.activation(root[:, :], var[:, :], ACT.Sqrt).then_inc(root_ready, 1)
                if n == 1:
                    act.wait_ge(loaded_small, 16 * SMALL)
                o = 4 * (n - 1)
                for b in range(B):
                    cols = slice(b * S, (b + 1) * S)
                    for part, full, high, rows, c in (("m", nTm, nTh, P, o), ("t", nTt, nT3, 3 * CT, o + 2)):
                        ps = made(act, f"n{n}_{part}{b}")
                        for dst in (full, high):
                            ins = act.activation(dst[0:rows, cols], ps[0:rows, :], ACT.Identity,
                                                 scale=gcol[0:rows, c:c + 1], bias=gcol[0:rows, c + 1:c + 2])
                        ins.then_inc(by_act, 1)

            def out_weights(a, i, v):
                q = at[a]
                reach(act, q["rawo"], i * 16 + 16)
                if not isinstance(i, int) or i > 0:
                    arrived(act, a, i, v, "outb")
                copy(wo[:, :], raw["o"][:, :]).then_inc(q["wo"], 1)

            def spread_sums(a, i, v):
                unit = i * B + v + (0 if a == 1 else -1)
                ps = arrived(act, a, i, v, "sums")
                reach(act, at[a]["o"], unit)
                take(a, "sums", copy(rbs[:, :], ps))

            norm_out(1)
            q = at[0]

            def high1(i, v, kind):
                if not inside(i, v + 1, B, UNITS):
                    return
                b = (v + 1) % B
                ps = arrived(act, 0, i, v, kind)
                if kind == "k":
                    copy(kS[0:64, b, 0, :], ps[0:64, :])
                    copy(kS[64:P, b, 1, :], ps[64:P, :]).then_inc(q["kh"], 1)
                elif kind == "q":
                    copy(qS[0:64, b, 0, :], ps[0:64, :], scale=D1 ** -0.5)
                    copy(qS[64:P, b, 1, :], ps[64:P, :], scale=D1 ** -0.5).then_inc(q["qh"], 1)
                else:
                    reach(act, q["pv"], i * 16 + 8 * v)
                    ps = ps.rearrange("p (k d) -> p k d", k=KC)
                    copy(vH[:, b, 0, :, 0:64], ps[:, :, 0:64])
                    copy(vH[:, b, 1, :, 64:P], ps[:, :, 64:P]).then_inc(q["vh"], 1)

            def exp1(i, k):
                if not inside(i, k, 16, 16 * PAIRS):
                    return
                reach(act, q["m"], i * 16 + k + 1)
                if k % 4 == 0:
                    reach(act, q["t"], i * 16 + k - 4)
                if k % 8 == 0:
                    reach(act, q["rden"], i * B + k // 8 - 1)
                act.activation(pr[:, k // 4 % 2, k % 4, :], bank[k % 2], ACT.Exp,
                               bias=nmax[:, k // 4 % 2, k % 4:k % 4 + 1],
                               accum_out=den[:, k // 8 % B, k % 4, k // 4 % 2:k // 4 % 2 + 1]).then_inc(q["p"], 1)

            def high_p(i, k):
                reach(act, q["t"], i * 16 + k + 1)
                reach(act, q["pv"], i * 16 + k - 3)
                copy(pH[:, k % 4, :], bank[2 + k % 2]).then_inc(q["ph"], 1)

            def self_attention(i):
                for k in range(16):
                    v, step = k // 8, k % 8
                    high_p(i, k)
                    if step < 3:
                        high1(i, v, ("k", "q", "v")[step])
                    if step == 2 and v == 1:
                        out_weights(0, i, 0)
                    if step == 3 and inside(i, v - 1, B, UNITS):
                        spread_sums(0, i, v)
                    exp1(i, k + 5)

            high1(0, -1, "k")
            high1(0, -1, "q")
            exp1(0, 0)
            exp1(0, 1)
            high1(0, -1, "v")
            for k in range(2, 5):
                exp1(0, k)
            sweep(act, PAIRS, self_attention)
            spread_sums(0, PAIRS, 0)

            norm_out(2)
            r = at[1]

            def exps2(i, k):
                if not inside(i, k, 4, 4 * PAIRS):
                    return
                half = k % 2
                reach(act, r["t"], i * 4 + k - 1)
                if half == 0:
                    reach(act, r["rden"], i * B + k // 2 - 1)
                for j in range(2):
                    reach(act, r["m"], i * 8 + 2 * k + j + 1)
                    for h in range(2):
                        ins = act.activation(P2[:, k % 2, 2 * j + h, 0:T], bank[j][:, h * T:(h + 1) * T],
                                             ACT.Exp, bias=nmax2[:, k % 2, 2 * j + h:2 * j + h + 1],
                                             accum_out=den[:, k // 2 % B, 2 * half + j, h:h + 1])
                    ins.then_inc(r["p"], 1)

            def high2(i, v, kind):
                if not inside(i, v + 2, B, UNITS):
                    return
                b = v % B
                ps = arrived(act, 1, i, v, kind)
                if kind == "k":
                    copy(k2H[0:64, b, 0, :], ps[0:64, 0:T])
                    copy(k2H[64:P, b, 1, :], ps[64:P, 0:T]).then_inc(r["kh"], 1)
                else:
                    copy(q2H[:, b, :], ps, scale=D1 ** -0.5).then_inc(r["qh"], 1)

            def cross_attention(i):
                for k in range(4):
                    exps2(i, k + 2)
                    if k % 2:
                        high2(i, k // 2, "k")
                        high2(i, k // 2, "q")
                        if k == 1:
                            out_weights(1, i, 0)
                        spread_sums(1, i, k // 2)

            high2(0, -2, "k")
            high2(0, -2, "q")
            exps2(0, 0)
            high2(0, -1, "k")
            high2(0, -1, "q")
            exps2(0, 1)
            sweep(act, PAIRS, cross_attention)

            norm_out(3)
            for c in range(FCH):
                for h in range(B):
                    reach(act, ff_g, c * B + h + 1)
                    reach(act, ff_hid, (c - 2) * B + h + 1)
                    act.activation(gel[:, c % 2, h * S:(h + 1) * S], bank[2 + h], ACT.Gelu,
                                   bias=b1col[:, FCH + c:FCH + c + 1]).then_inc(ff_gel, 1)

        @block.vector
        def _(dve):
            steps = 0

            def link(ins):
                nonlocal steps
                steps += 1
                ins.then_inc(dve_step, 1)
                dve.wait_ge(dve_step, steps)

            dve.wait_ge(loaded_ctx, 96)
            link(dve.tensor_tensor_reduce(out=ipj[:, :], in0=ipn[:, :], in1=ipn[:, :], scale=1.0, scalar=0.0,
                                          op0=ALU.mult, op1=ALU.add, accum_out=ips[:, 0:1]))
            dve.tensor_scalar(ips[:, 1:2], ips[:, 0:1], TINY, None, ALU.max).then_inc(square_ready, 1)
            dve.wait_ge(root_ready, 1)
            link(dve.tensor_scalar(ips[:, 1:2], ips[:, 3:4], EPS_NORM, None, ALU.max))
            link(dve.reciprocal(ips[:, 2:3], ips[:, 1:2]))
            dve.tensor_scalar(ipj[:, :], ipn[:, :], ips[:, 2:3], None, ALU.mult).then_inc(s_ipn, 1)
            dve.wait_ge(masks_ready, 1)
            heads = ident[:, :].rearrange("p (j r) -> p j r", j=4)
            link(dve.tensor_reduce(low_q[:, :], heads[:, :, 16:24], AX.XY, ALU.add))
            link(dve.tensor_reduce(low_k[:, :], heads[:, :, 8:16], AX.XY, ALU.add))
            link(dve.tensor_scalar(sign_q[:, :], low_q[:, :], -2.0, 1.0, ALU.mult, ALU.add))
            link(dve.tensor_scalar(sign_k[:, :], low_k[:, :], -2.0, 1.0, ALU.mult, ALU.add))
            dve.tensor_copy(ipT[:, :, :], made(dve, "ipT")[:, 0:EC * B * NIP].rearrange("p (c n) -> p c n", c=EC))\
                .then_inc(by_dve, 1)
            for h in range(B):
                dve.tensor_copy(nTt[0:CT, h * S:(h + 1) * S], made(dve, f"x_t{h}")[0:CT, :]).then_inc(by_dve, 1)
            for n, (name, _) in enumerate([u for u in USES if u[0][:3] in ("K0_", "Q0_")]):
                ps = made(dve, name)
                dve.wait_ge(hi_ready, n + 1)
                g = int(name.split("_")[1])
                if name[0] == "K":
                    link(dve.tensor_scalar(tm0[:, n % 2, 0:B * T], hi0[:, n % 2, 0:B * T].bitcast(F32),
                                           sign_k[:, 0:1], None, ALU.mult))
                    for j in range(4):
                        r = slice(32 * j, 32 * j + 32)
                        ins = dve.scalar_tensor_tensor(
                            out=KB0[r, g, :, j, :], in0=ps[r, 0:B * T].rearrange("p (b t) -> p b t", b=B),
                            scalar=low_k[r, 0:1], in1=tm0[r, n % 2, 0:B * T].rearrange("p (b t) -> p b t", b=B),
                            op0=ALU.mult, op1=ALU.add)
                    ins.then_inc(by_dve, 1)
                else:
                    h = int(name.split("_")[2])
                    link(dve.tensor_scalar(tm0[:, n % 2, :], hi0[:, n % 2, :].bitcast(F32), sign_q[:, 0:1], None,
                                           ALU.mult))
                    link(dve.tensor_scalar(scl[:, :], ps, D0 ** -0.5, low_q[:, 0:1], ALU.mult, ALU.mult))
                    dve.tensor_tensor(QT0[:, g, h * S:(h + 1) * S], scl[:, :], tm0[:, n % 2, :], ALU.add)\
                        .then_inc(by_dve, 1)
            for b in range(B):
                ps = made(dve, f"GVt_{b}")
                for j in range(4):
                    r = slice(32 * j, 32 * j + 32)
                    dve.tensor_copy(GVt[r, b, :, j, 0:TXTAIL], ps[r, 0:TXTAIL].rearrange("p (g t) -> p g t", g=1)
                                    .broadcast_to([32, G4, TXTAIL]))
                    dve.tensor_copy(GVt[r, b, :, j, TXTAIL:TXTAIL + D0],
                                    ps[r, TXTAIL:TXTAIL + C].rearrange("p (g j d) -> p g j d", j=4, d=D0)[:, :, j, :])
                    ins = dve.tensor_copy(GVt[r, b, :, j, TXTAIL + D0:RHT],
                                          ps[r, TXTAIL + C:TXTAIL + C + NIP].rearrange("p (g n) -> p g n", g=1)
                                          .broadcast_to([32, G4, NIP]))
                ins.then_inc(by_dve, 1)
            for b in range(B):
                dve.tensor_tensor(VB0[:, b, :], made(dve, f"VB_{b}")[0:4 * HEADS, 0:C], bmask[:, :], ALU.mult)\
                    .then_inc(by_dve, 1)

            def max0(i, k):
                if not inside(i, k, STEPS0, QT * STEPS0):
                    return
                v, g = k // G4, k % G4
                sc = (bank01, bank23)[k % 2][:, :, 0:2 * T].rearrange("p k (j t) -> p k j t", j=2)
                reach(dve, s0_ready, i * STEPS0 + k + 1)
                if g == 0:
                    reach(dve, st0_saved, i * 6 + 3 * v - 3)
                dve.tensor_reduce(nmax0[:, k % 5, :].rearrange("p (k j) -> p k j", k=2), sc[:, :, :, 0:TT], AX.X,
                                  ALU.max, negate=True)
                dve.tensor_copy(st0[:, v % B, 4 * g:4 * g + 4, 2 + D0 + NIP:ST].rearrange("p (k j) n -> p k j n", k=2),
                                sc[:, :, :, TT:T]).then_inc(m0_ready, 1)

            def norms0(i, k):
                b, g = k // G4, k % G4
                for j in range(4):
                    if j % 2 == 0:
                        reach(dve, u0_ready, i * 2 * STEPS0 + 2 * k + j // 2 + 1)
                    u = bank67[:, j // 2, j % 2 * RHS:j % 2 * RHS + RHS]
                    dve.tensor_tensor_reduce(out=P0[:, k % 5, j, 0:TT], in0=u[:, 0:TT], in1=P0[:, k % 5, j, 0:TT],
                                             scale=1.0, scalar=0.0, op0=ALU.mult, op1=ALU.add,
                                             accum_out=st0[:, b, 4 * g + j, 0:1])
                    if j % 2:
                        h = 4 * g + j - 1
                        dve.tensor_copy(st0[:, b, h:h + 2, 2:2 + D0 + NIP],
                                        bank67[:, j // 2, 0:2 * RHS].rearrange("p (j t) -> p j t", j=2)[:, :, TT:RHS])\
                            .then_inc(u0_taken, 1)

            def first_block(i):
                for k in range(STEPS0):
                    max0(i, k + 3)
                    norms0(i, k)

            max0(0, 0)
            max0(0, 1)
            max0(0, 2)
            sweep(dve, QT, first_block)
            reach(dve, st0_saved, 6 * QT)
            sq, sums = sta[:, :, :, 0], sta[:, :, :, 1]
            text, dots, simg = sta[:, :, :, 2:2 + D0], sta[:, :, :, 2 + D0:2 + D0 + NIP], sta[:, :, :, 2 + D0 + NIP:ST]

            def wide(t, n):
                return t[:, :, :].rearrange("p t (h o) -> p t h o", o=1).broadcast_to([P, NT, HEADS, n])

            dve.tensor_scalar(h3[:, :, :], sq, TINY, None, ALU.max).then_inc(square_ready, 1)
            dve.wait_ge(root_ready, 2)
            link(dve.scalar_tensor_tensor(out=h2[:, :, :], in0=sums, scalar=EPS_NORM, in1=h1[:, :, :],
                                          op0=ALU.mult, op1=ALU.max))
            link(dve.reciprocal(h1[:, :, :], h2[:, :, :]))
            link(dve.tensor_tensor(f1[:, :, :, :], dots, wide(h1, NIP), ALU.mult))
            link(dve.scalar_tensor_tensor(out=f2[:, :, :, :], in0=f1[:, :, :, :], scalar=SEM_SCALE, in1=simg,
                                          op0=ALU.mult, op1=ALU.add))
            link(dve.tensor_reduce(h2[:, :, :], f2[:, :, :, :], AX.X, ALU.max))
            dve.tensor_tensor(f1[:, :, :, :], f2[:, :, :, :], wide(h2, NIP), ALU.subtract).then_inc(f_ready, 1)
            link(dve.reciprocal(h3[:, :, :], sums))
            dve.tensor_tensor(TX[:, :, :, :], text, wide(h3, D0), ALU.mult).then_inc(dve_step, 1)
            steps += 1
            dve.wait_ge(fe_ready, 1)
            link(dve.tensor_reduce(h1[:, :, :], f2[:, :, :, :], AX.X, ALU.add))
            link(dve.reciprocal(h2[:, :, :], h1[:, :, :]))
            dve.wait_ge(loaded_small, 16 * SMALL)
            for b in range(B):
                ins = dve.tensor_tensor(h3[:, b * QT:(b + 1) * QT, :], h2[:, b * QT:(b + 1) * QT, :],
                                        smask[:, :].rearrange("p (t o) -> p t o", o=1).broadcast_to([P, QT, HEADS]),
                                        ALU.mult)
            link(ins)
            dve.tensor_tensor(f1[:, :, :, :], f2[:, :, :, :], wide(h3, NIP), ALU.mult).then_inc(fn_ready, 1)
            dve.wait_ge(bias_added, 1)
            for k in range(4):
                dve.tensor_tensor(X[:, 2 * k:2 * k + 2, :], X[:, 2 * k:2 * k + 2, :],
                                  made(dve, f"out_{k}")[:, 0:2 * C].rearrange("p (t c) -> p t c", t=2), ALU.add)\
                    .then_inc(by_dve, 1)
            dve.wait_ge(by_dve, sum(e == "dve" for _, e in USES))

            norms = 0

            def norm():
                nonlocal steps, norms
                for t in range(NT):
                    dve.bn_stats(bn6[:, t, :], X[:, t, :]).then_inc(dve_step, 1)
                for t in range(NT):
                    dve.wait_ge(dve_step, steps + t + 1)
                    dve.bn_aggr(mv[:, t, :], bn6[:, t, :]).then_inc(dve_step, 1)
                steps += 2 * NT
                dve.wait_ge(dve_step, steps)
                dve.tensor_scalar(var[:, :], mv[:, :, 1], EPS_LN, None, ALU.add).then_inc(square_ready, 1)
                norms += 1
                dve.wait_ge(root_ready, 2 + norms)
                link(dve.reciprocal(rstd[:, :], root[:, :]))
                for t in range(NT):
                    ins = dve.tensor_scalar(XN[:, t, :], X[:, t, :], mv[:, t, 0:1], rstd[:, t:t + 1],
                                            ALU.subtract, ALU.mult)
                ins.then_inc(xn_ready, 1)
                low = slice(2 * CT, 3 * CT)
                for b in range(B):
                    cols = slice(b * S, (b + 1) * S)
                    taken(dve, f"n{norms}_m{b}")
                    dve.tensor_tensor(nTl[:, cols], nTm[:, cols], nTh[:, cols].bitcast(F32), ALU.subtract)\
                        .then_inc(nl_ready, 1)
                    taken(dve, f"n{norms}_t{b}")
                    dve.tensor_tensor(nT3[low, cols], nTt[low, cols], nT3[low, cols].bitcast(F32), ALU.subtract)\
                        .then_inc(nl_ready, 1)

            def add_out(a, i, v, half):
                kind = ("outa", "outb")[half]
                if not inside(i, v - 1, B, UNITS):
                    return
                t = (v - 1) % B * QT + 2 * half
                take(a, kind, dve.tensor_tensor(X[:, t:t + 2, :], X[:, t:t + 2, :],
                                                arrived(dve, a, i, v, kind)[:, 0:2 * C]
                                                .rearrange("p (t c) -> p t c", t=2), ALU.add))

            def inverse_sums(a, i, v):
                q = at[a]
                per = 16 if a == 0 else 8
                reach(dve, q["p"], i * per + per // 2 * (v + 1))
                reach(dve, q["rsp"], i * B + v - 1)
                dve.reciprocal(rden[:, v, :, :], den[:, v, :, :]).then_inc(q["rden"], 1)

            norm()
            dve.wait_ge(bias_added, 2)
            dve.wait_ge(zeroed, 8)
            q = at[0]

            def low1(i, v, kind):
                if not inside(i, v + 1, B, UNITS):
                    return
                b = (v + 1) % B
                ps = arrived(dve, 0, i, v, kind)
                reach(dve, q[kind + "h"], i * B + v + 2)
                if kind == "k":
                    dve.tensor_tensor(kL[0:64, b, 0, :], ps[0:64, :], kS[0:64, b, 0, :].bitcast(F32), ALU.subtract)
                    ins = dve.tensor_tensor(kL[64:P, b, 1, :], ps[64:P, :], kS[64:P, b, 1, :].bitcast(F32),
                                            ALU.subtract)
                elif kind == "q":
                    dve.scalar_tensor_tensor(out=qS[64:P, b, 0, :], in0=ps[0:64, :], scalar=D1 ** -0.5,
                                             in1=qS[0:64, b, 0, :].bitcast(F32), op0=ALU.mult, op1=ALU.subtract)
                    ins = dve.scalar_tensor_tensor(out=qS[0:64, b, 1, :], in0=ps[64:P, :], scalar=D1 ** -0.5,
                                                   in1=qS[64:P, b, 1, :].bitcast(F32), op0=ALU.mult,
                                                   op1=ALU.subtract)
                else:
                    ps = ps.rearrange("p (k d) -> p k d", k=KC)
                    for h in range(2):
                        c = slice(64 * h, 64 * h + 64)
                        ins = dve.tensor_tensor(vL[:, b, h, :, c], ps[:, :, c], vH[:, b, h, :, c].bitcast(F32),
                                                ALU.subtract)
                take(0, kind, ins)

            def max1(i, k):
                if not inside(i, k, 16, 16 * PAIRS):
                    return
                reach(dve, q["s"], i * 16 + k + 1)
                dve.tensor_reduce(nmax[:, k // 4 % 2, k % 4:k % 4 + 1], bank[k % 2], AX.X, ALU.max, negate=True)\
                    .then_inc(q["m"], 1)

            def low_p(i, k):
                reach(dve, q["ph"], i * 16 + k + 1)
                dve.tensor_tensor(pL[:, k % 4, :], bank[2 + k % 2], pH[:, k % 4, :].bitcast(F32), ALU.subtract)\
                    .then_inc(q["pd"], 1)

            def scale_out1(i, v):
                if not inside(i, v - 1, B, UNITS):
                    return
                gone(dve, 0, i, v, "sums")
                reach(dve, q["pv"], i * 16 + 8 * v)
                b = (v - 1) % B
                dve.tensor_tensor(oT[:, b, :], bank[4 + b], rbs[:, :], ALU.mult).then_inc(q["o"], 1)

            def self_attention(i):
                for k in range(16):
                    v, step = k // 8, k % 8
                    max1(i, k + 5)
                    low_p(i, k)
                    if step < 3:
                        low1(i, v, ("k", "q", "v")[step])
                    if step == 4:
                        scale_out1(i, v)
                        inverse_sums(0, i, v)
                    if step in (5, 6):
                        add_out(0, i, v, step - 5)

            low1(0, -1, "k")
            low1(0, -1, "q")
            max1(0, 0)
            max1(0, 1)
            low1(0, -1, "v")
            for k in range(2, 5):
                max1(0, k)
            sweep(dve, PAIRS, self_attention)
            scale_out1(PAIRS, 0)
            add_out(0, PAIRS, 0, 0)
            add_out(0, PAIRS, 0, 1)
            gone(dve, 0, PAIRS, 0, "outb")

            norm()
            dve.wait_ge(bias_added, 3)
            r = at[1]

            def max2(i, k):
                if not inside(i, k, 4, 4 * PAIRS):
                    return
                for j in range(2):
                    reach(dve, r["s"], i * 8 + 2 * k + j + 1)
                    dve.tensor_reduce(nmax2[:, k % 2, 2 * j:2 * j + 2],
                                      bank[j][:, 0:2 * T].rearrange("p (h t) -> p h t", h=2),
                                      AX.X, ALU.max, negate=True).then_inc(r["m"], 1)

            def evac2(i, k):
                if not inside(i, k, 4, 4 * PAIRS):
                    return
                reach(dve, r["t"], i * 4 + k + 1)
                reach(dve, r["pv"], i * 4 + k - 1)
                dve.tensor_copy(P2T[:, k % 2, :, :], bank[2 + k % 2].rearrange("p (j s) -> p j s", j=4))
                dve.tensor_copy(P2Tt[:, k % 2, :], bank[4][:, 0:P]).then_inc(r["pd"], 1)

            def values2(i, v):
                if not inside(i, v + 1, B, UNITS):
                    return
                b = (v + 1) % B
                ps = arrived(dve, 1, i, v, "v")
                reach(dve, r["pv"], i * 4 + 2 * v)
                for h in range(2):
                    dve.tensor_copy(vZ2[:, b, h, 64 * h:64 * h + 64], ps[:, 64 * h:64 * h + 64])
                for j in range(2):
                    for h in range(2):
                        rows = slice(64 * j + 32 * h, 64 * j + 32 * h + 32)
                        ins = dve.tensor_copy(vZ2t[rows, b, j, 64 * h:64 * h + 64],
                                              ps[rows, P + 64 * h:P + 64 * h + 64])
                take(1, "v", ins)

            def low2(i, v, kind):
                if not inside(i, v + 2, B, UNITS):
                    return
                b = v % B
                ps = arrived(dve, 1, i, v, kind)
                reach(dve, r[kind + "h"], i * B + v + 3)
                if kind == "k":
                    dve.tensor_tensor(k2L[0:64, b, 0, :], ps[0:64, 0:T], k2H[0:64, b, 0, :].bitcast(F32),
                                      ALU.subtract)
                    ins = dve.tensor_tensor(k2L[64:P, b, 1, :], ps[64:P, 0:T], k2H[64:P, b, 1, :].bitcast(F32),
                                            ALU.subtract)
                else:
                    ins = dve.scalar_tensor_tensor(out=q2L[:, b, :], in0=ps, scalar=D1 ** -0.5,
                                                   in1=q2H[:, b, :].bitcast(F32), op0=ALU.mult, op1=ALU.subtract)
                take(1, kind, ins)

            def scale_out2(i, v):
                gone(dve, 1, i, v, "sums")
                reach(dve, r["pv"], i * 4 + 2 * v + 2)
                dve.tensor_tensor(oT[:, v, :], bank[5], rbs[:, :], ALU.mult).then_inc(r["o"], 1)

            def cross_attention(i):
                for k in range(4):
                    v = k // 2
                    max2(i, k + 2)
                    evac2(i, k + 1)
                    if k % 2 == 0:
                        values2(i, v)
                        inverse_sums(1, i, v)
                        add_out(1, i, v, 0)
                        add_out(1, i, v, 1)
                    else:
                        low2(i, v, "k")
                        low2(i, v, "q")
                        scale_out2(i, v)

            low2(0, -2, "k")
            low2(0, -2, "q")
            values2(0, -1)
            max2(0, 0)
            low2(0, -1, "k")
            low2(0, -1, "q")
            max2(0, 1)
            evac2(0, 0)
            sweep(dve, PAIRS, cross_attention)
            add_out(1, PAIRS, 0, 0)
            add_out(1, PAIRS, 0, 1)
            gone(dve, 1, PAIRS, 0, "outb")
            gone(dve, 1, PAIRS, 0, "outa")

            norm()
            dve.wait_ge(bias_added, 4)
            for c in range(FCH):
                for h in range(B):
                    reach(dve, ff_a, c * B + h + 1)
                    reach(dve, ff_gel, c * B + h + 1)
                    reach(dve, ff_out, (c - 2) * B + h + 1)
                    cols = slice(h * S, (h + 1) * S)
                    dve.scalar_tensor_tensor(out=hid[:, c % 2, cols], in0=bank[h], scalar=b1col[:, c:c + 1],
                                             in1=gel[:, c % 2, cols], op0=ALU.add, op1=ALU.mult).then_inc(ff_hid, 1)
            for k, t in enumerate(range(0, NT, 3)):
                n = min(3, NT - t)
                reach(dve, ff_out, (FCH - 1) * B + (t + n - 1) // QT + 1)
                dve.tensor_tensor(X[:, t:t + n, :], X[:, t:t + n, :],
                                  bank[4 + k][:, 0:n * C].rearrange("p (t c) -> p t c", t=n), ALU.add)\
                    .then_inc(x_final, 1)

        @block.tensor
        def _(pe):
            def done(ins):
                ins.then_inc(ps_ready, 1)

            pe.wait_ge(masks_ready, 1)
            pe.wait_ge(loaded_ctx, 96)
            for c in range(EC):
                ps = make(pe, f"cT{c}")
                for b in range(B):
                    pe.transpose(ps[:, b * T:b * T + P], cm[:, b, c * P:(c + 1) * P], ident[:, :])
                    ins = pe.transpose(ps[:, b * T + P:(b + 1) * T], ct[:, b, c * P:(c + 1) * P],
                                       ident[0:TTAIL, 0:TTAIL])
                done(ins)
            pe.wait_ge(s_ipn, 1)
            ps = make(pe, "ipT")
            for c in range(EC):
                ins = pe.transpose(ps[:, c * 8:(c + 1) * 8], ipj[:, c * P:(c + 1) * P], ident[0:8, 0:8])
            done(ins)

            def turn(src, kind):
                for part, cols in (("m", slice(0, P)), ("t", slice(P, C))):
                    for h in range(B):
                        ps = make(pe, f"{kind}_{part}{h}")
                        for t in range(QT):
                            ins = pe.transpose(ps[0:cols.stop - cols.start, t * P:(t + 1) * P],
                                               src[:, h * QT + t, cols], ident[:, :])
                        done(ins)

            pe.wait_ge(loaded_x, 16)
            turn(X, "x")
            pe.wait_ge(spread_ready, 6)
            taken(pe, "cT1")
            for g in range(G4):
                ps = make(pe, f"K0_{g}")[:, 0:B * T].rearrange("p (b t) -> p b t", b=B)
                for k, cols in ((0, slice(0, TT)), (1, slice(TT, T))):
                    for c in range(EC):
                        ins = pe.matmul(ps[:, :, cols], wke[:, k, c, 4 * g:4 * g + 4, :], cT[:, c, :, cols],
                                        start=(c == 0), stop=(c == EC - 1))
                done(ins)
            taken(pe, "x_m1")
            taken(pe, "x_t1")
            for g in range(G4):
                for h in range(B):
                    ps = make(pe, f"Q0_{g}_{h}")
                    pe.matmul(ps, wqe[:, 4 * g:4 * g + 4, :], nTm[:, h * S:(h + 1) * S], start=True, stop=False)
                    done(pe.matmul(ps, wqet[:, 4 * g:4 * g + 4, :], nTt[0:CT, h * S:(h + 1) * S], start=False, stop=True))
            pe.wait_ge(ip_ready, EC + EC * B)
            taken(pe, "ipT")
            for tail in range(2):
                for b in range(B):
                    ps = make(pe, f"GVt_{b}" if tail else f"GV_{b}")
                    at_ = 0
                    lo = P if tail else 0
                    for width, rhs in ((TT - lo, lambda c: cT[:, c, b, lo:TT]), (C, lambda c: wkv0[:, 2, c, :]),
                                       (NIP, lambda c: ipT[:, c, b * NIP:(b + 1) * NIP])):
                        for c in range(EC):
                            lhs = cT4[:, c, b, :, :] if tail else cT[:, c, b, 0:P]
                            ins = pe.matmul(ps[:, at_:at_ + width], lhs, rhs(c), start=(c == 0), stop=(c == EC - 1))
                        at_ += width
                    done(ins)
            for b in range(B):
                ps = make(pe, f"VB_{b}")
                for c in range(EC):
                    ins = pe.matmul(ps[0:4 * HEADS, 0:C], ipR[:, c, b, :, :], wkv0[:, 3, c, :],
                                    start=(c == 0), stop=(c == EC - 1))
                done(ins)
            taken(pe, "GVt_1")
            taken(pe, "VB_1")
            taken(pe, "GV_1")

            def scores0(i, k):
                if not inside(i, k, STEPS0, QT * STEPS0):
                    return
                v, g = k // G4, k % G4
                reach(pe, q0_ready, i * STEPS0 + k + 1)
                reach(pe, p0_ready, i * STEPS0 + k - 1)
                sc = (bank01, bank23)[k % 2]
                for j in range(2):
                    ins = pe.matmul(sc[:, j, 0:2 * T], qs0[:, v % B, g, :], KB0[:, g, v % B, 2 * j:2 * j + 2, :],
                                    start=True, stop=True)
                ins.then_inc(s0_ready, 1)

            def turn0(i, k):
                if not inside(i, k, STEPS0, QT * STEPS0):
                    return
                reach(pe, p0_ready, i * STEPS0 + k + 1)
                reach(pe, pt0_ready, i * STEPS0 + k)
                for j in range(4):
                    pe.transpose(bank45[:, 0, j * P:(j + 1) * P], P0[:, k % STEPS0 % 5, j, 0:P], ident[:, :])
                reach(pe, p0t_ready, i * STEPS0 + k + 1)
                pe.transpose(bank45[:, 1, 0:P], P0t[:, k % 2, :, :], ident[:, :]).then_inc(t0_ready, 1)

            def mix0(i, n):
                b, g = n // G4, n % G4
                reach(pe, pt0_ready, i * STEPS0 + n + 1)
                for k in range(2):
                    reach(pe, u0_taken, i * 2 * STEPS0 + 2 * n + k - 1)
                    for j in range(2):
                        pe.matmul(bank67[:, k, j * RHS:(j + 1) * RHS], PT0[:, n % 2, 2 * k + j, :],
                                  GV[:, b, 4 * g + 2 * k + j, :], start=(j == 0), stop=False, skip_group_check=True)
                    ins = pe.matmul(bank67[:, k, 0:2 * RHS].rearrange("p (j t) -> p j t", j=2)[:, :, P:RHS],
                                    PT0t[:, n % 2, :], GVt[:, b, g, 2 * k:2 * k + 2, :], start=False, stop=True,
                                    skip_group_check=True)
                    ins.then_inc(u0_ready, 1)

            def first_block(i):
                for k in range(STEPS0):
                    scores0(i, k + 3)
                    turn0(i, k + 1)
                    mix0(i, k)

            scores0(0, 0)
            scores0(0, 1)
            scores0(0, 2)
            turn0(0, 0)
            sweep(pe, QT, first_block)
            pe.wait_ge(fn_ready, 1)
            for h in range(B):
                ps = make(pe, f"F_{h}")
                for t in range(QT):
                    ins = pe.transpose(ps[0:4 * HEADS, t * P:(t + 1) * P],
                                       f1[:, h * QT + t, :, :].rearrange("p h n -> p (h n)"), ident[:, :])
                done(ins)
            for part, lo, hi in (("m", 0, P), ("t", P, C)):
                for b in range(B):
                    ps = make(pe, f"O_{part}{b}")[0:hi - lo, :]
                    taken(pe, f"F_{b}")
                    pe.matmul(ps, VB0[:, b, lo:hi], FT[:, b * S:(b + 1) * S], start=True, stop=False,
                              skip_group_check=True)
                    for t in range(QT):
                        tx = TX[:, b * QT + t, :, :].rearrange("p h d -> p (h d)")
                        ins = pe.matmul(ps[:, t * P:(t + 1) * P], tx[:, lo:hi], ident[:, :], start=False,
                                        stop=True, skip_group_check=True)
                    done(ins)
            for k in range(4):
                ps = make(pe, f"out_{k}")
                taken(pe, "O_t1")
                for j in range(2):
                    t = 2 * k + j
                    pe.matmul(ps[:, j * C:(j + 1) * C], OTm[:, t * P:(t + 1) * P], wo0[:, :], start=True, stop=False)
                    ins = pe.matmul(ps[:, j * C:(j + 1) * C], OTt[:, t * P:(t + 1) * P], wo0t[:, :], start=False,
                                    stop=True)
                done(ins)

            def turn_norm(n):
                pe.wait_ge(xn_ready, n)
                for b in range(B):
                    for part in ("m", "t"):
                        ps = make(pe, f"n{n}_{part}{b}")
                        if part == "t":
                            pe.wait_ge(xn3_ready, n)
                        for t in range(QT):
                            src = XN[:, b * QT + t, 0:P] if part == "m" else XN3[:, b * QT + t, :, :]\
                                .rearrange("p r c -> p (r c)")
                            ins = pe.transpose(ps[0:P if part == "m" else 3 * CT, t * P:(t + 1) * P], src,
                                               ident[:, :])
                        done(ins)
                taken(pe, f"n{n}_t{B - 1}")
                pe.wait_ge(nl_ready, 4 * n)

            def by_weights(ps, high, low, third, cols):
                pe.matmul(ps, high, nTh[:, cols], start=True, stop=False)
                pe.matmul(ps, low, nTh[:, cols], start=False, stop=False)
                pe.matmul(ps, high, nTl[:, cols], start=False, stop=False)
                return pe.matmul(ps, third, nT3[:, cols], start=False, stop=True)

            def spread_sums(a, i, v):
                ps = use(pe, a, i, v, "sums")
                reach(pe, at[a]["rsp"], i * B + v + (0 if a == 0 else 1))
                for t in range(QT):
                    ins = pe.transpose(ps[:, t * P:(t + 1) * P], rsp[:, t, :, :], ident[:, :])
                finish(a, "sums", ins)

            def project(a, i, v, half):
                if not inside(i, v - 1, B, UNITS):
                    return
                kind, b = ("outa", "outb")[half], (v - 1) % B
                ps = use(pe, a, i, v, kind)
                reach(pe, at[a]["o"], i * B + v)
                if v == 1:
                    reach(pe, at[a]["wo"], i + 1)
                for j in range(2):
                    t = 2 * half + j
                    ins = pe.matmul(ps[:, j * C:(j + 1) * C], oT[:, b, t * P:(t + 1) * P], wo[:, :],
                                    start=True, stop=True)
                finish(a, kind, ins)

            turn_norm(1)
            q = at[0]

            def inputs1(i, v, kind):
                if not inside(i, v + 1, B, UNITS):
                    return
                if kind == "k" and v % 2:
                    reach(pe, q["w"], (i + (v + 1) // 2) * 12 + 12)
                b = (v + 1) % B
                ps = use(pe, 0, i, v, kind)
                if kind != "v":
                    ins = by_weights(ps, wh[kind][:, :], wl[kind][:, :], w3[kind][:, :], slice(b * S, (b + 1) * S))
                else:
                    for k in range(KC):
                        o, cols = ps[:, k * P:(k + 1) * P], slice(b * S + k * P, b * S + (k + 1) * P)
                        pe.matmul(o, nTh[:, cols], wh["v"][:, :], start=(k == 0), stop=False, skip_group_check=True)
                        pe.matmul(o, nTh[:, cols], wl["v"][:, :], start=False, stop=False, skip_group_check=True)
                        pe.matmul(o, nTl[:, cols], wh["v"][:, :], start=False, stop=False, skip_group_check=True)
                        ins = pe.matmul(o, nT3[:, cols], w3["v"][:, :], start=False, stop=True,
                                        skip_group_check=True)
                finish(0, kind, ins)

            def scores1(i, k):
                if not inside(i, k, 16, 16 * PAIRS):
                    return
                b, h, j = k // 8 % B, k // 4 % 2, k % 4
                if k % 8 == 0:
                    v = k // 8
                    gone(pe, 0, i, v - 1, "k")
                    gone(pe, 0, i, v - 1, "q")
                    reach(pe, q["kc"], i * 4 + 2 * v + 2)
                reach(pe, q["p"], i * 16 + k - 1)
                for keys in (kS, kL):
                    ins = pe.matmul(bank[k % 2], qS[:, b, h, j * P:(j + 1) * P], keys[:, b, h, :],
                                    start=(keys is kS), stop=(keys is kL))
                ins.then_inc(q["s"], 1)

            def turn1(i, k):
                if k % 4 == 0:
                    reach(pe, q["p"], i * 16 + k + 4)
                reach(pe, q["pd"], i * 16 + k - 1)
                for t in range(QT):
                    ins = pe.transpose(bank[2 + k % 2][:, t * P:(t + 1) * P],
                                       pr[:, k // 4 % 2, t, k % 4 * P:(k % 4 + 1) * P], ident[:, :])
                ins.then_inc(q["t"], 1)

            def mix1(i, k):
                if not inside(i, k, 16, 16 * PAIRS):
                    return
                b, h, j = k // 8 % B, k // 4 % 2, k % 4
                if k % 8 == 0:
                    reach(pe, q["o"], i * B + k // 8 - 1)
                    gone(pe, 0, i, k // 8 - 1, "v")
                reach(pe, q["pd"], i * 16 + k + 1)
                o = bank[4 + b]
                pe.matmul(o, vH[:, b, h, j, :], pH[:, k % 4, :], start=(k % 8 == 0), stop=False)
                pe.matmul(o, vL[:, b, h, j, :], pH[:, k % 4, :], start=False, stop=False)
                pe.matmul(o, vH[:, b, h, j, :], pL[:, k % 4, :], start=False, stop=(k % 8 == 7))\
                    .then_inc(q["pv"], 1)

            def self_attention(i):
                for k in range(16):
                    v, step = k // 8, k % 8
                    scores1(i, k + 5)
                    turn1(i, k)
                    mix1(i, k - 1)
                    if step < 3:
                        inputs1(i, v, ("k", "q", "v")[step])
                    if step == 3 and inside(i, v - 1, B, UNITS):
                        spread_sums(0, i, v)
                    if step in (5, 6):
                        project(0, i, v, step - 5)

            inputs1(0, -1, "k")
            inputs1(0, -1, "q")
            scores1(0, 0)
            scores1(0, 1)
            inputs1(0, -1, "v")
            for k in range(2, 5):
                scores1(0, k)
            sweep(pe, PAIRS, self_attention)
            mix1(PAIRS - 1, 15)
            spread_sums(0, PAIRS, 0)
            project(0, PAIRS, 0, 0)
            project(0, PAIRS, 0, 1)

            turn_norm(2)
            r = at[1]

            def keys_queries2(i, v, kind):
                if not inside(i, v + 2, B, UNITS):
                    return
                b = v % B
                if kind == "k" and b == 0:
                    reach(pe, r["w"], (i + (v + 2) // 2) * 6 + 6)
                ps = use(pe, 1, i, v, kind)
                if kind == "k":
                    for c in range(EC):
                        ins = pe.matmul(ps[:, 0:T], cwk[:, c, :], cT[:, c, b, :], start=(c == 0), stop=(c == EC - 1))
                else:
                    ins = by_weights(ps, wh["q"][:, :], wl["q"][:, :], w3["q"][:, :], slice(b * S, (b + 1) * S))
                finish(1, kind, ins)

            def values2(i, v):
                if not inside(i, v + 1, B, UNITS):
                    return
                b = (v + 1) % B
                if b == 0:
                    reach(pe, r["wv"], (i + (v + 1) // 2) * 2 + 2)
                ps = use(pe, 1, i, v, "v")
                for tail in range(2):
                    for c in range(EC):
                        lhs = cT4[:, c, b, :, :] if tail else cT[:, c, b, 0:P]
                        ins = pe.matmul(ps[:, tail * P:(tail + 1) * P], lhs, cwv[:, c, :],
                                        start=(tail == 0 and c == 0), stop=(c == 1), skip_group_check=True)
                finish(1, "v", ins)

            def scores2(i, k):
                if not inside(i, k, 4, 4 * PAIRS):
                    return
                b, half = k // 2 % B, k % 2
                if half == 0:
                    gone(pe, 1, i, k // 2 - 2, "k")
                    gone(pe, 1, i, k // 2 - 2, "q")
                for j in range(2):
                    reach(pe, r["p"], i * 8 + 2 * k + j - 1)
                    o, t = bank[j][:, 0:2 * T], 2 * half + j
                    cols = slice(t * P, (t + 1) * P)
                    pe.matmul(o, q2H[:, b, cols], k2H[:, b, :, :], start=True, stop=False)
                    pe.matmul(o, q2H[:, b, cols], k2L[:, b, :, :], start=False, stop=False)
                    pe.matmul(o, q2L[:, b, cols], k2H[:, b, :, :], start=False, stop=True).then_inc(r["s"], 1)

            def turn2(i, k):
                if not inside(i, k, 4, 4 * PAIRS):
                    return
                reach(pe, r["p"], i * 8 + 2 * k + 2)
                reach(pe, r["pd"], i * 4 + k - 1)
                for h in range(2):
                    for j in range(2):
                        c = 2 * h + j
                        pe.transpose(bank[2 + k % 2][:, c * P:(c + 1) * P], P2[:, k % 2, 2 * j + h, 0:P],
                                     ident[:, :])
                reach(pe, r["pd"], i * 4 + k)
                reach(pe, r["pt"], i * 4 + k + 1)
                pe.transpose(bank[4][:, 0:P], P2t[:, k % 2, :, :], ident[:, :]).then_inc(r["t"], 1)

            def mix2(i, k):
                b, half = k // 2, k % 2
                if half == 0:
                    reach(pe, r["o"], i * B + b)
                    gone(pe, 1, i, b - 1, "v")
                reach(pe, r["pd"], i * 4 + k + 1)
                for h in range(2):
                    pe.matmul(bank[5][:, half * 256:half * 256 + 256], vZ2[:, b, h, :],
                              P2T[:, k % 2, 2 * h:2 * h + 2, :], start=(h == 0), stop=False, skip_group_check=True)
                for j in range(2):
                    o = half * 256 + j * P
                    ins = pe.matmul(bank[5][:, o:o + P], vZ2t[:, b, j, :], P2Tt[:, k % 2, :], start=False, stop=True,
                                    skip_group_check=True)
                ins.then_inc(r["pv"], 1)

            def cross_attention(i):
                for k in range(4):
                    v = k // 2
                    scores2(i, k + 2)
                    turn2(i, k + 1)
                    if k % 2 == 0:
                        values2(i, v)
                        project(1, i, v, 0)
                        mix2(i, k)
                        project(1, i, v, 1)
                    else:
                        keys_queries2(i, v, "k")
                        keys_queries2(i, v, "q")
                        spread_sums(1, i, v)
                        mix2(i, k)

            keys_queries2(0, -2, "k")
            keys_queries2(0, -2, "q")
            values2(0, -1)
            scores2(0, 0)
            keys_queries2(0, -1, "k")
            keys_queries2(0, -1, "q")
            scores2(0, 1)
            turn2(0, 0)
            sweep(pe, PAIRS, cross_attention)
            project(1, PAIRS, 0, 0)
            project(1, PAIRS, 0, 1)

            turn_norm(3)
            pe.wait_ge(ff_w, 4)

            def ff_in(c, s, made_sem, free):
                for h in range(B):
                    reach(pe, free, (c - 1) * B + h + 1)
                    w_ = slice(s * FF + c * P, s * FF + (c + 1) * P)
                    by_weights(bank[2 * s + h], f1h[:, w_], f1l[:, w_], f13[:, w_], slice(h * S, (h + 1) * S))\
                        .then_inc(made_sem, 1)

            def ff_back(c):
                for t in range(NT):
                    if t % QT == 0:
                        reach(pe, ff_hid, c * B + t // QT + 1)
                    ins = pe.matmul(bank[4 + t // 3][:, t % 3 * C:(t % 3 + 1) * C], hid[:, c % 2, t * P:(t + 1) * P],
                                    f2w[:, c, :], start=(c == 0 and t % 3 == 0), stop=(c == FCH - 1),
                                    skip_group_check=True)
                    if t % QT == QT - 1:
                        ins.then_inc(ff_out, 1)

            ff_in(0, 1, ff_g, ff_gel)
            ff_in(0, 0, ff_a, ff_hid)
            for c in range(FCH):
                if c + 1 < FCH:
                    ff_in(c + 1, 1, ff_g, ff_gel)
                ff_back(c)
                if c + 1 < FCH:
                    ff_in(c + 1, 0, ff_a, ff_hid)


def kernel(**inputs):
    import numpy as _np
    import concourse.bacc as _bacc
    from concourse import mybir as _mybir
    from concourse.bass_utils import run_bass_kernel_spmd as _run

    nc = _bacc.Bacc("TRN2", target_bir_lowering=False, num_devices=1)
    arrays, aps = {}, {}
    for name in inputs:
        a = _np.ascontiguousarray(inputs[name])
        arrays[f"in_{name}"] = a
        aps[name] = nc.dram_tensor(f"in_{name}", a.shape, _mybir.dt.from_np(a.dtype), kind="ExternalInput").ap()
    result = nc.dram_tensor("result", (B, S, C), _mybir.dt.float32, kind="ExternalOutput").ap()
    cross_attention_block_kernel(nc, aps, result)
    r = _run(nc, [arrays], core_ids=[0])
    return r.results[0]["result"]
```

```python
import concourse.bass as bass
from concourse import mybir
from contextlib import ExitStack

B, S, C = 2, 512, 160
T, E = 154, 256
NIP = 4
TT = T - NIP
HEADS = 20
P = 128
QT = S // P
NT = B * QT
N = B * S
CT = C - P
KC = S // P
EC = E // P
D0 = C // HEADS
D1 = 64
PAIRS = HEADS // 2
G4 = HEADS // 4
FF = 4 * C
FCH = FF // P
TXTAIL = TT - P
TTAIL = T - P
PW = 160
RHS = TT + D0 + NIP
RHT = TXTAIL + D0 + NIP
ST = 2 + D0 + NIP + NIP
STEPS0 = B * G4
EPS_NORM = 1e-12
EPS_LN = 1e-5
TINY = 1e-30
SEM_SCALE = 0.5


def cross_attention_block_kernel(nc, A, out):
    F32, F32R = mybir.dt.float32, mybir.dt.float32r
    ALU = mybir.AluOpType
    ACT = mybir.ActivationFunctionType
    AX = mybir.AxisListType
    x, ctx_in = A["x"], A["ctx_2048"]

    with ExitStack() as stack:
        def sb(name, shape, dt=F32):
            return stack.enter_context(nc.sbuf_tensor(name, shape, dt))

        def sem(name):
            return stack.enter_context(nc.semaphore(name))

        bank01 = stack.enter_context(nc.psum_tensor("bank01", [P, 2, 512], F32))
        bank23 = stack.enter_context(nc.psum_tensor("bank23", [P, 2, 512], F32))
        bank45 = stack.enter_context(nc.psum_tensor("bank45", [P, 2, 512], F32))
        bank67 = stack.enter_context(nc.psum_tensor("bank67", [P, 2, 512], F32))
        bank = [t[:, k, :] for t in (bank01, bank23, bank45, bank67) for k in range(2)]

        ident = sb("ident", [P, P])
        X = sb("X", [P, NT, C])
        nTm, nTt = sb("nTm", [P, N]), sb("nTt", [3 * CT, N])
        var, root = sb("var", [P, NT]), sb("root", [P, NT])
        bn6, mv, rstd = sb("bn6", [P, NT, 6]), sb("mv", [P, NT, 2]), sb("rstd", [P, NT])
        gcol = sb("gcol", [P, 12])
        scrap = sb("scrap", [P, 1])
        brow = sb("brow", [P, 4, C])
        b1col = sb("b1col", [P, 2 * FCH])
        smask = sb("smask", [P, QT])
        cm, ct = sb("cm", [P, B, E]), sb("ct", [TTAIL, B, E])
        cT = sb("cT", [P, EC, B, T])
        cT4 = sb("cT4", [P, EC, B, 4, 32])
        raw = {n: sb("raw_" + n, [P, P]) for n in ("q", "k", "v")}
        rawt = {n: sb("rawt_" + n, [P, P]) for n in ("q", "k", "v")}
        raw["o"] = sb("raw_o", [P, C])
        wh = {n: sb("wh_" + n, [P, P], F32R) for n in ("q", "k", "v")}
        wl = {n: sb("wl_" + n, [P, P], F32R) for n in ("q", "k", "v")}
        w3 = {n: sb("w3_" + n, [3 * CT, P], F32R) for n in ("q", "k", "v")}
        wo = sb("w_o", [P, C])
        first = ExitStack()

        def sb0(name, shape, dt=F32):
            return first.enter_context(nc.sbuf_tensor(name, shape, dt))

        wq0, wq0t = sb0("wq0", [P, C]), sb0("wq0t", [CT, C])
        wkv0 = sb0("wkv0", [P, 4, EC, C])
        wo0, wo0t = sb0("wo0", [P, C]), sb0("wo0t", [CT, C])
        wqe, wqet = sb0("wqe", [P, HEADS, 32]), sb0("wqet", [CT, HEADS, 32])
        wke = sb0("wke", [P, 2, EC, HEADS, 32])
        ipn, ips, ipj = sb0("ipn", [B * NIP, E]), sb0("ips", [B * NIP, 4]), sb0("ipj", [B * NIP, E])
        ipR = sb0("ipR", [P, EC, B, HEADS, NIP])
        ipT = sb0("ipT", [P, EC, B * NIP])
        low_q, low_k = sb0("low_q", [P, 1]), sb0("low_k", [P, 1])
        lows_q = sb0("lows_q", [P, 1])
        sign_q, sign_k = sb0("sign_q", [P, 1]), sb0("sign_k", [P, 1])
        QT0 = sb0("QT0", [P, G4, N], F32R)
        KB0 = sb0("KB0", [P, G4, B, 4, T], F32R)
        hi0, tm0 = sb0("hi0", [P, 2, 512], F32R), sb0("tm0", [P, 2, 512])
        GV, GVt = sb0("GV", [P, B, HEADS, RHS]), sb0("GVt", [P, B, G4, 4, RHT])
        VB0 = sb0("VB0", [4 * HEADS, B, C])
        VT0, VT0t = sb0("VT0", [P, B, 4 * HEADS]), sb0("VT0t", [CT, B, 4 * HEADS])
        VW0 = sb0("VW0", [4 * HEADS, B, C])
        bmask = sb0("bmask", [4 * HEADS, C])
        qs0 = sb0("qs0", [P, B, G4, P], F32R)
        nmax0 = sb0("nmax0", [P, 5, 4])
        P0 = sb0("P0", [P, 5, 4, PW])
        P0t = sb0("P0t", [P, 2, 4, 32])
        PT0, PT0t = sb0("PT0", [P, 2, 4, P]), sb0("PT0t", [P, 2, P])
        den0 = sb0("den0", [P, B, HEADS])
        st0 = sb0("st0", [P, B, HEADS, ST])
        sta = sb0("sta", [P, NT, HEADS, ST])
        h1, h2, h3 = sb0("h1", [P, NT, HEADS]), sb0("h2", [P, NT, HEADS]), sb0("h3", [P, NT, HEADS])
        f1 = sb0("f1", [P, NT, HEADS, NIP])
        f2 = sb0("f2", [P, NT, HEADS, NIP])
        FT = sb0("FT", [4 * HEADS, N])
        TX = sb0("TX", [P, NT, HEADS, D0])
        first.close()

        XN = sb("XN", [P, NT, C + 2 * CT])
        nTh, nTl, nT3 = sb("nTh", [P, N], F32R), sb("nTl", [P, N], F32R), sb("nT3", [3 * CT, N], F32R)
        nmax = sb("nmax", [P, 2, QT])
        den = sb("den", [P, B, QT, 2])
        rden = sb("rden", [P, B, QT, 2])
        rsp = sb("rsp", [P, QT, 2, D1])
        rbs = sb("rbs", [P, S])
        oT = sb("oT", [P, B, S])
        cwk, cwv = sb("cwk", [P, EC, P]), sb("cwv", [P, EC, P])
        q2H, q2L = sb("q2H", [P, B, S], F32R), sb("q2L", [P, B, S], F32R)
        k2H, k2L = sb("k2H", [P, B, 2, T], F32R), sb("k2L", [P, B, 2, T], F32R)
        vZ2, vZ2t = sb("vZ2", [P, B, 2, P]), sb("vZ2t", [P, B, 2, P])
        P2, P2t = sb("P2", [P, 2, 4, PW]), sb("P2t", [P, 2, 4, 32])
        P2T, P2Tt = sb("P2T", [P, 2, 4, P]), sb("P2Tt", [P, 2, P])
        nmax2 = sb("nmax2", [P, 2, 4])
        f1raw, f1rawt, f2w = sb("f1raw", [P, 2 * FF]), sb("f1rawt", [3 * CT, 2 * FF]), sb("f2w", [P, FCH, C])
        attn = ExitStack()

        def sba(name, shape, dt=F32R):
            return attn.enter_context(nc.sbuf_tensor(name, shape, dt))

        qS = sba("qS", [P, B, 2, S])
        kS = sba("kS", [P, B, 2, S])
        kL = sba("kL", [P, B, 2, S])
        vH = sba("vH", [P, B, 2, KC, P])
        vL = sba("vL", [P, B, 2, KC, P])
        pr = sba("pr", [P, 2, QT, S], F32)
        pH, pL = sba("pH", [P, 4, S]), sba("pL", [P, 4, S])
        attn.close()
        f1h, f1l = sb("f1h", [P, 2 * FF], F32R), sb("f1l", [P, 2 * FF], F32R)
        f13 = sb("f13", [3 * CT, 2 * FF], F32R)
        gel, hid = sb("gel", [P, 2, N]), sb("hid", [P, 2, N])
        block = stack.enter_context(nc.Block())

        loaded_x, loaded_ctx = sem("loaded_x"), sem("loaded_ctx")
        loaded_w0, loaded_small = sem("loaded_w0"), sem("loaded_small")
        masks_ready = sem("masks_ready")
        spread_ready = sem("spread_ready")
        ip_ready = sem("ip_ready")
        stored = sem("stored")
        ps_ready = sem("ps_ready")
        by_act, by_dve = sem("by_act"), sem("by_dve")
        hi_ready = sem("hi_ready")
        dve_step = sem("dve_step")
        pool_step = sem("pool_step")
        pool_held = sem("pool_held")
        s_ipn = sem("s_ipn")
        square_ready, root_ready = sem("square_ready"), sem("root_ready")

        USES = [("cT0", "act"), ("cT1", "act"), ("x_m0", "act"), ("x_m1", "act"), ("x_t0", "dve"),
                ("x_t1", "dve"), ("ipT", "dve")]
        USES += [("GV_0", "act"), ("GV_1", "act"), ("GVt_0", "dve"), ("GVt_1", "dve"),
                 ("VB_0", "dve"), ("VB_1", "dve")]
        USES += [(f"{n}_{g}", "dve") for g in range(G4) for n in ("K0", "Q0_0")]
        USES += [("VT_0", "act"), ("VT_1", "act"), ("VW_0", "act"), ("VW_1", "act")]
        USES += [(f"Q0_1_{g}", "dve") for g in range(G4)]
        for b in range(B):
            USES += [(f"TX_m{b}", "act"), (f"TX_t{b}", "act")]
        USES += [("F_0", "act"), ("F_1", "act")] + [(f"out_{k}", "dve") for k in range(4)]
        for k in (1, 2, 3):
            USES += [(f"n{k}_{p}", "dve") for p in ("m0", "t0", "m1", "t1")]
        index = {name: k for k, (name, _) in enumerate(USES)}
        count = {name: sum(e == eng for _, e in USES[:k + 1]) for k, (name, eng) in enumerate(USES)}

        def bank_of(name):
            k = index[name]
            return bank[k % 8] if k < index["n1_m0"] else bank[((0, 1, 2, 3), (0, 1, 2, 3), (0, 1, 4, 5))
                                                               [int(name[1]) - 1][(k - index["n1_m0"]) % 4]]

        def make(pe, name):
            k = index[name]
            if 8 <= k < index["n1_m0"]:
                taken(pe, USES[k - 8][0])
            return bank_of(name)

        def taken(eng, name):
            eng.wait_ge(by_act if USES[index[name]][1] == "act" else by_dve, count[name])

        def made(eng, name):
            eng.wait_ge(ps_ready, index[name] + 1)
            return bank_of(name)

        q0_ready, s0_ready, m0_ready = sem("q0_ready"), sem("s0_ready"), sem("m0_ready")
        p0_ready, p0t_ready, t0_ready, pt0_ready = sem("p0_ready"), sem("p0t_ready"), sem("t0_ready"), sem("pt0_ready")
        u0_ready, u0_taken, st0_saved = sem("u0_ready"), sem("u0_taken"), sem("st0_saved")
        f_ready, fe_ready, fn_ready = sem("f_ready"), sem("fe_ready"), sem("fn_ready")
        tx_ready = sem("tx_ready")
        xn_ready, xn3_ready, bias_added = sem("xn_ready"), sem("xn3_ready"), sem("bias_added")
        nh_ready, nl_ready = sem("nh_ready"), sem("nl_ready")
        names = ("raw", "rawo", "w", "wv", "wo", "s", "m", "p", "pt", "t", "ph", "pd", "pv", "rden", "rsp", "o",
                 "kh", "kc", "qh", "vh", "misc6", "misc7", "taken6", "taken7")
        at = [{n: sem(f"{n}_{kind}") for n in names} for kind in ("self", "cross")]
        zeroed = sem("zeroed")
        ff_raw, ff_w, ff_g, ff_a, ff_gel, ff_hid = (sem(f"ff_{n}") for n in ("raw", "w", "g", "a", "gel", "hid"))
        ff_out, x_final = sem("ff_out"), sem("x_final")

        def reach(eng, sem_, n):
            if isinstance(n, int) and n <= 0:
                return
            eng.wait_ge(sem_, n)

        def sweep(eng, total, body):
            body(0)
            with eng.Fori(1, total - 1) as i:
                body(i)
            body(total - 1)

        def inside(i, k, per, total):
            return not isinstance(i, int) or 0 <= i * per + k < total

        UNITS = B * PAIRS
        MISC = [[("q", 1, 7), ("v", 1, 6), ("sums", -1, 7), ("outa", -1, 6), ("k", 2, 7), ("outb", -1, 6)],
                [("v", 1, 6), ("outa", -1, 7), ("outb", -1, 6), ("k", 2, 7), ("q", 2, 6), ("sums", 0, 7)]]

        STEPS1 = {0: "q", 1: "v", 6: "k"}

        def shared(a, i, v, kind):
            b6 = {n: bk for n, _, bk in MISC[a]}[kind]

            def exact(u):
                n = 0
                for w_ in range(-2, u + 1):
                    for name, rel, bk in MISC[a]:
                        if 0 <= w_ + rel < UNITS and bk == b6:
                            n += 1
                        if w_ == u and name == kind:
                            break
                return n
            if isinstance(i, int):
                return b6, exact(B * i + v)
            return b6, i * 6 + (exact(B * 2 + v) - 12)

        def use(pe, a, i, v, kind):
            bk, n = shared(a, i, v, kind)
            reach(pe, at[a][f"taken{bk}"], n - 1)
            return bank[bk]

        def finish(a, kind, ins):
            ins.then_inc(at[a][f"misc{ {n: bk for n, _, bk in MISC[a]}[kind] }"], 1)

        def arrived(eng, a, i, v, kind):
            bk, n = shared(a, i, v, kind)
            reach(eng, at[a][f"misc{bk}"], n)
            return bank[bk]

        def take(a, kind, ins):
            ins.then_inc(at[a][f"taken{ {n: bk for n, _, bk in MISC[a]}[kind] }"], 1)

        def gone(eng, a, i, v, kind):
            bk, n = shared(a, i, v, kind)
            reach(eng, at[a][f"taken{bk}"], n)

        W_IN = [("L0_xattn_W_k", 0), ("L0_xattn_W_k_ip", 1), ("L0_xattn_W_v", 2), ("L0_xattn_W_v_ip", 3)]
        SMALL = 3 * 2 * 4 + 4 + 2

        @block.sync
        def _(sp):
            for b in range(B):
                sp.dma_start(cm[:, b, :], ctx_in[b, 0:P, :]).then_inc(loaded_ctx, 16)
                sp.dma_start(ct[:, b, :], ctx_in[b, P:T, :]).then_inc(loaded_ctx, 16)
                sp.dma_start(ipn[b * NIP:(b + 1) * NIP, :], ctx_in[b, TT:T, :]).then_inc(loaded_ctx, 16)
            sp.dma_start(X[:, :, :], x.rearrange("b (t p) c -> p (b t) c", p=P)).then_inc(loaded_x, 16)
            for name, k in W_IN:
                sp.dma_start(wkv0[:, k, :, :], A[name].rearrange("(c p) n -> p c n", p=P)).then_inc(loaded_w0, 16)
            sp.dma_start(wq0[:, :], A["L0_xattn_W_q"][0:P, :]).then_inc(loaded_w0, 16)
            sp.dma_start(wq0t[:, :], A["L0_xattn_W_q"][P:C, :]).then_inc(loaded_w0, 16)
            sp.dma_start(wo0[:, :], A["L0_xattn_W_out"][0:P, :]).then_inc(loaded_w0, 16)
            sp.dma_start(wo0t[:, :], A["L0_xattn_W_out"][P:C, :]).then_inc(loaded_w0, 16)
            for k in range(3):
                for j, v in enumerate(("g", "b")):
                    col = A[f"L1_xattn_ln{k + 1}_{v}"].rearrange("(c a) -> c a", a=1)
                    sp.dma_start(gcol[:, 4 * k + j:4 * k + j + 1], col[0:P, :]).then_inc(loaded_small, 16)
                    for rep in range(3):
                        sp.dma_start(gcol[rep * CT:(rep + 1) * CT, 4 * k + 2 + j:4 * k + 3 + j], col[P:C, :])\
                            .then_inc(loaded_small, 16)
            for k, v in enumerate(("L0_xattn_b_out", "L1_xattn_a1_bo", "L1_xattn_a2_bo", "L1_xattn_ff_b2")):
                sp.dma_start(brow[:, k, :], A[v].rearrange("(a c) -> a c", a=1).broadcast_to([P, C]))\
                    .then_inc(loaded_small, 16)
            sp.dma_start(b1col[:, :], A["L1_xattn_ff_b1"].rearrange("(c p) -> p c", p=P),
                         allow_slow_non_contiguous=True).then_inc(loaded_small, 16)
            sp.dma_start(smask[:, :], A["fside_S_0"].rearrange("(t p) -> p t", p=P),
                         allow_slow_non_contiguous=True).then_inc(loaded_small, 16)

            def load_pair(i, a):
                q, pre = at[a], ("a1", "a2")[a]
                if a == 0:
                    reach(sp, q["w"], i * 12)
                else:
                    reach(sp, q["wv"], i * 2)
                for n in ("q", "k", "v"):
                    src = A[f"L1_xattn_{pre}_w{n}"]
                    sp.dma_start(raw[n][:, :], src[0:P, bass.ds(i * P, P)]).then_inc(q["raw"], 16)
                    if src.shape[0] == E:
                        sp.dma_start(rawt[n][:, :], src[P:E, bass.ds(i * P, P)]).then_inc(q["raw"], 16)
                    else:
                        for k in range(3):
                            sp.dma_start(rawt[n][k * CT:(k + 1) * CT, :], src[P:C, bass.ds(i * P, P)])\
                                .then_inc(q["raw"], 16)
                reach(sp, q["wo"], i)
                sp.dma_start(raw["o"][:, :], A[f"L1_xattn_{pre}_wo"][bass.ds(i * P, P), :])\
                    .then_inc(q["rawo"], 16)

            load_pair(0, 0)
            taken(sp, "out_3")
            ff1 = A["L1_xattn_ff_w1"]
            sp.dma_start(f1raw[:, :], ff1[0:P, :]).then_inc(ff_raw, 16)
            for k in range(3):
                sp.dma_start(f1rawt[k * CT:(k + 1) * CT, :], ff1[P:C, :]).then_inc(ff_raw, 16)
            sp.dma_start(f2w[:, :, :], A["L1_xattn_ff_w2"].rearrange("(c p) n -> p c n", p=P)).then_inc(ff_raw, 16)
            with sp.Fori(1, PAIRS) as i:
                load_pair(i, 0)
            sp.wait_ge(at[0]["w"], 12 * PAIRS)
            sp.wait_ge(at[0]["wo"], PAIRS)
            load_pair(0, 1)
            with sp.Fori(1, PAIRS) as i:
                load_pair(i, 1)
            rows = out.rearrange("b (t p) c -> p (b t) c", p=P)
            for k, t in enumerate(range(0, NT, 3)):
                n = min(3, NT - t)
                sp.wait_ge(x_final, k + 1)
                sp.dma_start(rows[:, t:t + n, :], X[:, t:t + n, :]).then_inc(stored, 16)
            sp.wait_ge(stored, 16 * 3)

        @block.gpsimd
        def _(pool):
            steps = 0

            def hold(sem_, value):
                if isinstance(value, int) and value <= 0:
                    return
                pool.wait_ge(sem_, value)
                pool.sem_inc(pool_held, 1)

            def link(ins):
                nonlocal steps
                steps += 1
                ins.then_inc(pool_step, 1)
                pool.wait_ge(pool_step, steps)

            link(pool.memset(ident[:, :], 0.0))
            pool.affine_select(out=ident[:, :], in_=ident[:, :], compare_op=ALU.not_equal, fill=1.0,
                               base=0, pattern=[[-1, P]], channel_multiplier=1).then_inc(masks_ready, 1)
            pool.memset(wke[:, :, :, :, :], 0.0)
            pool.memset(wqe[:, :, :], 0.0)
            pool.memset(wqet[:, :, :], 0.0).then_inc(masks_ready, 1)
            pool.memset(cT4[:, :, :, :, :], 0.0).then_inc(pool_step, 1)
            pool.memset(bmask[:, :], 1.0).then_inc(pool_step, 1)
            steps += 2
            pool.wait_ge(pool_step, steps)
            bm = bmask[:, :].rearrange("p (h d) -> p h d", d=D0)
            link(pool.affine_select(out=bm, in_=bm, compare_op=ALU.is_ge, fill=0.0, base=0,
                                    pattern=[[-NIP, HEADS], [0, D0]], channel_multiplier=1))
            pool.affine_select(out=bm, in_=bm, compare_op=ALU.is_ge, fill=0.0, base=NIP - 1,
                               pattern=[[NIP, HEADS], [0, D0]], channel_multiplier=-1).then_inc(masks_ready, 1)
            taken(pool, "cT1")
            for c in range(EC):
                pool.tensor_copy(ipR[:, c, :, :, :], cT[:, c, :, TT:T].rearrange("p b (h n) -> p b h n", h=1)
                                 .broadcast_to([P, B, HEADS, NIP])).then_inc(ip_ready, 1)
            for c in range(EC):
                for b in range(B):
                    pool.tensor_copy(cT4[:, c, b, :, 0:TTAIL],
                                     cT[:, c, b, P:T].rearrange("p (j n) -> p j n", j=1)
                                     .broadcast_to([P, 4, TTAIL])).then_inc(ip_ready, 1)
            def split_weights(names, q, before):
                for n in names:
                    pool.tensor_copy(wh[n][:, :], raw[n][:, :]).then_inc(q["w"], 1)
                    pool.tensor_copy(w3[n][:, :], rawt[n][0:3 * CT, :]).then_inc(q["w"], 1)
                hold(q["w"], before + 2 * len(names))
                for n in names:
                    pool.tensor_tensor(wl[n][:, :], raw[n][:, :], wh[n][:, :].bitcast(F32), ALU.subtract)\
                        .then_inc(q["w"], 1)
                    r = slice(0, CT)
                    pool.tensor_tensor(w3[n][r, :], rawt[n][r, :], w3[n][r, :].bitcast(F32), ALU.subtract)\
                        .then_inc(q["w"], 1)

            q = at[0]

            def weights1(i):
                if inside(i, 0, 1, PAIRS):
                    hold(q["raw"], i * 192 + 192)
                    if not isinstance(i, int) or i > 0:
                        bk, n = shared(0, i - 1, 0, "v")
                        hold(q[f"misc{bk}"], n)
                    split_weights(("q", "k", "v"), q, i * 12)

            pool.memset(GVt[:, :, :, :, :], 0.0).then_inc(masks_ready, 1)
            pool.memset(KB0[:, 3:G4, :, :, :].bitcast(F32), 0.0).then_inc(masks_ready, 1)
            pool.memset(P0[:, :, :, TT:PW], 0.0).then_inc(masks_ready, 1)
            weights1(0)
            def queries0(i, n):
                if inside(i, 0, 1, QT):
                    if not isinstance(i, int) or i > 0:
                        hold(s0_ready, (i - 1) * STEPS0 + n + 1)
                    b, g = n // G4, n % G4
                    if isinstance(i, int) and i == 0:
                        taken(pool, f"Q0_{b}_{g}")
                    pool.tensor_copy(qs0[:, b, g, :], QT0[:, g, bass.ds(i * P + b * S, P)]).then_inc(q0_ready, 1)

            def tails0(i, k):
                if inside(i, k, STEPS0, QT * STEPS0):
                    hold(p0_ready, i * STEPS0 + k + 1)
                    hold(t0_ready, i * STEPS0 + k - 1)
                    pool.tensor_copy(P0t[:, k % 2, :, :], P0[:, k % 5, :, P:PW]).then_inc(p0t_ready, 1)

            def save0(i, b):
                if inside(i, 0, 1, QT):
                    hold(u0_taken, i * 2 * STEPS0 + 2 * (b + 1) * G4)
                    t = bass.ds(i + b * QT, 1)
                    pool.tensor_copy(sta[:, t, :, 0:1], st0[:, b:b + 1, :, 0:1]).then_inc(st0_saved, 1)
                    pool.tensor_copy(sta[:, t, :, 1:2], den0[:, b:b + 1, :].rearrange("p b (h o) -> p b h o", o=1))\
                        .then_inc(st0_saved, 1)
                    pool.tensor_copy(sta[:, t, :, 2:ST], st0[:, b:b + 1, :, 2:ST]).then_inc(st0_saved, 1)

            def first_block(i):
                for k in range(STEPS0):
                    tails0(i, k + 2)
                    if k == 0:
                        save0(i - 1, 1)
                    if k == 5:
                        save0(i, 0)
                    queries0(i + 1, k)

            for n in range(STEPS0):
                queries0(0, n)
            tails0(0, 0)
            tails0(0, 1)
            sweep(pool, QT, first_block)
            save0(QT - 1, 1)
            pool.wait_ge(loaded_small, 16 * SMALL)
            taken(pool, "x_t1")
            pool.tensor_tensor(X[:, :, :], X[:, :, :], brow[:, 0:1, :].broadcast_to([P, NT, C]), ALU.add)\
                .then_inc(bias_added, 1)
            taken(pool, "out_3")
            for t in (kL[:, :, :, :].bitcast(F32), vH[:, :, :, :, :].bitcast(F32), vL[:, :, :, :, :].bitcast(F32),
                      k2H[:, :, :, :].bitcast(F32), k2L[:, :, :, :].bitcast(F32), vZ2[:, :, :, :],
                      vZ2t[:, :, :, :], P2[:, :, :, T:PW]):
                pool.memset(t, 0.0).then_inc(zeroed, 1)

            def after_norm(k):
                pool.wait_ge(xn_ready, B * (k + 1))
                pool.tensor_tensor(X[:, :, :], X[:, :, :], brow[:, k + 1:k + 2, :].broadcast_to([P, NT, C]),
                                   ALU.add).then_inc(bias_added, 1)

            def spread(a, i, b):
                q = at[a]
                if not inside(i, 0, 1, PAIRS):
                    return
                hold(q["rden"], i * B + b + 1)
                if not (isinstance(i, int) and i * B + b == 0):
                    bk, n = shared(a, i, b + (0 if a == 0 else -1), "sums")
                    hold(q[f"misc{bk}"], n)
                pool.tensor_copy(rsp[:, :, :, :], rden[:, b, :, :].rearrange("p t (h o) -> p t h o", o=1)
                                 .broadcast_to([P, QT, 2, D1])).then_inc(q["rsp"], 1)

            after_norm(0)

            def self_attention(i):
                weights1(i + 1)
                spread(0, i, 0)
                spread(0, i, 1)

            sweep(pool, PAIRS, self_attention)

            r = at[1]

            def weights2(i):
                if inside(i, 0, 1, PAIRS):
                    hold(r["raw"], i * 128 + 128)
                    if not isinstance(i, int) or i > 0:
                        for kind in ("k", "q"):
                            bk, n = shared(1, i - 1, -1, kind)
                            hold(r[f"misc{bk}"], n)
                    for c, src in enumerate((raw, rawt)):
                        pool.tensor_copy(cwk[:, c, :], src["k"][:, :]).then_inc(r["w"], 1)
                    split_weights(("q",), r, i * 6 + 2)

            def value_weights2(i):
                if inside(i, 0, 1, PAIRS):
                    hold(r["raw"], i * 128 + 128)
                    if not isinstance(i, int) or i > 0:
                        bk, n = shared(1, i - 1, 0, "v")
                        hold(r[f"misc{bk}"], n)
                    for c, src in enumerate((raw, rawt)):
                        pool.tensor_copy(cwv[:, c, :], src["v"][:, :]).then_inc(r["wv"], 1)

            def tails2(i, k):
                if inside(i, k, 4, 4 * PAIRS):
                    hold(r["p"], i * 8 + 2 * k + 2)
                    hold(r["t"], i * 4 + k - 1)
                    pool.tensor_copy(P2t[:, k % 2, :, :], P2[:, k % 2, :, P:PW]).then_inc(r["pt"], 1)

            def cross_attention(i):
                weights2(i + 1)
                tails2(i, 2)
                spread(1, i, 0)
                value_weights2(i + 1)
                tails2(i, 3)
                tails2(i, 4)
                spread(1, i, 1)
                tails2(i, 5)

            bk, n = shared(0, PAIRS - 1, 0, "v")
            hold(q[f"misc{bk}"], n)
            weights2(0)
            value_weights2(0)
            pool.wait_ge(ff_raw, 16 * 5)
            hold(q["p"], 16 * PAIRS)
            pool.tensor_copy(f13[:, :], f1rawt[:, :]).then_inc(ff_w, 1)
            pool.tensor_copy(f1h[:, :], f1raw[:, :]).then_inc(ff_w, 1)
            pool.wait_ge(ff_w, 2)
            low = slice(0, CT)
            pool.tensor_tensor(f13[low, :], f1rawt[low, :], f13[low, :].bitcast(F32), ALU.subtract).then_inc(ff_w, 1)
            pool.tensor_tensor(f1l[:, :], f1raw[:, :], f1h[:, :].bitcast(F32), ALU.subtract).then_inc(ff_w, 1)
            tails2(0, 0)
            tails2(0, 1)
            after_norm(1)
            sweep(pool, PAIRS, cross_attention)
            after_norm(2)

        @block.scalar
        def _(act):
            def copy(out_, in_, **kw):
                return act.activation(out_, in_, ACT.Copy, **kw)

            act.wait_ge(square_ready, 1)
            act.activation(ips[:, 3:4], ips[:, 1:2], ACT.Sqrt).then_inc(root_ready, 1)
            for c in range(EC):
                copy(cT[:, c, :, :], made(act, f"cT{c}")[:, 0:B * T].rearrange("p (b t) -> p b t", b=B))\
                    .then_inc(by_act, 1)
            act.wait_ge(masks_ready, 2)
            act.wait_ge(loaded_w0, 16 * 8)
            for h in range(B):
                copy(nTm[:, h * S:(h + 1) * S], made(act, f"x_m{h}")).then_inc(by_act, 1)
            for dst, src in [(wke[:, k, c, :, 0:24], wkv0[:, k, c, :]) for k in range(2) for c in range(EC)] + [
                    (wqe[:, :, 0:24], wq0[:, :]), (wqet[:, :, 0:24], wq0t[:, :])]:
                rows = src.shape[0]
                copy(dst.rearrange("p h (r d) -> p h r d", r=3),
                     src.rearrange("p (h r d) -> p h r d", r=1, d=D0)
                     .broadcast_to([rows, HEADS, 3, D0])).then_inc(spread_ready, 1)
            for b in range(B):
                ps = made(act, f"GV_{b}")
                copy(GV[:, b, :, 0:P], ps[:, 0:P].rearrange("p (h t) -> p h t", h=1).broadcast_to([P, HEADS, P]))
                copy(GV[:, b, :, P:TT], ps[:, P:TT].rearrange("p (h t) -> p h t", h=1)
                     .broadcast_to([P, HEADS, TXTAIL]), scale=2.0)
                copy(GV[:, b, :, TT:TT + D0], ps[:, TT:TT + C].rearrange("p (h d) -> p h d", d=D0))
                copy(GV[:, b, :, TT + D0:RHS], ps[:, TT + C:TT + C + NIP].rearrange("p (h n) -> p h n", h=1)
                     .broadcast_to([P, HEADS, NIP])).then_inc(by_act, 1)

            halves = [u[0] for u in USES if u[0][:3] in ("K0_", "Q0_")]
            for n, name in enumerate(halves):
                if n == 2 * G4:
                    for b in range(B):
                        ps = made(act, f"VT_{b}")
                        copy(VT0[:, b, :], ps[:, 0:4 * HEADS])
                        copy(VT0t[:, b, :], ps[0:CT, 4 * HEADS:8 * HEADS]).then_inc(by_act, 1)
                    for b in range(B):
                        copy(VW0[:, b, :], made(act, f"VW_{b}")[0:4 * HEADS, 0:C]).then_inc(by_act, 1)
                if n >= 2:
                    taken(act, halves[n - 2])
                cols = B * T if name[0] == "K" else 512
                copy(hi0[:, n % 2, 0:cols], made(act, name)[:, 0:cols],
                     scale=1.0 if name[0] == "K" else D0 ** -0.5).then_inc(hi_ready, 1)

            def exps0(i, k):
                if not inside(i, k, STEPS0, QT * STEPS0):
                    return
                v, g = k // G4, k % G4
                reach(act, m0_ready, i * STEPS0 + k + 1)
                reach(act, u0_taken, i * 2 * STEPS0 + 2 * k - 8)
                if g == 0:
                    reach(act, st0_saved, i * 6 + 3 * v - 3)
                for j in range(4):
                    ins = act.activation(P0[:, k % 5, j, 0:TT],
                                         (bank01, bank23)[k % 2][:, j // 2, j % 2 * T:j % 2 * T + TT],
                                         ACT.Exp, bias=nmax0[:, k % 5, j:j + 1],
                                         accum_out=den0[:, v % B, 4 * g + j:4 * g + j + 1])
                ins.then_inc(p0_ready, 1)

            def evac0(i, k):
                if not inside(i, k, STEPS0, QT * STEPS0):
                    return
                reach(act, t0_ready, i * STEPS0 + k + 1)
                reach(act, u0_ready, i * 2 * STEPS0 + 2 * k - 2)
                copy(PT0[:, k % 2, :, :], bank45[:, 0, :].rearrange("p (j s) -> p j s", j=4))
                copy(PT0t[:, k % 2, :], bank45[:, 1, 0:P]).then_inc(pt0_ready, 1)

            def first_block(i):
                for k in range(STEPS0):
                    exps0(i, k + 2)
                    evac0(i, k + 1)

            exps0(0, 0)
            exps0(0, 1)
            evac0(0, 0)
            sweep(act, QT, first_block)
            act.wait_ge(square_ready, 2)
            act.activation(h1[:, :, :], h3[:, :, :], ACT.Sqrt).then_inc(root_ready, 1)
            for b in range(B):
                cols, t = slice(b * S, (b + 1) * S), slice(b * QT, (b + 1) * QT)
                copy(nTm[:, cols], made(act, f"TX_m{b}")).then_inc(by_act, 1)
                copy(nTt[0:CT, cols], made(act, f"TX_t{b}")[0:CT, :]).then_inc(by_act, 1)
                act.wait_ge(f_ready, b + 1)
                act.activation(f2[:, t, :, :], f1[:, t, :, :], ACT.Exp).then_inc(fe_ready, 1)
            for b in range(B):
                copy(FT[:, b * S:(b + 1) * S], made(act, f"F_{b}")[0:4 * HEADS, :]).then_inc(by_act, 1)

            def norm_root(n, b):
                act.wait_ge(square_ready, 2 + B * (n - 1) + b + 1)
                k = slice(b * QT, (b + 1) * QT)
                act.activation(root[:, k], var[:, k], ACT.Sqrt).then_inc(root_ready, 1)
                if b == B - 1:
                    act.activation(scrap[:, :], ident[:, 0:1], ACT.Exp if n < 3 else ACT.Gelu)

            def norm_tails(n, b):
                act.wait_ge(xn_ready, B * (n - 1) + b + 1)
                t = slice(b * QT, (b + 1) * QT)
                copy(XN[:, t, C:C + 2 * CT].rearrange("p t (r c) -> p t r c", r=2),
                     XN[:, t, P:C].rearrange("p t (r c) -> p t r c", r=1).broadcast_to([P, QT, 2, CT]))\
                    .then_inc(xn3_ready, 1)

            def norm_high(n, b):
                cols = slice(b * S, (b + 1) * S)
                if n == 1:
                    act.wait_ge(loaded_small, 16 * SMALL)
                for part, high, rows, c in (("m", nTh, P, 4 * n - 4), ("t", nT3, 3 * CT, 4 * n - 2)):
                    act.activation(high[0:rows, cols], made(act, f"n{n}_{part}{b}")[0:rows, :], ACT.Identity,
                                   scale=gcol[0:rows, c:c + 1], bias=gcol[0:rows, c + 1:c + 2])\
                        .then_inc(nh_ready, 1)

            def out_weights(a, i, v):
                q = at[a]
                reach(act, q["rawo"], i * 16 + 16)
                if not isinstance(i, int) or i > 0:
                    arrived(act, a, i, v, "outb")
                copy(wo[:, :], raw["o"][:, :]).then_inc(q["wo"], 1)

            def spread_sums(a, i, v):
                unit = i * B + v + (0 if a == 1 else -1)
                ps = arrived(act, a, i, v, "sums")
                reach(act, at[a]["o"], unit)
                take(a, "sums", copy(rbs[:, :], ps))

            for b in range(B):
                norm_root(1, b)
                norm_tails(1, b)
            for b in range(B):
                norm_high(1, b)
            q = at[0]

            def high1(i, v, kind):
                ahead = 2 if kind == "k" else 1
                if not inside(i, v + ahead, B, UNITS):
                    return
                b = (v + ahead) % B
                ps = arrived(act, 0, i, v, kind)
                if kind == "k":
                    copy(kS[0:64, b, 0, :], ps[0:64, :])
                    copy(kS[64:P, b, 1, :], ps[64:P, :]).then_inc(q["kh"], 1)
                elif kind == "q":
                    copy(qS[0:64, b, 0, :], ps[0:64, :], scale=D1 ** -0.5)
                    copy(qS[64:P, b, 1, :], ps[64:P, :], scale=D1 ** -0.5).then_inc(q["qh"], 1)
                else:
                    reach(act, q["pv"], i * 16 + 8 * v)
                    act.wait_ge(zeroed, 3)
                    ps = ps.rearrange("p (k d) -> p k d", k=KC)
                    copy(vH[:, b, 0, :, 0:64], ps[:, :, 0:64])
                    copy(vH[:, b, 1, :, 64:P], ps[:, :, 64:P]).then_inc(q["vh"], 1)

            def copy_keys(i, v, h):
                if not inside(i, v + 2, B, UNITS):
                    return
                b = v % B
                reach(act, q["kh"], i * B + v + 3)
                own, other = (slice(0, 64), slice(64, P)) if h == 0 else (slice(64, P), slice(0, 64))
                copy(kS[other, b, h, :], kS[own, b, h, :]).then_inc(q["kc"], 1)

            def exp1(i, k):
                if not inside(i, k, 16, 16 * PAIRS):
                    return
                reach(act, q["m"], i * 16 + k + 1)
                if k % 4 == 0:
                    reach(act, q["t"], i * 16 + k - 4)
                if k % 8 == 0:
                    reach(act, q["rden"], i * B + k // 8 - 1)
                act.activation(pr[:, k // 4 % 2, k % 4, :], bank[k % 2], ACT.Exp,
                               bias=nmax[:, k // 4 % 2, k % 4:k % 4 + 1],
                               accum_out=den[:, k // 8 % B, k % 4, k // 4 % 2:k // 4 % 2 + 1]).then_inc(q["p"], 1)

            def high_p(i, k):
                reach(act, q["t"], i * 16 + k + 1)
                reach(act, q["pv"], i * 16 + k - 3)
                copy(pH[:, k % 4, :], bank[2 + k % 2]).then_inc(q["ph"], 1)

            def self_attention(i):
                for k in range(16):
                    v, step = k // 8, k % 8
                    high_p(i, k)
                    if step in STEPS1:
                        high1(i, v, STEPS1[step])
                    if step == 7:
                        for h in range(2):
                            copy_keys(i, v, h)
                    if step == 2 and v == 1:
                        out_weights(0, i, 0)
                    if step == 3 and inside(i, v - 1, B, UNITS):
                        spread_sums(0, i, v)
                    exp1(i, k + 5)
                    if k == 15 and isinstance(i, int) and i == PAIRS - 1:
                        norm_root(2, 0)

            high1(0, -2, "k")
            copy_keys(0, -2, 0)
            copy_keys(0, -2, 1)
            high1(0, -1, "v")
            high1(0, -1, "q")
            exp1(0, 0)
            exp1(0, 1)
            for k in range(2, 5):
                exp1(0, k)
            high1(0, -1, "k")
            copy_keys(0, -1, 0)
            copy_keys(0, -1, 1)
            sweep(act, PAIRS, self_attention)
            norm_tails(2, 0)
            norm_high(2, 0)
            spread_sums(0, PAIRS, 0)
            norm_root(2, 1)

            r = at[1]

            def exps2(i, k):
                if not inside(i, k, 4, 4 * PAIRS):
                    return
                half = k % 2
                reach(act, r["t"], i * 4 + k - 1)
                if half == 0:
                    reach(act, r["rden"], i * B + k // 2 - 1)
                for j in range(2):
                    reach(act, r["m"], i * 8 + 2 * k + j + 1)
                    for h in range(2):
                        ins = act.activation(P2[:, k % 2, 2 * j + h, 0:T], bank[j][:, h * T:(h + 1) * T],
                                             ACT.Exp, bias=nmax2[:, k % 2, 2 * j + h:2 * j + h + 1],
                                             accum_out=den[:, k // 2 % B, 2 * half + j, h:h + 1])
                    ins.then_inc(r["p"], 1)

            def high2(i, v, kind):
                if not inside(i, v + 2, B, UNITS):
                    return
                b = v % B
                ps = arrived(act, 1, i, v, kind)
                if kind == "k":
                    copy(k2H[0:64, b, 0, :], ps[0:64, 0:T])
                    copy(k2H[64:P, b, 1, :], ps[64:P, 0:T]).then_inc(r["kh"], 1)
                else:
                    copy(q2H[:, b, :], ps, scale=D1 ** -0.5).then_inc(r["qh"], 1)

            def cross_attention(i):
                for k in range(4):
                    exps2(i, k + 2)
                    if k % 2:
                        high2(i, k // 2, "k")
                        high2(i, k // 2, "q")
                        if k == 1:
                            out_weights(1, i, 0)
                        spread_sums(1, i, k // 2)

            high2(0, -2, "k")
            high2(0, -2, "q")
            norm_tails(2, 1)
            norm_high(2, 1)
            exps2(0, 0)
            high2(0, -1, "k")
            high2(0, -1, "q")
            exps2(0, 1)
            sweep(act, PAIRS, cross_attention)
            for b in range(B):
                norm_root(3, b)
                norm_tails(3, b)
                norm_high(3, b)

            for c in range(FCH):
                for h in range(B):
                    reach(act, ff_g, c * B + h + 1)
                    reach(act, ff_hid, (c - 2) * B + h + 1)
                    act.activation(gel[:, c % 2, h * S:(h + 1) * S], bank[2 + h], ACT.Gelu,
                                   bias=b1col[:, FCH + c:FCH + c + 1]).then_inc(ff_gel, 1)

        @block.vector
        def _(dve):
            steps = 0

            def link(ins):
                nonlocal steps
                steps += 1
                ins.then_inc(dve_step, 1)
                dve.wait_ge(dve_step, steps)

            link(dve.memset(KB0[:, 0:3, :, :, :].bitcast(F32), 0.0))
            dve.wait_ge(loaded_ctx, 96)
            link(dve.tensor_tensor_reduce(out=ipj[:, :], in0=ipn[:, :], in1=ipn[:, :], scale=1.0, scalar=0.0,
                                          op0=ALU.mult, op1=ALU.add, accum_out=ips[:, 0:1]))
            dve.tensor_scalar(ips[:, 1:2], ips[:, 0:1], TINY, None, ALU.max).then_inc(square_ready, 1)
            dve.wait_ge(root_ready, 1)
            link(dve.tensor_scalar(ips[:, 1:2], ips[:, 3:4], EPS_NORM, None, ALU.max))
            link(dve.reciprocal(ips[:, 2:3], ips[:, 1:2]))
            dve.tensor_scalar(ipj[:, :], ipn[:, :], ips[:, 2:3], None, ALU.mult).then_inc(s_ipn, 1)
            dve.wait_ge(masks_ready, 1)
            heads = ident[:, :].rearrange("p (j r) -> p j r", j=4)
            link(dve.tensor_reduce(low_q[:, :], heads[:, :, 16:24], AX.XY, ALU.add))
            link(dve.tensor_reduce(low_k[:, :], heads[:, :, 8:16], AX.XY, ALU.add))
            dve.tensor_scalar(lows_q[:, :], low_q[:, :], D0 ** -0.5, None, ALU.mult).then_inc(dve_step, 1)
            steps += 1
            link(dve.tensor_scalar(sign_q[:, :], low_q[:, :], -2.0, 1.0, ALU.mult, ALU.add))
            link(dve.tensor_scalar(sign_k[:, :], low_k[:, :], -2.0, 1.0, ALU.mult, ALU.add))
            for h in range(B):
                dve.tensor_copy(nTt[0:CT, h * S:(h + 1) * S], made(dve, f"x_t{h}")[0:CT, :]).then_inc(by_dve, 1)
            dve.tensor_copy(ipT[:, :, :], made(dve, "ipT")[:, 0:EC * B * NIP].rearrange("p (c n) -> p c n", c=EC))\
                .then_inc(by_dve, 1)
            dve.wait_ge(masks_ready, 4)
            for b in range(B):
                ps = made(dve, f"GVt_{b}")
                for j in range(4):
                    r = slice(32 * j, 32 * j + 32)
                    dve.tensor_copy(GVt[r, b, :, j, 0:TXTAIL], ps[r, 0:TXTAIL].rearrange("p (g t) -> p g t", g=1)
                                    .broadcast_to([32, G4, TXTAIL]))
                    dve.tensor_copy(GVt[r, b, :, j, TXTAIL:TXTAIL + D0],
                                    ps[r, TXTAIL:TXTAIL + C].rearrange("p (g j d) -> p g j d", j=4, d=D0)[:, :, j, :])
                    ins = dve.tensor_copy(GVt[r, b, :, j, TXTAIL + D0:RHT],
                                          ps[r, TXTAIL + C:TXTAIL + C + NIP].rearrange("p (g n) -> p g n", g=1)
                                          .broadcast_to([32, G4, NIP]))
                ins.then_inc(by_dve, 1)
            for b in range(B):
                dve.tensor_tensor(VB0[:, b, :], made(dve, f"VB_{b}")[0:4 * HEADS, 0:C], bmask[:, :], ALU.mult)\
                    .then_inc(by_dve, 1)
            dve.wait_ge(masks_ready, 6)
            for n, (name, _) in enumerate([u for u in USES if u[0][:3] in ("K0_", "Q0_")]):
                ps = made(dve, name)
                dve.wait_ge(hi_ready, n + 1)
                g = int(name.split("_")[1])
                if name[0] == "K":
                    link(dve.tensor_scalar(tm0[:, n % 2, 0:B * T], hi0[:, n % 2, 0:B * T].bitcast(F32),
                                           sign_k[:, 0:1], None, ALU.mult))
                    for j in range(4):
                        r = slice(32 * j, 32 * j + 32)
                        ins = dve.scalar_tensor_tensor(
                            out=KB0[r, g, :, j, :], in0=ps[r, 0:B * T].rearrange("p (b t) -> p b t", b=B),
                            scalar=low_k[r, 0:1], in1=tm0[r, n % 2, 0:B * T].rearrange("p (b t) -> p b t", b=B),
                            op0=ALU.mult, op1=ALU.add)
                    ins.then_inc(by_dve, 1)
                else:
                    h, g = (int(v) for v in name.split("_")[1:])
                    link(dve.tensor_scalar(tm0[:, n % 2, :], hi0[:, n % 2, :].bitcast(F32), sign_q[:, 0:1], None,
                                           ALU.mult))
                    dve.scalar_tensor_tensor(out=QT0[:, g, h * S:(h + 1) * S], in0=ps, scalar=lows_q[:, 0:1],
                                             in1=tm0[:, n % 2, :], op0=ALU.mult, op1=ALU.add).then_inc(by_dve, 1)
            def max0(i, k):
                if not inside(i, k, STEPS0, QT * STEPS0):
                    return
                v, g = k // G4, k % G4
                sc = (bank01, bank23)[k % 2][:, :, 0:2 * T].rearrange("p k (j t) -> p k j t", j=2)
                reach(dve, s0_ready, i * STEPS0 + k + 1)
                if g == 0:
                    reach(dve, st0_saved, i * 6 + 3 * v - 3)
                dve.tensor_reduce(nmax0[:, k % 5, :].rearrange("p (k j) -> p k j", k=2), sc[:, :, :, 0:TT], AX.X,
                                  ALU.max, negate=True)
                dve.tensor_copy(st0[:, v % B, 4 * g:4 * g + 4, 2 + D0 + NIP:ST].rearrange("p (k j) n -> p k j n", k=2),
                                sc[:, :, :, TT:T]).then_inc(m0_ready, 1)

            def norms0(i, k):
                b, g = k // G4, k % G4
                for j in range(4):
                    if j % 2 == 0:
                        reach(dve, u0_ready, i * 2 * STEPS0 + 2 * k + j // 2 + 1)
                    u = bank67[:, j // 2, j % 2 * RHS:j % 2 * RHS + RHS]
                    dve.tensor_tensor_reduce(out=P0[:, k % 5, j, 0:TT], in0=u[:, 0:TT], in1=P0[:, k % 5, j, 0:TT],
                                             scale=1.0, scalar=0.0, op0=ALU.mult, op1=ALU.add,
                                             accum_out=st0[:, b, 4 * g + j, 0:1])
                    if j % 2:
                        h = 4 * g + j - 1
                        dve.tensor_copy(st0[:, b, h:h + 2, 2:2 + D0 + NIP],
                                        bank67[:, j // 2, 0:2 * RHS].rearrange("p (j t) -> p j t", j=2)[:, :, TT:RHS])\
                            .then_inc(u0_taken, 1)

            def first_block(i):
                for k in range(STEPS0):
                    max0(i, k + 3)
                    norms0(i, k)

            max0(0, 0)
            max0(0, 1)
            max0(0, 2)
            sweep(dve, QT, first_block)
            reach(dve, st0_saved, 6 * QT)
            sq, sums = sta[:, :, :, 0], sta[:, :, :, 1]
            text, dots, simg = sta[:, :, :, 2:2 + D0], sta[:, :, :, 2 + D0:2 + D0 + NIP], sta[:, :, :, 2 + D0 + NIP:ST]

            dve.tensor_scalar(h3[:, :, :], sq, TINY, None, ALU.max).then_inc(square_ready, 1)
            link(dve.reciprocal(h2[:, :, :], sums))
            batches = [slice(b * QT, (b + 1) * QT) for b in range(B)]

            def wide(t, k, n):
                return t[:, k, :].rearrange("p t (h o) -> p t h o", o=1).broadcast_to([P, QT, HEADS, n])

            for k in batches:
                dve.tensor_tensor(TX[:, k, :, :], text[:, k], wide(h2, k, D0), ALU.mult).then_inc(tx_ready, 1)
            dve.wait_ge(root_ready, 2)
            dve.wait_ge(tx_ready, B)
            link(dve.scalar_tensor_tensor(out=h2[:, :, :], in0=sums, scalar=EPS_NORM, in1=h1[:, :, :],
                                          op0=ALU.mult, op1=ALU.max))
            link(dve.reciprocal(h1[:, :, :], h2[:, :, :]))
            for k in batches:
                link(dve.tensor_tensor(f1[:, k, :, :], dots[:, k], wide(h1, k, NIP), ALU.mult))
                link(dve.scalar_tensor_tensor(out=f2[:, k, :, :], in0=f1[:, k, :, :], scalar=SEM_SCALE,
                                              in1=simg[:, k], op0=ALU.mult, op1=ALU.add))
                link(dve.tensor_reduce(h2[:, k, :], f2[:, k, :, :], AX.X, ALU.max))
                dve.tensor_tensor(f1[:, k, :, :], f2[:, k, :, :], wide(h2, k, NIP), ALU.subtract).then_inc(f_ready, 1)
            dve.wait_ge(loaded_small, 16 * SMALL)
            for b, k in enumerate(batches):
                dve.wait_ge(fe_ready, b + 1)
                link(dve.tensor_reduce(h1[:, k, :], f2[:, k, :, :], AX.X, ALU.add))
                link(dve.reciprocal(h2[:, k, :], h1[:, k, :]))
                link(dve.tensor_tensor(h3[:, k, :], h2[:, k, :], smask[:, :].rearrange("p (t o) -> p t o", o=1)
                                       .broadcast_to([P, QT, HEADS]), ALU.mult))
                dve.tensor_tensor(f1[:, k, :, :], f2[:, k, :, :], wide(h3, k, NIP), ALU.mult).then_inc(fn_ready, 1)
            dve.wait_ge(bias_added, 1)
            for k in range(4):
                dve.tensor_tensor(X[:, 2 * k:2 * k + 2, :], X[:, 2 * k:2 * k + 2, :],
                                  made(dve, f"out_{k}")[:, 0:2 * C].rearrange("p (t c) -> p t c", t=2), ALU.add)\
                    .then_inc(by_dve, 1)
            taken(dve, "out_3")

            def norm_rows(n, b):
                nonlocal steps
                tiles = range(b * QT, (b + 1) * QT)
                k = slice(b * QT, (b + 1) * QT)
                for t in tiles:
                    dve.bn_stats(bn6[:, t, :], X[:, t, :]).then_inc(dve_step, 1)
                for m, t in enumerate(tiles):
                    dve.wait_ge(dve_step, steps + m + 1)
                    dve.bn_aggr(mv[:, t, :], bn6[:, t, :]).then_inc(dve_step, 1)
                steps += 2 * QT
                dve.wait_ge(dve_step, steps)
                dve.tensor_scalar(var[:, k], mv[:, k, 1], EPS_LN, None, ALU.add).then_inc(square_ready, 1)
                dve.wait_ge(root_ready, 2 + B * (n - 1) + b + 1)
                link(dve.reciprocal(rstd[:, k], root[:, k]))
                for t in tiles:
                    ins = dve.tensor_scalar(XN[:, t, 0:C], X[:, t, :], mv[:, t, 0:1], rstd[:, t:t + 1],
                                            ALU.subtract, ALU.mult)
                ins.then_inc(xn_ready, 1)

            def norm_split(n, b):
                low = slice(2 * CT, 3 * CT)
                cols = slice(b * S, (b + 1) * S)
                for m, (part, full, high, dst, rows) in enumerate((("m", nTm, nTh, nTl, slice(0, P)),
                                                                   ("t", nTt, nT3, nT3, low))):
                    ps = made(dve, f"n{n}_{part}{b}")
                    c = 4 * n - 4 + 2 * m
                    dve.wait_ge(nh_ready, 4 * (n - 1) + 2 * b + m + 1)
                    dve.tensor_scalar(full[rows, cols], ps[rows, :], gcol[rows, c:c + 1],
                                      gcol[rows, c + 1:c + 2], ALU.mult, ALU.add).then_inc(by_dve, 1)
                    taken(dve, f"n{n}_{part}{b}")
                    dve.tensor_tensor(dst[rows, cols], full[rows, cols], high[rows, cols].bitcast(F32),
                                      ALU.subtract).then_inc(nl_ready, 1)

            def add_out(a, i, v, half):
                kind = ("outa", "outb")[half]
                if not inside(i, v - 1, B, UNITS):
                    return
                t = (v - 1) % B * QT + 2 * half
                take(a, kind, dve.tensor_tensor(X[:, t:t + 2, :], X[:, t:t + 2, :],
                                                arrived(dve, a, i, v, kind)[:, 0:2 * C]
                                                .rearrange("p (t c) -> p t c", t=2), ALU.add))

            def inverse_sums(a, i, v):
                q = at[a]
                per = 16 if a == 0 else 8
                reach(dve, q["p"], i * per + per // 2 * (v + 1))
                reach(dve, q["rsp"], i * B + v - 1)
                dve.reciprocal(rden[:, v, :, :], den[:, v, :, :]).then_inc(q["rden"], 1)

            for b in range(B):
                norm_rows(1, b)
            for b in range(B):
                norm_split(1, b)
            q = at[0]

            def low1(i, v, kind):
                ahead = 2 if kind == "k" else 1
                if not inside(i, v + ahead, B, UNITS):
                    return
                b = (v + ahead) % B
                ps = arrived(dve, 0, i, v, kind)
                reach(dve, q[kind + "h"], i * B + v + ahead + 1)
                if kind == "k":
                    dve.wait_ge(zeroed, 1)
                    dve.tensor_tensor(kL[0:64, b, 0, :], ps[0:64, :], kS[0:64, b, 0, :].bitcast(F32), ALU.subtract)
                    ins = dve.tensor_tensor(kL[64:P, b, 1, :], ps[64:P, :], kS[64:P, b, 1, :].bitcast(F32),
                                            ALU.subtract)
                elif kind == "q":
                    dve.scalar_tensor_tensor(out=qS[64:P, b, 0, :], in0=ps[0:64, :], scalar=D1 ** -0.5,
                                             in1=qS[0:64, b, 0, :].bitcast(F32), op0=ALU.mult, op1=ALU.subtract)
                    ins = dve.scalar_tensor_tensor(out=qS[0:64, b, 1, :], in0=ps[64:P, :], scalar=D1 ** -0.5,
                                                   in1=qS[64:P, b, 1, :].bitcast(F32), op0=ALU.mult,
                                                   op1=ALU.subtract)
                else:
                    ps = ps.rearrange("p (k d) -> p k d", k=KC)
                    for h in range(2):
                        c = slice(64 * h, 64 * h + 64)
                        ins = dve.tensor_tensor(vL[:, b, h, :, c], ps[:, :, c], vH[:, b, h, :, c].bitcast(F32),
                                                ALU.subtract)
                take(0, kind, ins)

            def max1(i, k):
                if not inside(i, k, 16, 16 * PAIRS):
                    return
                reach(dve, q["s"], i * 16 + k + 1)
                dve.tensor_reduce(nmax[:, k // 4 % 2, k % 4:k % 4 + 1], bank[k % 2], AX.X, ALU.max, negate=True)\
                    .then_inc(q["m"], 1)

            def low_p(i, k):
                reach(dve, q["ph"], i * 16 + k + 1)
                dve.tensor_tensor(pL[:, k % 4, :], bank[2 + k % 2], pH[:, k % 4, :].bitcast(F32), ALU.subtract)\
                    .then_inc(q["pd"], 1)

            def scale_out1(i, v):
                if not inside(i, v - 1, B, UNITS):
                    return
                gone(dve, 0, i, v, "sums")
                reach(dve, q["pv"], i * 16 + 8 * v)
                b = (v - 1) % B
                dve.tensor_tensor(oT[:, b, :], bank[4 + b], rbs[:, :], ALU.mult).then_inc(q["o"], 1)

            def self_attention(i):
                for k in range(16):
                    v, step = k // 8, k % 8
                    max1(i, k + 5)
                    low_p(i, k)
                    if step in STEPS1:
                        low1(i, v, STEPS1[step])
                    if step == 4:
                        scale_out1(i, v)
                        inverse_sums(0, i, v)
                    if step in (5, 7):
                        add_out(0, i, v, step // 7)
                    if k == 15 and isinstance(i, int) and i == PAIRS - 1:
                        for kind in ("outa", "outb"):
                            gone(dve, 0, i, 1, kind)
                        norm_rows(2, 0)

            low1(0, -2, "k")
            low1(0, -1, "v")
            low1(0, -1, "q")
            max1(0, 0)
            max1(0, 1)
            dve.wait_ge(bias_added, 2)
            for k in range(2, 5):
                max1(0, k)
            low1(0, -1, "k")
            sweep(dve, PAIRS, self_attention)
            norm_split(2, 0)
            scale_out1(PAIRS, 0)
            add_out(0, PAIRS, 0, 0)
            add_out(0, PAIRS, 0, 1)
            gone(dve, 0, PAIRS, 0, "outa")
            gone(dve, 0, PAIRS, 0, "outb")
            norm_rows(2, 1)

            r = at[1]

            def max2(i, k):
                if not inside(i, k, 4, 4 * PAIRS):
                    return
                for j in range(2):
                    reach(dve, r["s"], i * 8 + 2 * k + j + 1)
                    dve.tensor_reduce(nmax2[:, k % 2, 2 * j:2 * j + 2],
                                      bank[j][:, 0:2 * T].rearrange("p (h t) -> p h t", h=2),
                                      AX.X, ALU.max, negate=True).then_inc(r["m"], 1)

            def evac2(i, k):
                if not inside(i, k, 4, 4 * PAIRS):
                    return
                reach(dve, r["t"], i * 4 + k + 1)
                reach(dve, r["pv"], i * 4 + k - 1)
                dve.tensor_copy(P2T[:, k % 2, :, :], bank[2 + k % 2].rearrange("p (j s) -> p j s", j=4))
                dve.tensor_copy(P2Tt[:, k % 2, :], bank[4][:, 0:P]).then_inc(r["pd"], 1)

            def values2(i, v):
                if not inside(i, v + 1, B, UNITS):
                    return
                b = (v + 1) % B
                ps = arrived(dve, 1, i, v, "v")
                reach(dve, r["pv"], i * 4 + 2 * v)
                for h in range(2):
                    dve.tensor_copy(vZ2[:, b, h, 64 * h:64 * h + 64], ps[:, 64 * h:64 * h + 64])
                for j in range(2):
                    for h in range(2):
                        rows = slice(64 * j + 32 * h, 64 * j + 32 * h + 32)
                        ins = dve.tensor_copy(vZ2t[rows, b, j, 64 * h:64 * h + 64],
                                              ps[rows, P + 64 * h:P + 64 * h + 64])
                take(1, "v", ins)

            def low2(i, v, kind):
                if not inside(i, v + 2, B, UNITS):
                    return
                b = v % B
                ps = arrived(dve, 1, i, v, kind)
                reach(dve, r[kind + "h"], i * B + v + 3)
                if kind == "k":
                    dve.tensor_tensor(k2L[0:64, b, 0, :], ps[0:64, 0:T], k2H[0:64, b, 0, :].bitcast(F32),
                                      ALU.subtract)
                    ins = dve.tensor_tensor(k2L[64:P, b, 1, :], ps[64:P, 0:T], k2H[64:P, b, 1, :].bitcast(F32),
                                            ALU.subtract)
                else:
                    ins = dve.scalar_tensor_tensor(out=q2L[:, b, :], in0=ps, scalar=D1 ** -0.5,
                                                   in1=q2H[:, b, :].bitcast(F32), op0=ALU.mult, op1=ALU.subtract)
                take(1, kind, ins)

            def scale_out2(i, v):
                gone(dve, 1, i, v, "sums")
                reach(dve, r["pv"], i * 4 + 2 * v + 2)
                dve.tensor_tensor(oT[:, v, :], bank[5], rbs[:, :], ALU.mult).then_inc(r["o"], 1)

            def cross_attention(i):
                for k in range(4):
                    v = k // 2
                    max2(i, k + 2)
                    evac2(i, k + 1)
                    if k % 2 == 0:
                        values2(i, v)
                        inverse_sums(1, i, v)
                        add_out(1, i, v, 0)
                        add_out(1, i, v, 1)
                    else:
                        low2(i, v, "k")
                        low2(i, v, "q")
                        scale_out2(i, v)

            low2(0, -2, "k")
            low2(0, -2, "q")
            values2(0, -1)
            max2(0, 0)
            norm_split(2, 1)
            low2(0, -1, "k")
            low2(0, -1, "q")
            max2(0, 1)
            evac2(0, 0)
            dve.wait_ge(bias_added, 3)
            sweep(dve, PAIRS, cross_attention)
            gone(dve, 1, PAIRS - 1, 1, "outa")
            gone(dve, 1, PAIRS - 1, 1, "outb")
            norm_rows(3, 0)
            add_out(1, PAIRS, 0, 0)
            add_out(1, PAIRS, 0, 1)
            gone(dve, 1, PAIRS, 0, "outb")
            gone(dve, 1, PAIRS, 0, "outa")
            norm_rows(3, 1)
            for b in range(B):
                norm_split(3, b)

            dve.wait_ge(bias_added, 4)
            for c in range(FCH):
                for h in range(B):
                    reach(dve, ff_a, c * B + h + 1)
                    reach(dve, ff_gel, c * B + h + 1)
                    reach(dve, ff_out, (c - 2) * B + h + 1)
                    cols = slice(h * S, (h + 1) * S)
                    dve.scalar_tensor_tensor(out=hid[:, c % 2, cols], in0=bank[h], scalar=b1col[:, c:c + 1],
                                             in1=gel[:, c % 2, cols], op0=ALU.add, op1=ALU.mult).then_inc(ff_hid, 1)
            for k, t in enumerate(range(0, NT, 3)):
                n = min(3, NT - t)
                reach(dve, ff_out, (FCH - 1) * B + (t + n - 1) // QT + 1)
                dve.tensor_tensor(X[:, t:t + n, :], X[:, t:t + n, :],
                                  bank[4 + k][:, 0:n * C].rearrange("p (t c) -> p t c", t=n), ALU.add)\
                    .then_inc(x_final, 1)

        @block.tensor
        def _(pe):
            def done(ins):
                ins.then_inc(ps_ready, 1)

            pe.wait_ge(masks_ready, 1)
            pe.wait_ge(loaded_ctx, 96)
            for c in range(EC):
                ps = make(pe, f"cT{c}")
                for b in range(B):
                    pe.transpose(ps[:, b * T:b * T + P], cm[:, b, c * P:(c + 1) * P], ident[:, :])
                    ins = pe.transpose(ps[:, b * T + P:(b + 1) * T], ct[:, b, c * P:(c + 1) * P],
                                       ident[0:TTAIL, 0:TTAIL])
                done(ins)
            def turn(src, kind):
                for part, cols in (("m", slice(0, P)), ("t", slice(P, C))):
                    for h in range(B):
                        ps = make(pe, f"{kind}_{part}{h}")
                        for t in range(QT):
                            ins = pe.transpose(ps[0:cols.stop - cols.start, t * P:(t + 1) * P],
                                               src[:, h * QT + t, cols], ident[:, :])
                        done(ins)

            pe.wait_ge(loaded_x, 16)
            turn(X, "x")
            pe.wait_ge(s_ipn, 1)
            ps = make(pe, "ipT")
            for c in range(EC):
                ins = pe.transpose(ps[:, c * 8:(c + 1) * 8], ipj[:, c * P:(c + 1) * P], ident[0:8, 0:8])
            done(ins)
            pe.wait_ge(loaded_w0, 16 * 8)
            pe.wait_ge(ip_ready, EC + EC * B)
            taken(pe, "ipT")
            for tail in range(2):
                for b in range(B):
                    ps = make(pe, f"GVt_{b}" if tail else f"GV_{b}")
                    at_ = 0
                    lo = P if tail else 0
                    for width, rhs in ((TT - lo, lambda c: cT[:, c, b, lo:TT]), (C, lambda c: wkv0[:, 2, c, :]),
                                       (NIP, lambda c: ipT[:, c, b * NIP:(b + 1) * NIP])):
                        for c in range(EC):
                            lhs = cT4[:, c, b, :, :] if tail else cT[:, c, b, 0:P]
                            ins = pe.matmul(ps[:, at_:at_ + width], lhs, rhs(c), start=(c == 0), stop=(c == EC - 1))
                        at_ += width
                    done(ins)
            for b in range(B):
                ps = make(pe, f"VB_{b}")
                for c in range(EC):
                    ins = pe.matmul(ps[0:4 * HEADS, 0:C], ipR[:, c, b, :, :], wkv0[:, 3, c, :],
                                    start=(c == 0), stop=(c == EC - 1))
                done(ins)
            pe.wait_ge(spread_ready, 6)
            taken(pe, "x_m1")
            taken(pe, "x_t1")

            def keys0(g):
                ps = make(pe, f"K0_{g}")[:, 0:B * T].rearrange("p (b t) -> p b t", b=B)
                for k, cols in ((0, slice(0, TT)), (1, slice(TT, T))):
                    for c in range(EC):
                        ins = pe.matmul(ps[:, :, cols], wke[:, k, c, 4 * g:4 * g + 4, :], cT[:, c, :, cols],
                                        start=(c == 0), stop=(c == EC - 1))
                done(ins)

            def rows0(b, g):
                cols = slice(b * S, (b + 1) * S)
                ps = make(pe, f"Q0_{b}_{g}")
                pe.matmul(ps, wqe[:, 4 * g:4 * g + 4, :], nTm[:, cols], start=True, stop=False)
                done(pe.matmul(ps, wqet[:, 4 * g:4 * g + 4, :], nTt[0:CT, cols], start=False, stop=True))

            for g in range(G4):
                keys0(g)
                rows0(0, g)
            for b in range(B):
                ps = make(pe, f"VT_{b}")
                taken(pe, f"VB_{b}")
                pe.transpose(ps[:, 0:4 * HEADS], VB0[:, b, 0:P], ident[0:4 * HEADS, 0:4 * HEADS])
                done(pe.transpose(ps[0:CT, 4 * HEADS:8 * HEADS], VB0[:, b, P:C], ident[0:4 * HEADS, 0:4 * HEADS]))
            for b in range(B):
                ps = make(pe, f"VW_{b}")
                taken(pe, f"VT_{b}")
                pe.matmul(ps[0:4 * HEADS, 0:C], VT0[:, b, :], wo0[:, :], start=True, stop=False)
                done(pe.matmul(ps[0:4 * HEADS, 0:C], VT0t[:, b, :], wo0t[:, :], start=False, stop=True))
            for g in range(G4):
                rows0(1, g)

            def vacated(*banks):
                for k in banks:
                    taken(pe, USES[max(n for n in range(index["TX_m0"]) if n % 8 == k)][0])

            def scores0(i, k):
                if not inside(i, k, STEPS0, QT * STEPS0):
                    return
                v, g = k // G4, k % G4
                reach(pe, q0_ready, i * STEPS0 + k + 1)
                reach(pe, p0_ready, i * STEPS0 + k - 1)
                sc = (bank01, bank23)[k % 2]
                for j in range(2):
                    ins = pe.matmul(sc[:, j, 0:2 * T], qs0[:, v % B, g, :], KB0[:, g, v % B, 2 * j:2 * j + 2, :],
                                    start=True, stop=True)
                ins.then_inc(s0_ready, 1)

            def turn0(i, k):
                if not inside(i, k, STEPS0, QT * STEPS0):
                    return
                reach(pe, p0_ready, i * STEPS0 + k + 1)
                reach(pe, pt0_ready, i * STEPS0 + k)
                for j in range(4):
                    pe.transpose(bank45[:, 0, j * P:(j + 1) * P], P0[:, k % 5, j, 0:P], ident[:, :])
                reach(pe, p0t_ready, i * STEPS0 + k + 1)
                pe.transpose(bank45[:, 1, 0:P], P0t[:, k % 2, :, :], ident[:, :]).then_inc(t0_ready, 1)

            def mix0(i, n):
                b, g = n // G4, n % G4
                reach(pe, pt0_ready, i * STEPS0 + n + 1)
                for k in range(2):
                    reach(pe, u0_taken, i * 2 * STEPS0 + 2 * n + k - 1)
                    for j in range(2):
                        pe.matmul(bank67[:, k, j * RHS:(j + 1) * RHS], PT0[:, n % 2, 2 * k + j, :],
                                  GV[:, b, 4 * g + 2 * k + j, :], start=(j == 0), stop=False, skip_group_check=True)
                    ins = pe.matmul(bank67[:, k, 0:2 * RHS].rearrange("p (j t) -> p j t", j=2)[:, :, P:RHS],
                                    PT0t[:, n % 2, :], GVt[:, b, g, 2 * k:2 * k + 2, :], start=False, stop=True,
                                    skip_group_check=True)
                    ins.then_inc(u0_ready, 1)

            def first_block(i):
                for k in range(STEPS0):
                    scores0(i, k + 3)
                    turn0(i, k + 1)
                    mix0(i, k)

            vacated(0, 1)
            scores0(0, 0)
            vacated(2, 3)
            scores0(0, 1)
            scores0(0, 2)
            vacated(4, 5)
            turn0(0, 0)
            vacated(6, 7)
            sweep(pe, QT, first_block)
            for b in range(B):
                pe.wait_ge(tx_ready, b + 1)
                for part, lo, hi in (("m", 0, P), ("t", P, C)):
                    ps = make(pe, f"TX_{part}{b}")
                    for t in range(QT):
                        tx = TX[:, b * QT + t, :, :].rearrange("p h d -> p (h d)")
                        ins = pe.transpose(ps[0:hi - lo, t * P:(t + 1) * P], tx[:, lo:hi], ident[:, :])
                    done(ins)
            outs = []
            for k in range(4):
                ps = make(pe, f"out_{k}")
                outs.append(ps)
                taken(pe, f"TX_t{k // 2}")
                for j in range(2):
                    t, o = slice((2 * k + j) * P, (2 * k + j + 1) * P), ps[:, j * C:(j + 1) * C]
                    pe.matmul(o, nTm[:, t], wo0[:, :], start=(j == 0), stop=False, skip_group_check=True)
                    pe.matmul(o, nTt[0:CT, t], wo0t[:, :], start=False, stop=False, skip_group_check=True)
            for b in range(B):
                pe.wait_ge(fn_ready, b + 1)
                ps = make(pe, f"F_{b}")
                for t in range(QT):
                    ins = pe.transpose(ps[0:4 * HEADS, t * P:(t + 1) * P],
                                       f1[:, b * QT + t, :, :].rearrange("p h n -> p (h n)"), ident[:, :])
                done(ins)
            for k in range(4):
                taken(pe, f"F_{k // 2}")
                for j in range(2):
                    t = slice((2 * k + j) * P, (2 * k + j + 1) * P)
                    ins = pe.matmul(outs[k][:, j * C:(j + 1) * C], FT[:, t], VW0[:, k // 2, :], start=False,
                                    stop=True, skip_group_check=True)
                done(ins)

            def turn_norm(n, b):
                for part, cols in (("m", slice(0, P)), ("t", slice(P, C + 2 * CT))):
                    ps = make(pe, f"n{n}_{part}{b}")
                    pe.wait_ge(xn_ready if part == "m" else xn3_ready, B * (n - 1) + b + 1)
                    for t in range(QT):
                        ins = pe.transpose(ps[0:cols.stop - cols.start, t * P:(t + 1) * P],
                                           XN[:, b * QT + t, cols], ident[:, :])
                    done(ins)

            def turned(n, b):
                taken(pe, f"n{n}_t{b}")
                pe.wait_ge(nl_ready, 4 * (n - 1) + 2 * (b + 1))

            def by_weights(ps, high, low, third, cols):
                pe.matmul(ps, high, nTh[:, cols], start=True, stop=False)
                pe.matmul(ps, low, nTh[:, cols], start=False, stop=False)
                pe.matmul(ps, high, nTl[:, cols], start=False, stop=False)
                return pe.matmul(ps, third, nT3[:, cols], start=False, stop=True)

            def spread_sums(a, i, v):
                ps = use(pe, a, i, v, "sums")
                reach(pe, at[a]["rsp"], i * B + v + (0 if a == 0 else 1))
                for t in range(QT):
                    ins = pe.transpose(ps[:, t * P:(t + 1) * P], rsp[:, t, :, :], ident[:, :])
                finish(a, "sums", ins)

            def project(a, i, v, half):
                if not inside(i, v - 1, B, UNITS):
                    return
                kind, b = ("outa", "outb")[half], (v - 1) % B
                ps = use(pe, a, i, v, kind)
                reach(pe, at[a]["o"], i * B + v)
                if v == 1:
                    reach(pe, at[a]["wo"], i + 1)
                for j in range(2):
                    t = 2 * half + j
                    ins = pe.matmul(ps[:, j * C:(j + 1) * C], oT[:, b, t * P:(t + 1) * P], wo[:, :],
                                    start=True, stop=True)
                finish(a, kind, ins)

            for b in range(B):
                turn_norm(1, b)
            turned(1, 0)
            q = at[0]

            def inputs1(i, v, kind):
                ahead = 2 if kind == "k" else 1
                if not inside(i, v + ahead, B, UNITS):
                    return
                b = (v + ahead) % B
                if kind == "k" and b == 0:
                    reach(pe, q["w"], (i + (v + 2) // 2) * 12 + 12)
                ps = use(pe, 0, i, v, kind)
                if kind != "v":
                    ins = by_weights(ps, wh[kind][:, :], wl[kind][:, :], w3[kind][:, :], slice(b * S, (b + 1) * S))
                else:
                    for k in range(KC):
                        o, cols = ps[:, k * P:(k + 1) * P], slice(b * S + k * P, b * S + (k + 1) * P)
                        pe.matmul(o, nTh[:, cols], wh["v"][:, :], start=(k == 0), stop=False, skip_group_check=True)
                        pe.matmul(o, nTh[:, cols], wl["v"][:, :], start=False, stop=False, skip_group_check=True)
                        pe.matmul(o, nTl[:, cols], wh["v"][:, :], start=False, stop=False, skip_group_check=True)
                        ins = pe.matmul(o, nT3[:, cols], w3["v"][:, :], start=False, stop=True,
                                        skip_group_check=True)
                finish(0, kind, ins)

            def scores1(i, k):
                if not inside(i, k, 16, 16 * PAIRS):
                    return
                b, h, j = k // 8 % B, k // 4 % 2, k % 4
                if k % 8 == 0:
                    v = k // 8
                    gone(pe, 0, i, v - 2, "k")
                    gone(pe, 0, i, v - 1, "q")
                    reach(pe, q["kc"], i * 4 + 2 * v + 2)
                reach(pe, q["p"], i * 16 + k - 1)
                for keys in (kS, kL):
                    ins = pe.matmul(bank[k % 2], qS[:, b, h, j * P:(j + 1) * P], keys[:, b, h, :],
                                    start=(keys is kS), stop=(keys is kL))
                ins.then_inc(q["s"], 1)

            def turn1(i, k):
                if k % 4 == 0:
                    reach(pe, q["p"], i * 16 + k + 4)
                reach(pe, q["pd"], i * 16 + k - 1)
                for t in range(QT):
                    ins = pe.transpose(bank[2 + k % 2][:, t * P:(t + 1) * P],
                                       pr[:, k // 4 % 2, t, k % 4 * P:(k % 4 + 1) * P], ident[:, :])
                ins.then_inc(q["t"], 1)

            def mix1(i, k):
                if not inside(i, k, 16, 16 * PAIRS):
                    return
                b, h, j = k // 8 % B, k // 4 % 2, k % 4
                if k % 8 == 0:
                    reach(pe, q["o"], i * B + k // 8 - 1)
                    gone(pe, 0, i, k // 8 - 1, "v")
                reach(pe, q["pd"], i * 16 + k + 1)
                o = bank[4 + b]
                pe.matmul(o, vH[:, b, h, j, :], pH[:, k % 4, :], start=(k % 8 == 0), stop=False)
                pe.matmul(o, vL[:, b, h, j, :], pH[:, k % 4, :], start=False, stop=False)
                pe.matmul(o, vH[:, b, h, j, :], pL[:, k % 4, :], start=False, stop=(k % 8 == 7))\
                    .then_inc(q["pv"], 1)

            def self_attention(i):
                for k in range(16):
                    v, step = k // 8, k % 8
                    scores1(i, k + 5)
                    turn1(i, k)
                    mix1(i, k - 2)
                    if step in STEPS1:
                        inputs1(i, v, STEPS1[step])
                    if step == 3 and inside(i, v - 1, B, UNITS):
                        spread_sums(0, i, v)
                    if step in (5, 7):
                        project(0, i, v, step // 7)

            inputs1(0, -2, "k")
            inputs1(0, -1, "v")
            inputs1(0, -1, "q")
            turned(1, 1)
            scores1(0, 0)
            scores1(0, 1)
            for k in range(2, 5):
                scores1(0, k)
            inputs1(0, -1, "k")
            sweep(pe, PAIRS, self_attention)
            mix1(PAIRS - 1, 14)
            turn_norm(2, 0)
            mix1(PAIRS - 1, 15)
            spread_sums(0, PAIRS, 0)
            project(0, PAIRS, 0, 0)
            project(0, PAIRS, 0, 1)

            gone(pe, 0, PAIRS, 0, "outa")
            gone(pe, 0, PAIRS, 0, "outb")
            turned(2, 0)
            r = at[1]

            def keys_queries2(i, v, kind):
                if not inside(i, v + 2, B, UNITS):
                    return
                b = v % B
                if kind == "k" and b == 0:
                    reach(pe, r["w"], (i + (v + 2) // 2) * 6 + 6)
                ps = use(pe, 1, i, v, kind)
                if kind == "k":
                    for c in range(EC):
                        ins = pe.matmul(ps[:, 0:T], cwk[:, c, :], cT[:, c, b, :], start=(c == 0), stop=(c == EC - 1))
                else:
                    ins = by_weights(ps, wh["q"][:, :], wl["q"][:, :], w3["q"][:, :], slice(b * S, (b + 1) * S))
                finish(1, kind, ins)

            def values2(i, v):
                if not inside(i, v + 1, B, UNITS):
                    return
                b = (v + 1) % B
                if b == 0:
                    reach(pe, r["wv"], (i + (v + 1) // 2) * 2 + 2)
                ps = use(pe, 1, i, v, "v")
                for tail in range(2):
                    for c in range(EC):
                        lhs = cT4[:, c, b, :, :] if tail else cT[:, c, b, 0:P]
                        ins = pe.matmul(ps[:, tail * P:(tail + 1) * P], lhs, cwv[:, c, :],
                                        start=(tail == 0 and c == 0), stop=(c == 1), skip_group_check=True)
                finish(1, "v", ins)

            def scores2(i, k):
                if not inside(i, k, 4, 4 * PAIRS):
                    return
                b, half = k // 2 % B, k % 2
                if half == 0:
                    gone(pe, 1, i, k // 2 - 2, "k")
                    gone(pe, 1, i, k // 2 - 2, "q")
                for j in range(2):
                    reach(pe, r["p"], i * 8 + 2 * k + j - 1)
                    o, t = bank[j][:, 0:2 * T], 2 * half + j
                    cols = slice(t * P, (t + 1) * P)
                    pe.matmul(o, q2H[:, b, cols], k2H[:, b, :, :], start=True, stop=False)
                    pe.matmul(o, q2H[:, b, cols], k2L[:, b, :, :], start=False, stop=False)
                    pe.matmul(o, q2L[:, b, cols], k2H[:, b, :, :], start=False, stop=True).then_inc(r["s"], 1)

            def turn2(i, k):
                if not inside(i, k, 4, 4 * PAIRS):
                    return
                reach(pe, r["p"], i * 8 + 2 * k + 2)
                reach(pe, r["pd"], i * 4 + k - 1)
                for h in range(2):
                    for j in range(2):
                        c = 2 * h + j
                        pe.transpose(bank[2 + k % 2][:, c * P:(c + 1) * P], P2[:, k % 2, 2 * j + h, 0:P],
                                     ident[:, :])

            def turn_tails2(i, k):
                if not inside(i, k, 4, 4 * PAIRS):
                    return
                reach(pe, r["pd"], i * 4 + k)
                reach(pe, r["pt"], i * 4 + k + 1)
                pe.transpose(bank[4][:, 0:P], P2t[:, k % 2, :, :], ident[:, :]).then_inc(r["t"], 1)

            def mix2(i, k):
                b, half = k // 2, k % 2
                if half == 0:
                    reach(pe, r["o"], i * B + b)
                    gone(pe, 1, i, b - 1, "v")
                reach(pe, r["pd"], i * 4 + k + 1)
                for h in range(2):
                    pe.matmul(bank[5][:, half * 256:half * 256 + 256], vZ2[:, b, h, :],
                              P2T[:, k % 2, 2 * h:2 * h + 2, :], start=(h == 0), stop=False, skip_group_check=True)
                for j in range(2):
                    o = half * 256 + j * P
                    ins = pe.matmul(bank[5][:, o:o + P], vZ2t[:, b, j, :], P2Tt[:, k % 2, :], start=False, stop=True,
                                    skip_group_check=True)
                ins.then_inc(r["pv"], 1)

            def cross_attention(i):
                for k in range(4):
                    v = k // 2
                    scores2(i, k + 2)
                    turn2(i, k + 1)
                    if k % 2 == 0:
                        values2(i, v)
                        turn_tails2(i, k + 1)
                        project(1, i, v, 0)
                        mix2(i, k)
                        project(1, i, v, 1)
                    else:
                        keys_queries2(i, v, "k")
                        turn_tails2(i, k + 1)
                        keys_queries2(i, v, "q")
                        mix2(i, k)
                        spread_sums(1, i, v)

            keys_queries2(0, -2, "k")
            keys_queries2(0, -2, "q")
            turn_norm(2, 1)
            values2(0, -1)
            scores2(0, 0)
            keys_queries2(0, -1, "k")
            turned(2, 1)
            keys_queries2(0, -1, "q")
            scores2(0, 1)
            turn2(0, 0)
            turn_tails2(0, 0)
            sweep(pe, PAIRS, cross_attention)
            project(1, PAIRS, 0, 0)
            project(1, PAIRS, 0, 1)
            for b in range(B):
                turn_norm(3, b)

            pe.wait_ge(ff_w, 4)

            def ff_in(c, s, made_sem, free):
                for h in range(B):
                    if c == 0 and s == 1:
                        turned(3, h)
                    reach(pe, free, (c - 1) * B + h + 1)
                    w_ = slice(s * FF + c * P, s * FF + (c + 1) * P)
                    by_weights(bank[2 * s + h], f1h[:, w_], f1l[:, w_], f13[:, w_], slice(h * S, (h + 1) * S))\
                        .then_inc(made_sem, 1)

            def ff_back(c):
                for t in range(NT):
                    if t % QT == 0:
                        reach(pe, ff_hid, c * B + t // QT + 1)
                    ins = pe.matmul(bank[4 + t // 3][:, t % 3 * C:(t % 3 + 1) * C], hid[:, c % 2, t * P:(t + 1) * P],
                                    f2w[:, c, :], start=(c == 0 and t % 3 == 0), stop=(c == FCH - 1),
                                    skip_group_check=True)
                    if t % QT == QT - 1:
                        ins.then_inc(ff_out, 1)

            ff_in(0, 1, ff_g, ff_gel)
            ff_in(0, 0, ff_a, ff_hid)
            for c in range(FCH):
                if c + 1 < FCH:
                    ff_in(c + 1, 1, ff_g, ff_gel)
                ff_back(c)
                if c + 1 < FCH:
                    ff_in(c + 1, 0, ff_a, ff_hid)


def kernel(**inputs):
    import numpy as _np
    import concourse.bacc as _bacc
    from concourse import mybir as _mybir
    from concourse.bass_utils import run_bass_kernel_spmd as _run

    nc = _bacc.Bacc("TRN2", target_bir_lowering=False, num_devices=1)
    arrays, aps = {}, {}
    for name in inputs:
        a = _np.ascontiguousarray(inputs[name])
        arrays[f"in_{name}"] = a
        aps[name] = nc.dram_tensor(f"in_{name}", a.shape, _mybir.dt.from_np(a.dtype), kind="ExternalInput").ap()
    result = nc.dram_tensor("result", (B, S, C), _mybir.dt.float32, kind="ExternalOutput").ap()
    cross_attention_block_kernel(nc, aps, result)
    r = _run(nc, [arrays], core_ids=[0])
    return r.results[0]["result"]
```
